# Optimizing a Trainium2 kernel written in Bass

```python
import numpy as np
import jax
import jax.numpy as jnp

def _softmax(x, axis=-1):
    return jax.nn.softmax(x, axis=axis)

def _gelu(x):
    return jax.nn.gelu(x, approximate=True)

def _silu(x):
    return jax.nn.silu(x)

def _sigmoid(x):
    return jax.nn.sigmoid(x)

def _layernorm(x, axis=-1, eps=1e-05):
    m = jnp.mean(x, axis=axis, keepdims=True)
    v = jnp.var(x, axis=axis, keepdims=True)
    return (x - m) / jnp.sqrt(v + eps)

def _scatter_add(tgt, idx, src, axis=0):
    return tgt.at[idx].add(src)

def _segment_sum(src, seg, n):
    return jax.ops.segment_sum(src, seg, n)
kernel_name = 'mk_adaln_attn_ffn_d1_seqx_r8_47701f'

def setup_inputs(seed: int=0):
    np.random.seed(seed)
    _w = jnp.asarray

    def _rec_inputs():
        import jax
        import jax.numpy as jnp
        _rk = jax.random.key(seed)
        x = -0.000125 + 0.9999 * jax.random.normal(jax.random.fold_in(_rk, 1), (8, 128, 512), jnp.float32)
        _lenS = 128 - jax.random.randint(jax.random.fold_in(_rk, 7), (8,), 0, max(1, 128 // 4) + 1, jnp.int32)
        _lenS2 = 128 - jax.random.randint(jax.random.fold_in(_rk, 8), (8,), 0, max(1, 128 // 4) + 1, jnp.int32)
        itok_B_3_7 = jax.random.randint(jax.random.fold_in(_rk, 11), (8,), 3, 8, jnp.int32)
        itok_Bx16_0_63 = jax.random.randint(jax.random.fold_in(_rk, 12), (8, 16), 0, 64, jnp.int32)
        itok_B_207_1644 = jax.random.randint(jax.random.fold_in(_rk, 13), (8,), 207, 1645, jnp.int32)
        return (x, itok_B_3_7, itok_Bx16_0_63, itok_B_207_1644)
    x, itok_B_3_7, itok_Bx16_0_63, itok_B_207_1644 = _rec_inputs()

    def _L0_cond_setup():
        import jax, jax.numpy as jnp
        import numpy as np
        MAX_LORAS, OUT, IN = (8, 512, 512)
        B, S = (4, 256)
        key = jax.random.key(seed)
        k1, k2, k3 = jax.random.split(key, 3)
        x = jax.random.normal(k1, (B, S, IN), dtype=jnp.float32)
        weight = jax.random.normal(k2, (MAX_LORAS, OUT, IN), dtype=jnp.float32) * 0.02
        adapter_ids = jax.random.randint(k3, (B,), 0, MAX_LORAS, dtype=jnp.int32)
        return {'x': x, 'weight': weight, 'adapter_ids': adapter_ids}
    _L0_cond_all = _L0_cond_setup()
    _L0_cond_in = {k: v for k, v in _L0_cond_all.items() if k in ('weight',)}
    del _L0_cond_all

    def _L0_attn_setup():
        import jax, jax.numpy as jnp
        import numpy as np
        B, S, D = (2, 256, 512)
        NH, NKV = (32, 8)
        HD = D // NH
        NREP = NH // NKV
        SCALE = HD ** (-0.5)
        key = jax.random.key(seed)
        kx, kq, kk, kv, ko = jax.random.split(key, 5)
        s = 0.02
        return {'x': jax.random.normal(kx, (B, S, D), dtype=jnp.float32), 'wq': jax.random.normal(kq, (D, NH * HD), dtype=jnp.float32) * s, 'wk': jax.random.normal(kk, (D, NKV * HD), dtype=jnp.float32) * s, 'wv': jax.random.normal(kv, (D, NKV * HD), dtype=jnp.float32) * s, 'wo': jax.random.normal(ko, (NH * HD, D), dtype=jnp.float32) * s}
    _L0_attn_all = _L0_attn_setup()
    _L0_attn_in = {k: v for k, v in _L0_attn_all.items() if k in ('wq', 'wk', 'wv', 'wo')}
    del _L0_attn_all

    def _L0_cond2_setup():
        import jax, jax.numpy as jnp
        import numpy as np
        B, S, HID = (4, 128, 512)
        D, HQ, HK = (128, 32, 8)
        PAGES, PSIZE, NPP = (64, 32, 16)
        THETA = 10000.0
        EPS = 1e-06
        SCALE = 1.0 / float(np.sqrt(D))

        def _rmsnorm(t, w):
            var = jnp.mean(t * t, axis=-1, keepdims=True)
            return t * jax.lax.rsqrt(var + EPS) * w

        def _rope(t, pos):
            inv_freq = 1.0 / THETA ** (jnp.arange(0, D, 2, dtype=jnp.float32) / D)
            freqs = pos[..., None].astype(jnp.float32) * inv_freq
            cos = jnp.cos(freqs)[:, :, None, :]
            sin = jnp.sin(freqs)[:, :, None, :]
            t1, t2 = (t[..., :D // 2], t[..., D // 2:])
            return jnp.concatenate([t1 * cos - t2 * sin, t2 * cos + t1 * sin], axis=-1)
        key = jax.random.key(seed)
        ks = jax.random.split(key, 10)
        x = jax.random.normal(ks[0], (B, S, HID), jnp.float32)
        Wq = jax.random.normal(ks[1], (HQ * D, HID), jnp.float32) * 0.02
        Wk = jax.random.normal(ks[2], (HK * D, HID), jnp.float32) * 0.02
        Wv = jax.random.normal(ks[3], (HK * D, HID), jnp.float32) * 0.02
        Wo = jax.random.normal(ks[4], (HID, HQ * D), jnp.float32) * 0.02
        q_norm_w = jax.random.uniform(ks[5], (D,), jnp.float32)
        k_norm_w = jax.random.uniform(ks[6], (D,), jnp.float32)
        k_cache = jax.random.normal(ks[7], (PAGES, PSIZE, HK, D), jnp.float32)
        v_cache = jax.random.normal(ks[8], (PAGES, PSIZE, HK, D), jnp.float32)
        block_table = jnp.arange(B * NPP, dtype=jnp.int32).reshape(B, NPP)
        cache_seqlens = jax.random.randint(ks[9], (B,), 0, 475).astype(jnp.int32)
        return dict(x=x, Wq=Wq, Wk=Wk, Wv=Wv, Wo=Wo, q_norm_w=q_norm_w, k_norm_w=k_norm_w, k_cache=k_cache, v_cache=v_cache, block_table=block_table, cache_seqlens=cache_seqlens)
    _L0_cond2_all = _L0_cond2_setup()
    _L0_cond2_in = {k: v for k, v in _L0_cond2_all.items() if k in ('Wq', 'Wk', 'Wv', 'Wo', 'q_norm_w', 'k_norm_w', 'k_cache', 'v_cache')}
    del _L0_cond2_all

    def _L0_ffn_setup():
        import jax, jax.numpy as jnp
        import numpy as np
        B, T, D_IN, D_OUT = (8, 256, 512, 512)
        N_LORAS, RANK = (16, 32)
        SCALING = 1.0
        key = jax.random.key(seed)
        ks = jax.random.split(key, 8)
        std = 1.0 / D_IN ** 0.5
        x = jax.random.normal(ks[0], (B, T, D_IN), dtype=jnp.float32)
        idx = jax.random.randint(ks[1], (B,), 0, N_LORAS)
        gate = jax.nn.one_hot(idx, N_LORAS, dtype=jnp.float32)
        kernel = jax.random.normal(ks[2], (D_IN, D_OUT), dtype=jnp.float32) * std
        bias = jnp.zeros((D_OUT,), dtype=jnp.float32)
        lora_A = jax.random.normal(ks[3], (N_LORAS, RANK, D_IN), dtype=jnp.float32) * std
        lora_B = jax.random.normal(ks[4], (N_LORAS, D_OUT, RANK), dtype=jnp.float32) * 0.01
        lora_A_shared = jax.random.normal(ks[5], (RANK, D_IN), dtype=jnp.float32) * std
        lora_B_shared = jax.random.normal(ks[6], (D_OUT, RANK), dtype=jnp.float32) * 0.01
        return {'x': x, 'gate': gate, 'kernel': kernel, 'bias': bias, 'lora_A': lora_A, 'lora_B': lora_B, 'lora_A_shared': lora_A_shared, 'lora_B_shared': lora_B_shared}
    _L0_ffn_all = _L0_ffn_setup()
    _L0_ffn_in = {k: v for k, v in _L0_ffn_all.items() if k in ('gate', 'kernel', 'bias', 'lora_A', 'lora_B', 'lora_A_shared', 'lora_B_shared')}
    del _L0_ffn_all
    return {'x': x, 'itok_B_3_7': itok_B_3_7, 'itok_Bx16_0_63': itok_Bx16_0_63, 'itok_B_207_1644': itok_B_207_1644, 'L0_cond_weight': _L0_cond_in['weight'], 'L0_attn_wq': _L0_attn_in['wq'], 'L0_attn_wk': _L0_attn_in['wk'], 'L0_attn_wv': _L0_attn_in['wv'], 'L0_attn_wo': _L0_attn_in['wo'], 'L0_cond2_Wq': _L0_cond2_in['Wq'], 'L0_cond2_Wk': _L0_cond2_in['Wk'], 'L0_cond2_Wv': _L0_cond2_in['Wv'], 'L0_cond2_Wo': _L0_cond2_in['Wo'], 'L0_cond2_q_norm_w': _L0_cond2_in['q_norm_w'], 'L0_cond2_k_norm_w': _L0_cond2_in['k_norm_w'], 'L0_cond2_k_cache': _L0_cond2_in['k_cache'], 'L0_cond2_v_cache': _L0_cond2_in['v_cache'], 'L0_ffn_gate': _L0_ffn_in['gate'], 'L0_ffn_kernel': _L0_ffn_in['kernel'], 'L0_ffn_bias': _L0_ffn_in['bias'], 'L0_ffn_lora_A': _L0_ffn_in['lora_A'], 'L0_ffn_lora_B': _L0_ffn_in['lora_B'], 'L0_ffn_lora_A_shared': _L0_ffn_in['lora_A_shared'], 'L0_ffn_lora_B_shared': _L0_ffn_in['lora_B_shared']}

def reference(x, itok_B_3_7, itok_Bx16_0_63, itok_B_207_1644, L0_cond_weight, L0_attn_wq, L0_attn_wk, L0_attn_wv, L0_attn_wo, L0_cond2_Wq, L0_cond2_Wk, L0_cond2_Wv, L0_cond2_Wo, L0_cond2_q_norm_w, L0_cond2_k_norm_w, L0_cond2_k_cache, L0_cond2_v_cache, L0_ffn_gate, L0_ffn_kernel, L0_ffn_bias, L0_ffn_lora_A, L0_ffn_lora_B, L0_ffn_lora_A_shared, L0_ffn_lora_B_shared):
    import jax
    import jax.numpy as jnp

    def _L0_cond_ref(x, weight, adapter_ids):
        import jax, jax.numpy as jnp
        import numpy as np
        MAX_LORAS, OUT, IN = (8, 512, 512)
        B, S = (4, 256)
        w = weight[adapter_ids]
        return jnp.einsum('bsi,boi->bso', x, w)

    def _L0_attn_ref(x, wq, wk, wv, wo):
        import jax, jax.numpy as jnp
        import numpy as np
        B, S, D = (2, 256, 512)
        NH, NKV = (32, 8)
        HD = D // NH
        NREP = NH // NKV
        SCALE = HD ** (-0.5)
        b, s, _ = x.shape
        q = (x @ wq).reshape(b, s, NH, HD)
        k = (x @ wk).reshape(b, s, NKV, HD)
        v = (x @ wv).reshape(b, s, NKV, HD)
        k = jnp.repeat(k, NREP, axis=2)
        v = jnp.repeat(v, NREP, axis=2)
        scores = jnp.einsum('bihd,bjhd->bhij', q, k) * SCALE
        causal = jnp.tril(jnp.ones((s, s), dtype=bool))
        scores = jnp.where(causal, scores, jnp.finfo(scores.dtype).min)
        attn = jax.nn.softmax(scores, axis=-1)
        out = jnp.einsum('bhij,bjhd->bihd', attn, v)
        out = out.reshape(b, s, NH * HD)
        return out @ wo

    def _L0_cond2_ref(x, Wq, Wk, Wv, Wo, q_norm_w, k_norm_w, k_cache, v_cache, block_table, cache_seqlens):
        import jax, jax.numpy as jnp
        import numpy as np
        B, S, HID = (4, 128, 512)
        D, HQ, HK = (128, 32, 8)
        PAGES, PSIZE, NPP = (64, 32, 16)
        THETA = 10000.0
        EPS = 1e-06
        SCALE = 1.0 / float(np.sqrt(D))

        def _rmsnorm(t, w):
            var = jnp.mean(t * t, axis=-1, keepdims=True)
            return t * jax.lax.rsqrt(var + EPS) * w

        def _rope(t, pos):
            inv_freq = 1.0 / THETA ** (jnp.arange(0, D, 2, dtype=jnp.float32) / D)
            freqs = pos[..., None].astype(jnp.float32) * inv_freq
            cos = jnp.cos(freqs)[:, :, None, :]
            sin = jnp.sin(freqs)[:, :, None, :]
            t1, t2 = (t[..., :D // 2], t[..., D // 2:])
            return jnp.concatenate([t1 * cos - t2 * sin, t2 * cos + t1 * sin], axis=-1)
        bsz, seqlen, _ = x.shape
        q = jnp.einsum('bsd,ed->bse', x, Wq).reshape(bsz, seqlen, HQ, D)
        k = jnp.einsum('bsd,ed->bse', x, Wk).reshape(bsz, seqlen, HK, D)
        v = jnp.einsum('bsd,ed->bse', x, Wv).reshape(bsz, seqlen, HK, D)
        q = _rmsnorm(q, q_norm_w)
        k = _rmsnorm(k, k_norm_w)
        pos = cache_seqlens[:, None] + jnp.arange(seqlen)[None, :]
        q = _rope(q, pos)
        k = _rope(k, pos)
        L = NPP * PSIZE
        kc = k_cache[block_table].reshape(bsz, L, HK, D)
        vc = v_cache[block_table].reshape(bsz, L, HK, D)
        k_all = jnp.concatenate([kc, k], axis=1)
        v_all = jnp.concatenate([vc, v], axis=1)
        valid_c = jnp.arange(L)[None, :] < cache_seqlens[:, None]
        valid = jnp.concatenate([valid_c, jnp.ones((bsz, seqlen), dtype=bool)], axis=1)
        rep = HQ // HK
        k_all = jnp.repeat(k_all, rep, axis=2)
        v_all = jnp.repeat(v_all, rep, axis=2)
        scores = jnp.einsum('bqhd,bkhd->bhqk', q, k_all) * SCALE
        scores = jnp.where(valid[:, None, None, :], scores, -1e+30)
        probs = jax.nn.softmax(scores, axis=-1)
        o = jnp.einsum('bhqk,bkhd->bqhd', probs, v_all)
        o = o.reshape(bsz, seqlen, HQ * D)
        return jnp.einsum('bse,de->bsd', o, Wo)

    def _L0_ffn_ref(x, gate, kernel, bias, lora_A, lora_B, lora_A_shared, lora_B_shared):
        import jax, jax.numpy as jnp
        import numpy as np
        B, T, D_IN, D_OUT = (8, 256, 512, 512)
        N_LORAS, RANK = (16, 32)
        SCALING = 1.0
        base_out = jnp.matmul(x, kernel) + bias
        b = gate.shape[0]
        x_flat = x.reshape(b, -1, x.shape[-1])
        A_eff = jnp.einsum('bn,nri->bri', gate, lora_A)
        B_eff = jnp.einsum('bn,nor->bor', gate, lora_B)
        Ax = jnp.einsum('bri,bti->btr', A_eff, x_flat)
        delta_flat = jnp.einsum('bor,btr->bto', B_eff, Ax)
        Ax_s = jnp.einsum('ri,bti->btr', lora_A_shared, x_flat)
        delta_flat = delta_flat + jnp.einsum('or,btr->bto', lora_B_shared, Ax_s)
        delta = delta_flat.reshape(x.shape[:-1] + (kernel.shape[-1],))
        return base_out + (SCALING * delta).astype(base_out.dtype)
    x = x + _L0_attn_ref(_L0_cond_ref(x, L0_cond_weight, itok_B_3_7), L0_attn_wq, L0_attn_wk, L0_attn_wv, L0_attn_wo)
    x = x + _L0_ffn_ref(_L0_cond2_ref(x, L0_cond2_Wq, L0_cond2_Wk, L0_cond2_Wv, L0_cond2_Wo, L0_cond2_q_norm_w, L0_cond2_k_norm_w, L0_cond2_k_cache, L0_cond2_v_cache, itok_Bx16_0_63, itok_B_207_1644), L0_ffn_gate, L0_ffn_kernel, L0_ffn_bias, L0_ffn_lora_A, L0_ffn_lora_B, L0_ffn_lora_A_shared, L0_ffn_lora_B_shared)
    return x

_drawn_inputs = setup_inputs


def setup_inputs(seed=0):
    import zlib

    import numpy as np

    out = dict(_drawn_inputs(seed))
    spreads = {'L0_ffn_bias': (0.0, 0.1)}
    factors = {}
    for name, (base, spread) in spreads.items():
        noise = np.random.default_rng([zlib.crc32(name.encode()), seed]).standard_normal(out[name].shape)
        drawn = base * np.exp(spread * noise) if base else spread * noise
        out[name] = jnp.asarray(drawn.astype(out[name].dtype))
    for name, factor in factors.items():
        out[name] = (out[name] * factor).astype(out[name].dtype)
    return out
```

```python
from contextlib import ExitStack

import numpy as np
import concourse.bass as bass
from concourse import mybir

F32 = mybir.dt.float32
R32 = mybir.dt.float32r
BF16 = mybir.dt.bfloat16
I32 = mybir.dt.int32
ALU = mybir.AluOpType
ACT = mybir.ActivationFunctionType
AX = mybir.AxisListType

P = 128
B = 8
D = 512
C = D // P
H1, KV1, HD1 = 32, 8, 16
R1 = H1 // KV1
QKV1 = (H1 + 2 * KV1) * HD1
SCALE1 = HD1 ** -0.5
STEPS = B * KV1
H2, KV2, HD2 = 32, 8, 128
R2 = H2 // KV2
PAGES, PAGE, PAGES_ROW = 64, 32, 16
CACHED = PAGE * PAGES_ROW
KEYS = CACHED + P
KC = KEYS // P
SCALE2 = 1.0 / float(np.sqrt(HD2))
EPS = 1e-6
QC = R2 * HD2
WC = QC + 2 * HD2
GROUPS = KV2 * B
HALF = HD2 // 2
N_LORA, RANK = 16, 32
GJ = 8
LFLAT = D * RANK // GJ
MASKED = -1e30
LOWEST = -3e38
MAGIC_ROUND = 12582912.0
TWO_PI_PARTS = (6.28125, 0.0019350051879882812, 3.019916050561733e-07)
PI_SAFE = 3.1415925
RSQRT_MAGIC = 0x5F3759DF


def build_program(nc, I, out):
    ctx = ExitStack()
    with ctx:
        def sb(name, shape, dt=F32, scope=ctx):
            return scope.enter_context(nc.sbuf_tensor(name, shape, dt))

        def sem(name):
            return ctx.enter_context(nc.semaphore(name))

        x1_dram = nc.dram_tensor("x1_dram", [B, P, D], F32, kind="Internal").ap()
        tabs_dram = nc.dram_tensor("tabs_dram", [B, P, 4 * HD2], F32, kind="Internal").ap()
        aeff_dram = nc.dram_tensor("aeff_dram", [GJ, B, LFLAT], F32, kind="Internal").ap()
        beff_dram = nc.dram_tensor("beff_dram", [GJ, B, LFLAT], F32, kind="Internal").ap()

        bank = [ctx.enter_context(nc.psum_tensor(f"bank{i}", [P, 512], F32)) for i in range(4, 8)]
        pair = [ctx.enter_context(nc.psum_tensor(f"pair{i}", [P, 2, 512], F32)) for i in range(2)]
        b0, b1, b2, b3 = (pair[0][:, 0, :], pair[0][:, 1, :], pair[1][:, 0, :], pair[1][:, 1, :])
        b4, b5, b6, b7 = (t[:, :] for t in bank)

        xT_h = sb("xT_h", [P, C, B * P], R32)
        xT_l = sb("xT_l", [P, C, B * P], R32)
        ident = sb("ident", [P, P])
        ident_r = sb("ident_r", [P, P], R32)
        lens = sb("lens", [P, B])
        page_ids = sb("page_ids", [1, B * PAGES_ROW], I32)
        key_mask = sb("key_mask", [P, B, KEYS], BF16)
        acc2 = sb("acc2", [P, B, D])

        ph1 = ExitStack()
        s1 = lambda name, shape, dt=F32: sb(name, shape, dt, ph1)
        lw_raw = s1("lw_raw", [P, C, D])
        lw_h, lw_l = s1("lw_h", [P, C, D], R32), s1("lw_l", [P, C, D], R32)
        wa_h, wa_l = s1("wa_h", [P, C, QKV1], R32), s1("wa_l", [P, C, QKV1], R32)
        wo_h, wo_l = s1("wo_h", [P, C, D], R32), s1("wo_l", [P, C, D], R32)
        xr = [s1(f"xr{k}", [P, C, P]) for k in range(2)]
        x_in = [s1(f"x_in{k}", [P, D]) for k in range(2)]
        h_sb = s1("h_sb", [P, D])
        hT_h, hT_l = s1("hT_h", [P, C, P], R32), s1("hT_l", [P, C, P], R32)
        qs = s1("qs", [P, H1, 4, HD1], R32)
        ks = s1("ks", [P, KV1, 4, HD1], R32)
        vs = [s1(f"vs{k}", [P, KV1, 2, HD1], R32) for k in range(2)]
        causal = s1("causal", [P, P])
        ids = s1("ids", [1, B], I32)
        setup = ExitStack()
        s0 = lambda name, shape, dt=F32: sb(name, shape, dt, setup)
        w_raw, wo_raw = s0("w_raw", [P, C, QKV1]), s0("wo_raw", [P, C, D])
        lens_i = s0("lens_i", [P, B], I32)
        pos = s0("pos", [P, B])
        key_no = s0("key_no", [P, CACHED])
        tok_no = s0("tok_no", [P, 1])
        inv_freq = s0("inv_freq", [P, HALF])
        qw, kw = s0("qw", [P, HD2]), s0("kw", [P, HD2])
        ang = s0("ang", [P, B, HALF])
        turns = s0("turns", [P, B, HALF])
        cos = s0("cos", [P, B, HALF])
        sin = s0("sin", [P, B, HALF])
        tab = s0("tab", [P, B, HD2])
        gate_bd = s0("gate_bd", [P, GJ * B])
        la = acc2[:, 0:B // 2, :].rearrange("p b d -> p (b d)")
        leff = acc2[0:GJ * B, B // 2:B, :].rearrange("p b d -> p (b d)")
        setup.close()
        qT = [s1(f"qT{k}", [P, H1 // 2, P], R32) for k in range(2)]
        kT = [s1(f"kT{k}", [P, KV1 // 2, P], R32) for k in range(2)]
        p1 = [s1(f"p1_{k}", [P, R1, P]) for k in range(2)]
        mx1 = [s1(f"mx1_{k}", [P, R1]) for k in range(2)]
        nm1 = [s1(f"nm1_{k}", [P, R1]) for k in range(2)]
        sum1 = [s1(f"sum1_{k}", [P, H1]) for k in range(2)]
        inv1 = s1("inv1", [P, H1])
        pt_h = [s1(f"pt_h{k}", [P, R1, P], R32) for k in range(2)]
        pt_l = [s1(f"pt_l{k}", [P, R1, P], R32) for k in range(2)]
        osum = s1("osum", [P, H1, HD1])
        o_sb = s1("o_sb", [P, D])
        oT_h, oT_l = s1("oT_h", [P, C, P], R32), s1("oT_l", [P, C, P], R32)
        x1 = [s1(f"x1_{k}", [P, D]) for k in range(2)]
        ph1.close()

        ph2 = ExitStack()
        s2 = lambda name, shape, dt=F32: sb(name, shape, dt, ph2)
        wg_h = [s2(f"wg_h{k}", [P, C, WC], R32) for k in range(2)]
        wg_l = [s2(f"wg_l{k}", [P, C, WC], R32) for k in range(2)]
        wog_h = [s2(f"wog_h{k}", [P, R2, D], R32) for k in range(2)]
        wog_l = [s2(f"wog_l{k}", [P, R2, D], R32) for k in range(2)]
        wst = s2("wst", [P, WC + D])
        tabs = [s2(f"tabs{k}", [P, 4, HD2]) for k in range(2)]
        kv = [s2(f"kv{k}", [P, CACHED // P, 2 * HD2]) for k in range(2)]
        KT_h, KT_l = s2("KT_h", [P, KEYS], R32), s2("KT_l", [P, KEYS], R32)
        V_h, V_l = s2("V_h", [P, KC, HD2], R32), s2("V_l", [P, KC, HD2], R32)
        QT_h, QT_l = s2("QT_h", [P, QC], R32), s2("QT_l", [P, QC], R32)
        q_cos, q_sin = s2("q_cos", [P, R2, 2, HALF]), s2("q_sin", [P, R2, 2, HALF])
        k_cos, k_sin = s2("k_cos", [P, 2, HALF]), s2("k_sin", [P, 2, HALF])
        sq_junk = s2("sq_junk", [P, HD2])
        ssq = s2("ssq", [P, R2 + 1])
        nr_x, nr_t = s2("nr_x", [P, R2 + 1]), s2("nr_t", [P, R2 + 1])
        nr_i = s2("nr_i", [P, R2 + 1], I32)
        rstd = s2("rstd", [P, R2 + 1])
        q_scale = [s2(f"q_scale{k}", [P, R2]) for k in range(2)]
        q_nscale = [s2(f"q_nscale{k}", [P, R2]) for k in range(2)]
        prob = s2("prob", [P, R2, KEYS])
        mx2, nm2 = s2("mx2", [P, R2]), s2("nm2", [P, R2])
        sum2, inv2 = s2("sum2", [P, R2]), s2("inv2", [P, R2])
        PT_h = [s2(f"PT_h{k}", [P, R2 * P], R32) for k in range(2)]
        PT_l = [s2(f"PT_l{k}", [P, R2 * P], R32) for k in range(2)]
        OT_h, OT_l = s2("OT_h", [P, R2 * P], R32), s2("OT_l", [P, R2 * P], R32)
        ph2.close()

        s3 = lambda name, shape, dt=F32: sb(name, shape, dt)
        kern_raw = s3("kern_raw", [P, C, D])
        kern_h, kern_l = s3("kern_h", [P, C, D], R32), s3("kern_l", [P, C, D], R32)
        a_sh = s3("a_sh", [P, C, RANK])
        a_eff = s3("a_eff", [P, B, C, 2 * RANK])
        a_h, a_l = s3("a_h", [P, B, C, 2 * RANK], R32), s3("a_l", [P, B, C, 2 * RANK], R32)
        b_eff = s3("b_eff", [2 * RANK + 1, B, D])
        x1_in = [s3(f"x1_in{k}", [P, D]) for k in range(2)]
        oT3_h = [s3(f"oT3_h{k}", [P, C, P], R32) for k in range(2)]
        oT3_l = [s3(f"oT3_l{k}", [P, C, P], R32) for k in range(2)]
        ax = s3("ax", [P, 2 * RANK])
        axT = [s3(f"axT{k}", [2 * RANK + 1, P]) for k in range(2)]
        y = [s3(f"y{k}", [P, D]) for k in range(2)]

        sems = {}

        def ev(name):
            if name not in sems:
                sems[name] = sem(name)
            return sems[name]

        counted = {}

        def after(eng, ins, name, n=1):
            counted[name] = counted.get(name, 0) + n
            ins.then_inc(ev(name), n)
            eng.wait_ge(ev(name), counted[name])

        def wait(eng, name, n):
            if n >= 1:
                eng.wait_ge(ev(name), n)

        def f32(ap):
            return ap.bitcast(F32)

        def split_mm(pe, o, pairs):
            for n, (ah, al, bh, bl) in enumerate(pairs):
                pe.matmul(o, ah, bh, start=(n == 0), stop=False)
                pe.matmul(o, ah, bl, start=False, stop=False)
                last = pe.matmul(o, al, bh, start=False, stop=(n == len(pairs) - 1))
            return last

        def st_constants(who, e):
            if who == "sp":
                e.dma_start(ids[:, :], I["lora_ids"]).then_inc(ev("ld_ids"), 16)
                e.dma_start(page_ids[:, :], I["page_ids"]).then_inc(ev("ld_pages"), 16)
                e.dma_start(lens_i[:, :], I["lens"].partition_broadcast(P)).then_inc(ev("ld_small"), 16)
                e.dma_start(inv_freq[:, :], I["inv_freq"].partition_broadcast(P)).then_inc(ev("ld_small"), 16)
                e.dma_start(qw[:, :], I["q_norm_w"].partition_broadcast(P)).then_inc(ev("ld_small"), 16)
                e.dma_start(kw[:, :], I["k_norm_w"].partition_broadcast(P)).then_inc(ev("ld_small"), 16)
            if who == "pool":
                after(e, e.memset(ident[:, :], 0.0), "po_setup")
                after(e, e.affine_select(out=ident[:, :], in_=ident[:, :], compare_op=ALU.not_equal,
                                         fill=1.0, base=0, pattern=[[-1, P]], channel_multiplier=1), "po_setup")
                e.tensor_copy(ident_r[:, :], ident[:, :]).then_inc(ev("po_ident"), 1)
                after(e, e.memset(causal[:, :], 0.0), "po_setup")
                e.affine_select(out=causal[:, :], in_=causal[:, :], compare_op=ALU.is_ge, fill=MASKED,
                                base=0, pattern=[[-1, P]], channel_multiplier=1).then_inc(ev("po_causal"), 1)
                e.iota(key_no[:, :], pattern=[[1, CACHED]], base=0, channel_multiplier=0,
                       allow_small_or_imprecise_dtypes=True).then_inc(ev("po_iota"), 1)
                e.iota(tok_no[:, :], pattern=[[0, 1]], base=0, channel_multiplier=1,
                       allow_small_or_imprecise_dtypes=True).then_inc(ev("po_iota"), 1)
                e.memset(gate_bd[:, :], 0.0).then_inc(ev("po_gate0"), 1)
                e.memset(key_mask[:, :, CACHED:], 0.0).then_inc(ev("po_mask0"), 1)

        def st_lora_eff(who, e, which):
            src, dst = ((I["lora_a"], aeff_dram), (I["lora_b"], beff_dram))[which]
            if who == "sp":
                if which == 0:
                    wait(e, "po_gate0", 1)
                    for j in range(GJ):
                        e.dma_start(gate_bd[N_LORA * j:N_LORA * (j + 1), B * j:B * (j + 1)],
                                    I["gate_t"]).then_inc(ev("ld_gate"), 16)
                else:
                    wait(e, "pe_leff", LFLAT // 512)
                e.dma_start(la, src).then_inc(ev("ld_la"), 16)
                wait(e, "dv_leff", (LFLAT // 512) * (which + 1))
                e.dma_start(dst.rearrange("j b n -> (j b) n"), leff).then_inc(ev("st_leff"), 16)
            if who == "pe":
                if which == 0:
                    wait(e, "ld_gate", 16 * GJ)
                wait(e, "ld_la", 16 * (which + 1))
                for k in range(LFLAT // 512):
                    n = which * (LFLAT // 512) + k
                    wait(e, "dv_leff", n - 1)
                    e.matmul((b4, b5)[n % 2][0:GJ * B, :], gate_bd[:, :], la[:, 512 * k:512 * (k + 1)],
                             start=True, stop=True).then_inc(ev("pe_leff"), 1)
            if who == "dve":
                if which == 1:
                    wait(e, "st_leff", 16)
                for k in range(LFLAT // 512):
                    n = which * (LFLAT // 512) + k
                    wait(e, "pe_leff", n + 1)
                    e.tensor_copy(leff[:, 512 * k:512 * (k + 1)], (b4, b5)[n % 2][0:GJ * B, :]).then_inc(ev("dv_leff"), 1)

        def st_tables(who, e):
            if who == "dve":
                link = lambda ins: after(e, ins, "dv_tab")
                wait(e, "ld_small", 64)
                wait(e, "po_iota", 2)
                link(e.tensor_copy(lens[:, :], lens_i[:, :]))
                link(e.tensor_scalar(out=pos[:, :], in0=lens[:, :], scalar1=tok_no[:, 0:1], scalar2=None, op0=ALU.add))
                wait(e, "po_mask0", 1)
                for b in range(B):
                    e.tensor_scalar(out=key_mask[:, b, 0:CACHED], in0=key_no[:, :], scalar1=lens[:, b:b + 1],
                                    scalar2=MASKED, op0=ALU.is_ge, op1=ALU.mult).then_inc(ev("dv_mask"), 1)
                link(e.tensor_tensor(ang[:, :, :], pos[:, :].unsqueeze(2).broadcast_to([P, B, HALF]),
                                     inv_freq[:, :].unsqueeze(1).broadcast_to([P, B, HALF]), ALU.mult))
                link(e.tensor_scalar(out=turns[:, :, :], in0=ang[:, :, :], scalar1=float(1 / (2 * np.pi)),
                                     scalar2=MAGIC_ROUND, op0=ALU.mult, op1=ALU.add))
                link(e.tensor_scalar(out=turns[:, :, :], in0=turns[:, :, :], scalar1=-MAGIC_ROUND, scalar2=None, op0=ALU.add))
                for part in TWO_PI_PARTS:
                    link(e.scalar_tensor_tensor(out=ang[:, :, :], in0=turns[:, :, :], scalar=-part,
                                                in1=ang[:, :, :], op0=ALU.mult, op1=ALU.add))
                e.tensor_scalar(out=ang[:, :, :], in0=ang[:, :, :], scalar1=PI_SAFE, scalar2=-PI_SAFE,
                                op0=ALU.min, op1=ALU.max).then_inc(ev("dv_ang"), 1)
                wait(e, "ac_sin", 2)
                link(e.tensor_tensor(cos[:, :, :], cos[:, :, :], cos[:, :, :], ALU.mult))
                link(e.tensor_scalar(out=cos[:, :, :], in0=cos[:, :, :], scalar1=-2.0, scalar2=1.0, op0=ALU.mult, op1=ALU.add))
                for n, (w, t) in enumerate(((qw, 0), (qw, 1), (kw, 0), (kw, 1))):
                    wait(e, "st_tab", 16 * n)
                    for half in range(2):
                        if t == 0:
                            f, ww = cos, w[:, HALF * half:HALF * (half + 1)]
                        else:
                            f, ww = sin, w[:, HALF * (1 - half):HALF * (2 - half)]
                        dst = tab[:, :, HALF * half:HALF * (half + 1)]
                        link(e.tensor_tensor(dst, f[:, :, :], ww.unsqueeze(1).broadcast_to([P, B, HALF]), ALU.mult))
                        if t == 1 and half == 0:
                            link(e.tensor_scalar(out=dst, in0=dst, scalar1=-1.0, scalar2=None, op0=ALU.mult))
                    e.engine_nop().then_inc(ev("dv_tabn"), 1)
            if who == "act":
                wait(e, "dv_ang", 1)
                e.activation(sin[:, :, :], ang[:, :, :], ACT.Sin).then_inc(ev("ac_sin"), 1)
                e.activation(cos[:, :, :], ang[:, :, :], ACT.Sin, scale=0.5).then_inc(ev("ac_sin"), 1)
            if who == "sp":
                for n in range(4):
                    wait(e, "dv_tabn", n + 1)
                    e.dma_start(tabs_dram[:, :, HD2 * n:HD2 * (n + 1)].rearrange("b p d -> p b d"),
                                tab[:, :, :]).then_inc(ev("st_tab"), 16)

        def st_weights1(who, e):
            if who == "sp":
                e.dma_start(w_raw[:, :, :], I["w_qkv1"]).then_inc(ev("ld_w1"), 16)
                e.dma_start(wo_raw[:, :, :], I["w_o1"]).then_inc(ev("ld_w1"), 16)
            if who == "dve":
                wait(e, "ld_w1", 32)
                after(e, e.tensor_copy(wa_h[:, :, :], w_raw[:, :, :]), "dv_w1h")
                e.tensor_tensor(wa_l[:, :, :], w_raw[:, :, :], f32(wa_h[:, :, :]), ALU.subtract).then_inc(ev("dv_w1"), 1)
                after(e, e.tensor_copy(wo_h[:, :, :], wo_raw[:, :, :]), "dv_w1h")
                e.tensor_tensor(wo_l[:, :, :], wo_raw[:, :, :], f32(wo_h[:, :, :]), ALU.subtract).then_inc(ev("dv_w1"), 1)

        turn_bank = (b6, b7)
        turn_no = {}

        def turn(key):
            return turn_no.setdefault(key, len(turn_no))

        def turn_claim(pe, key):
            n = turn(key)
            wait(pe, f"turn_free{n % 2}", n // 2)
            return turn_bank[n % 2]

        def filled(e, key):
            if key in turn_no:
                wait(e, f"turn_ready{turn_no[key] % 2}", turn_no[key] // 2 + 1)

        def emptied(e, key):
            if key in turn_no:
                wait(e, f"turn_free{turn_no[key] % 2}", turn_no[key] // 2 + 1)

        def turn_ready(ins, key):
            ins.then_inc(ev(f"turn_ready{turn(key) % 2}"), 1)

        def turn_read(e, key):
            n = turn(key)
            wait(e, f"turn_ready{n % 2}", n // 2 + 1)
            return turn_bank[n % 2]

        def turn_done(ins, key):
            ins.then_inc(ev(f"turn_free{turn(key) % 2}"), 1)

        def evac_split(who, e, key, dst_h, dst_l, name):
            if who == "act":
                t = turn_read(e, key)
                e.activation(dst_h, t, ACT.Copy).then_inc(ev(f"ac_{name}"), 1)
            if who == "dve":
                t = turn_read(e, key)
                counted[name] = counted.get(name, 0) + 1
                wait(e, f"ac_{name}", counted[name])
                ins = e.tensor_tensor(dst_l, t, f32(dst_h), ALU.subtract)
                turn_done(ins, key)

        def flat(ap):
            return ap.rearrange("p a b -> p (a b)")

        def st_load1(who, e, b):
            if who == "sp":
                if b == 0:
                    wait(e, "ld_ids", 16)
                    st_load1.regs = [e.alloc_register(f"lora_id{k}") for k in range(B)]
                    e.load(st_load1.regs, ids[0:1, :])
                wait(e, "po_lw", b)
                w = e.snap(st_load1.regs[b], min_val=0, max_val=7)
                e.dma_start(lw_raw[:, :, :], I["lora_w"][bass.ds(w, 1), :, :, :].rearrange("a p c n -> (a p) c n"))\
                    .then_inc(ev("ld_lw"), 16)
                wait(e, "po_x", b - 1)
                e.dma_start(xr[b % 2][:, :, :], I["x_t"][:, :, P * b:P * (b + 1)]).then_inc(ev(f"ld_xr{b % 2}"), 16)

        def st_loadx(who, e, b):
            if who == "sp":
                wait(e, "dv_x1", b - 1)
                e.dma_start(x_in[b % 2][:, :], I["x"][b, :, :]).then_inc(ev(f"ld_x{b % 2}"), 16)

        def st_split1(who, e, b):
            cols = slice(P * b, P * (b + 1))
            if who == "dve":
                wait(e, "ld_lw", 16 * (b + 1))
                wait(e, "pe_cond", b)
                e.tensor_copy(lw_h[:, :, :], lw_raw[:, :, :]).then_inc(ev("dv_lw"), 1)
                wait(e, f"ld_xr{b % 2}", 16 * (b // 2 + 1))
                e.tensor_copy(xT_h[:, :, cols], xr[b % 2][:, :, :]).then_inc(ev("dv_x"), 1)
            if who == "pool":
                wait(e, "dv_lw", b + 1)
                wait(e, "pe_cond", b)
                e.tensor_tensor(lw_l[:, :, :], lw_raw[:, :, :], f32(lw_h[:, :, :]), ALU.subtract).then_inc(ev("po_lw"), 1)
                wait(e, "dv_x", b + 1)
                e.tensor_tensor(xT_l[:, :, cols], xr[b % 2][:, :, :], f32(xT_h[:, :, cols]), ALU.subtract).then_inc(ev("po_x"), 1)

        def st_cond(who, e, b):
            cols = slice(P * b, P * (b + 1))
            if who == "pe":
                wait(e, "po_lw", b + 1)
                wait(e, "po_x", b + 1)
                wait(e, "dv_x1", b - 2)
                split_mm(e, b0, [(xT_h[:, c, cols], xT_l[:, c, cols], lw_h[:, c, :], lw_l[:, c, :])
                                 for c in range(C)]).then_inc(ev("pe_cond"), 1)
            if who == "act":
                wait(e, "pe_cond", b + 1)
                filled(e, ("h", b - 1))
                e.activation(h_sb[:, :], b0, ACT.Copy).then_inc(ev("ac_h"), 1)

        def st_hT(who, e, b):
            if who == "pe":
                wait(e, "ac_h", b + 1)
                t = turn_claim(e, ("h", b))
                for c in range(C):
                    last = e.transpose(t[:, P * c:P * (c + 1)], h_sb[:, P * c:P * (c + 1)], ident[:, :])
                turn_ready(last, ("h", b))
            else:
                if who in ("act", "dve"):
                    wait(e, "pe_qkv", 2 * b)
                evac_split(who, e, ("h", b), flat(hT_h[:, :, :]), flat(hT_l[:, :, :]), "hT")

        def st_qkv1(who, e, b):
            if who == "pe":
                emptied(e, ("h", b))
                if b == 0:
                    wait(e, "dv_w1", 2)
                wait(e, "dv_qs", b)
                split_mm(e, b1, [(hT_h[:, c, :], hT_l[:, c, :], wa_h[:, c, 0:H1 * HD1], wa_l[:, c, 0:H1 * HD1])
                                 for c in range(C)]).then_inc(ev("pe_qkv"), 1)
                wait(e, "dv_vs", b)
                split_mm(e, b2[:, 0:2 * KV1 * HD1],
                         [(hT_h[:, c, :], hT_l[:, c, :], wa_h[:, c, H1 * HD1:], wa_l[:, c, H1 * HD1:])
                          for c in range(C)]).then_inc(ev("pe_qkv"), 1)
            q = b1.rearrange("p (h o d) -> p h o d", h=H1, o=1)
            k = b2[:, 0:KV1 * HD1].rearrange("p (h o d) -> p h o d", h=KV1, o=1)
            v = b2[:, KV1 * HD1:2 * KV1 * HD1].rearrange("p (h d) -> p h d", h=KV1)
            if who == "act":
                wait(e, "pe_qkv", 2 * b + 1)
                filled(e, ("tq", b - 1, 4))
                e.activation(qs[:, :, 0:2, :], q.broadcast_to([P, H1, 2, HD1]), ACT.Copy).then_inc(ev("ac_qs"), 1)
                wait(e, "pe_qkv", 2 * b + 2)
                e.activation(ks[:, :, 0::2, :], k.broadcast_to([P, KV1, 2, HD1]), ACT.Copy).then_inc(ev("ac_ks"), 1)
                wait(e, "pe_pv1", 8 * (b - 1))
                e.activation(vs[b % 2][:, :, 0, :], v, ACT.Copy).then_inc(ev("ac_vs"), 1)
            if who == "dve":
                wait(e, "ac_qs", b + 1)
                e.tensor_tensor(qs[:, :, 2:4, :], q.broadcast_to([P, H1, 2, HD1]), f32(qs[:, :, 0:2, :]),
                                ALU.subtract).then_inc(ev("dv_qs"), 1)
                wait(e, "ac_vs", b + 1)
                wait(e, "ac_ks", b + 1)
                e.tensor_tensor(ks[:, :, 1::2, :], k.broadcast_to([P, KV1, 2, HD1]), f32(ks[:, :, 0::2, :]),
                                ALU.subtract).then_inc(ev("dv_ks"), 1)
                e.tensor_tensor(vs[b % 2][:, :, 1, :], v, f32(vs[b % 2][:, :, 0, :]), ALU.subtract).then_inc(ev("dv_vs"), 1)

        def st_tq(who, e, b, k):
            key = ("tq", b, k)
            src = flat(ks[:, :, :, :].rearrange("p h f d -> p h (f d)")) if k == 4 else \
                flat(qs[:, :, :, :].rearrange("p h f d -> p h (f d)"))[:, 512 * k:512 * (k + 1)]
            if who == "pe":
                if k == 0:
                    wait(e, "dv_qs", b + 1)
                if k == 4:
                    wait(e, "dv_ks", b + 1)
                t = turn_claim(e, key).bitcast(R32)
                for j in range(4):
                    last = e.transpose(t[:, P * j:P * (j + 1)], src[:, P * j:P * (j + 1)], ident_r[:, :])
                turn_ready(last, key)
            if who == ("act", "dve")[k % 2]:
                dst = kT[b % 2][:, :, :] if k == 4 else qT[b % 2][:, 4 * k:4 * (k + 1), :]
                t = turn_read(e, key)
                wait(e, "pe_s1", 8 * (b - 1))
                if b == 0:
                    wait(e, "dv_w1", 2)
                    wait(e, "st_tab", 64)
                    wait(e, "st_leff", 32)
                ins = e.activation(flat(dst), t, ACT.Copy) if who == "act" else e.tensor_copy(flat(dst), t)
                turn_done(ins, key)

        def st_scores1(who, e, b, s):
            n = 8 * b + s
            half, pr = s % 2, s // 2
            rows = slice(64 * half, 64 * (half + 1))
            sc = (b4, b5)[n % 2]
            if who == "pe":
                if s == 0:
                    for k in range(5):
                        emptied(e, ("tq", b, k))
                if n == 0:
                    wait(e, "dv_leff", 2 * LFLAT // 512)
                wait(e, "dv_s1", 4 * (n - 1))
                for r in range(R1):
                    last = e.matmul(sc[:, P * r:P * (r + 1)], qT[b % 2][rows, 4 * pr + r, :],
                                    kT[b % 2][rows, pr, :], start=True, stop=True)
                last.then_inc(ev("pe_s1"), 1)
            if who == "dve":
                wait(e, "pe_s1", n + 1)
                filled(e, ("pt", n - 2))
                if n == 0:
                    wait(e, "po_causal", 1)
                wait(e, "ac_exp1", 4 * (n - 1))
                for r in range(R1):
                    e.tensor_tensor_reduce(out=p1[n % 2][:, r, :], in0=sc[:, P * r:P * (r + 1)], in1=causal[:, :],
                                           scale=1.0, scalar=LOWEST, op0=ALU.add, op1=ALU.max,
                                           accum_out=mx1[n % 2][:, r:r + 1]).then_inc(ev("dv_s1"), 1)
                wait(e, "dv_s1", 4 * (n + 1))
                e.tensor_scalar(out=nm1[n % 2][:, :], in0=mx1[n % 2][:, :], scalar1=-SCALE1, scalar2=None,
                                op0=ALU.mult).then_inc(ev("dv_nm1"), 1)
            if who == "act":
                wait(e, "dv_nm1", n + 1)
                wait(e, "dv_inv1", b - 1)
                for r in range(R1):
                    e.activation(p1[n % 2][:, r, :], p1[n % 2][:, r, :], ACT.Exp, bias=nm1[n % 2][:, r:r + 1],
                                 scale=SCALE1, accum_out=sum1[b % 2][:, R1 * s + r:R1 * s + r + 1])\
                        .then_inc(ev("ac_exp1"), 1)

        def st_pt1(who, e, b, s):
            n = 8 * b + s
            key = ("pt", n)
            if who == "pe":
                wait(e, "ac_exp1", 4 * (n + 1))
                t = turn_claim(e, key)
                for r in range(R1):
                    last = e.transpose(t[:, P * r:P * (r + 1)], p1[n % 2][:, r, :], ident[:, :])
                turn_ready(last, key)
            else:
                if who in ("act", "dve"):
                    wait(e, "pe_pv1", n - 1)
                evac_split(who, e, key, flat(pt_h[n % 2][:, :, :]), flat(pt_l[n % 2][:, :, :]), "pt1")

        def st_pv1(who, e, b, s):
            n = 8 * b + s
            if who == "pe":
                emptied(e, ("pt", n))
                if s == 0:
                    wait(e, "dv_vs", b + 1)
                if s % 4 == 0:
                    wait(e, "dv_osum", 2 * b + s // 4)
                for r in range(R1):
                    o = b3[:, 2 * HD1 * (R1 * (s % 4) + r):][:, 0:2 * HD1]
                    v = vs[b % 2][:, s, :, :].rearrange("p a d -> p (a d)")
                    e.matmul(o, pt_h[n % 2][:, r, :], v, start=True, stop=False)
                    last = e.matmul(o, pt_l[n % 2][:, r, :], v, start=False, stop=True)
                last.then_inc(ev("pe_pv1"), 1)

        def st_osum(who, e, b, half):
            if who == "dve":
                wait(e, "pe_pv1", 8 * b + 4 * (half + 1))
                if half == 0:
                    wait(e, "dv_onorm", b)
                e.tensor_reduce(osum[:, 16 * half:16 * (half + 1), :],
                                b3.rearrange("p (h a d) -> p h d a", h=16, a=2), AX.X, ALU.add)\
                    .then_inc(ev("dv_osum"), 1)

        def st_onorm(who, e, b):
            if who == "dve":
                wait(e, "ac_exp1", 32 * (b + 1))
                e.reciprocal(inv1[:, :], sum1[b % 2][:, :]).then_inc(ev("dv_inv1"), 1)
                wait(e, "dv_inv1", b + 1)
                wait(e, "dv_osum", 2 * (b + 1))
                filled(e, ("o", b - 1))
                e.tensor_tensor(o_sb[:, :].rearrange("p (h d) -> p h d", h=H1), osum[:, :, :],
                                inv1[:, :].unsqueeze(2).broadcast_to([P, H1, HD1]), ALU.mult)\
                    .then_inc(ev("dv_onorm"), 1)

        def st_oT(who, e, b):
            key = ("o", b)
            if who == "pe":
                wait(e, "dv_onorm", b + 1)
                t = turn_claim(e, key)
                for c in range(C):
                    last = e.transpose(t[:, P * c:P * (c + 1)], o_sb[:, P * c:P * (c + 1)], ident[:, :])
                turn_ready(last, key)
            else:
                if who in ("act", "dve"):
                    wait(e, "pe_wo1", b)
                evac_split(who, e, key, flat(oT_h[:, :, :]), flat(oT_l[:, :, :]), "oT")

        def st_wo1(who, e, b):
            if who == "pe":
                emptied(e, ("o", b))
                wait(e, "ac_h", min(b + 3, B))
                split_mm(e, b0, [(oT_h[:, c, :], oT_l[:, c, :], wo_h[:, c, :], wo_l[:, c, :]) for c in range(C)])\
                    .then_inc(ev("pe_wo1"), 1)
            if who == "dve":
                wait(e, "pe_wo1", b + 1)
                wait(e, f"ld_x{b % 2}", 16 * (b // 2 + 1))
                filled(e, ("x1", b - 2))
                wait(e, f"st_x1_{b % 2}", 16 * (b // 2))
                e.tensor_tensor(x1[b % 2][:, :], b0, x_in[b % 2][:, :], ALU.add).then_inc(ev("dv_x1"), 1)
            if who == "sp":
                wait(e, "dv_x1", b + 1)
                e.dma_start(x1_dram[b, :, :], x1[b % 2][:, :]).then_inc(ev(f"st_x1_{b % 2}"), 16)

        def st_x1T(who, e, b):
            key = ("x1", b)
            cols = slice(P * b, P * (b + 1))
            if who == "pe":
                wait(e, "dv_x1", b + 1)
                t = turn_claim(e, key)
                for c in range(C):
                    last = e.transpose(t[:, P * c:P * (c + 1)], x1[b % 2][:, P * c:P * (c + 1)], ident[:, :])
                turn_ready(last, key)
            elif who in ("act", "dve"):
                t = turn_read(e, key).rearrange("p (c t) -> p c t", c=C)
                if who == "act":
                    wait(e, "pe_cond", b + 1)
                    e.activation(xT_h[:, :, cols], t, ACT.Copy).then_inc(ev("ac_x1T"), 1)
                else:
                    wait(e, "ac_x1T", b + 1)
                    turn_done(e.tensor_tensor(xT_l[:, :, cols], t, f32(xT_h[:, :, cols]), ALU.subtract), key)

        def phase1_over(e):
            for key, n in turn_no.items():
                if n >= len(turn_no) - 2:
                    emptied(e, key)
            wait(e, "st_x1_0", 16 * (B // 2))
            wait(e, "st_x1_1", 16 * (B // 2))

        def st_phase2(who, e):
            phase1_over(e)

        def st_load2(who, e, i):
            if who == "sp":
                g, b = divmod(i, B)
                if i == 0:
                    wait(e, "ld_pages", 16)
                    st_load2.regs = [e.alloc_register(f"page{k}") for k in range(PAGES_ROW)]
                wait(e, "dv_k_rope", i - 1)
                wait(e, "dv_q_rope", i - 1)
                e.dma_start(tabs[i % 2][:, :, :], tabs_dram[b, :, :].rearrange("p (t d) -> p t d", t=4))\
                    .then_inc(ev(f"ld_tabs{i % 2}"), 16)
                e.load(st_load2.regs, page_ids[0:1, PAGES_ROW * b:PAGES_ROW * (b + 1)])
                wait(e, "pe_tk", i - 1)
                wait(e, "po_vl", i - 1)
                for k in range(PAGES_ROW):
                    page = e.snap(st_load2.regs[k], min_val=0, max_val=PAGES - 1)
                    j, c = k % (P // PAGE), k // (P // PAGE)
                    e.dma_start(kv[i % 2][PAGE * j:PAGE * (j + 1), c, :],
                                I["kv_cache"][g, bass.ds(page, 1), :, :].rearrange("a p n -> (a p) n"))\
                        .then_inc(ev(f"ld_kv{i % 2}"), 16)

        def st_wload(who, e, g, c):
            n = C * g + c
            w = g % 2
            if who == "sp":
                wait(e, "po_w", 2 * n)
                e.dma_start(wst[:, 0:WC], I["w_qkv2"][g, :, c, :]).then_inc(ev("ld_w2"), 16)
                e.dma_start(wst[:, WC:], I["w_o2"][g, :, c, :]).then_inc(ev("ld_w2"), 16)
            if who == "dve":
                wait(e, "ld_w2", 32 * (n + 1))
                if c == 0:
                    wait(e, "pe_wo2", B * (g - 1))
                e.tensor_copy(wg_h[w][:, c, :], wst[:, 0:WC]).then_inc(ev("dv_wh"), 1)
                e.tensor_copy(wog_h[w][:, c, :], wst[:, WC:]).then_inc(ev("dv_wh"), 1)
            if who == "pool":
                wait(e, "dv_wh", 2 * (n + 1))
                wait(e, "pe_wo2", B * (g - 1))
                e.tensor_tensor(wg_l[w][:, c, :], wst[:, 0:WC], f32(wg_h[w][:, c, :]), ALU.subtract).then_inc(ev("po_w"), 1)
                e.tensor_tensor(wog_l[w][:, c, :], wst[:, WC:], f32(wog_h[w][:, c, :]), ALU.subtract)\
                    .then_inc(ev("po_w"), 1)

        def st_proj(who, e, i, part):
            g, b = divmod(i, B)
            w = g % 2
            cols = slice(P * b, P * (b + 1))
            if who == "pe":
                if b == 0:
                    wait(e, "po_w", 2 * C * (g + 1))
                if part == 0:
                    wait(e, "dv_q_rope", i)
                    wait(e, "ac_sq", 5 * i)
                    split_mm(e, b4, [(xT_h[:, c, cols], xT_l[:, c, cols], wg_h[w][:, c, 0:QC], wg_l[w][:, c, 0:QC])
                                     for c in range(C)]).then_inc(ev("pe_q"), 1)
                else:
                    wait(e, "dv_vnew", i)
                    split_mm(e, b5[:, 0:2 * HD2],
                             [(xT_h[:, c, cols], xT_l[:, c, cols], wg_h[w][:, c, QC:], wg_l[w][:, c, QC:])
                              for c in range(C)]).then_inc(ev("pe_kv"), 1)

        def st_rope(who, e, i):
            q = b4.rearrange("p (h a d) -> p h a d", h=R2, a=2)
            k = b5[:, 0:HD2].rearrange("p (a d) -> p a d", a=2)
            t = tabs[i % 2]

            def tq(n):
                return t[:, n, :].rearrange("p (o a d) -> p o a d", o=1, a=2).broadcast_to([P, R2, 2, HALF])

            def tk(n):
                return t[:, n, :].rearrange("p (a d) -> p a d", a=2)

            if who == "act":
                wait(e, "dv_k_read", i)
                for h in range(R2):
                    wait(e, "dv_q_rope", i + 1)
                    after(e, e.activation(sq_junk[:, :], b4[:, HD2 * h:HD2 * (h + 1)], ACT.Square,
                                          accum_out=ssq[:, h:h + 1]), "ac_sq")
                wait(e, "pe_kv", i + 1)
                after(e, e.activation(sq_junk[:, :], b5[:, 0:HD2], ACT.Square, accum_out=ssq[:, R2:R2 + 1]), "ac_sq")
            if who == "dve":
                wait(e, "pe_q", i + 1)
                wait(e, f"ld_tabs{i % 2}", 16 * (i // 2 + 1))
                wait(e, "pe_tq", i)
                e.tensor_tensor(q_cos[:, :, :, :], q, tq(0), ALU.mult).then_inc(ev("dv_q_cos"), 1)
                wait(e, "po_q_rope", i)
                e.tensor_tensor(q_sin[:, :, :, :], q[:, :, ::-1, :], tq(1), ALU.mult).then_inc(ev("dv_q_rope"), 1)
                link = lambda ins: after(e, ins, "dv_nr")
                wait(e, "ac_sq", 5 * (i + 1))
                wait(e, "ac_exp2", 4 * (i - 1))
                e.tensor_scalar(out=nr_x[:, :], in0=ssq[:, :], scalar1=1.0 / HD2, scalar2=EPS,
                                op0=ALU.mult, op1=ALU.add).then_inc(ev("dv_k_read"), 1)
                wait(e, "dv_k_read", i + 1)
                link(e.tensor_scalar(out=nr_i[:, :], in0=nr_x[:, :].bitcast(I32), scalar1=1, scalar2=None,
                                     op0=ALU.logical_shift_right))
                link(e.tensor_scalar(out=rstd[:, :].bitcast(I32), in0=nr_i[:, :], scalar1=-1.0, scalar2=float(RSQRT_MAGIC),
                                     op0=ALU.mult, op1=ALU.add))
                link(e.tensor_scalar(out=nr_x[:, :], in0=nr_x[:, :], scalar1=-0.5, scalar2=None, op0=ALU.mult))
                for _ in range(3):
                    link(e.tensor_tensor(nr_t[:, :], rstd[:, :], rstd[:, :], ALU.mult))
                    link(e.tensor_tensor(nr_t[:, :], nr_t[:, :], nr_x[:, :], ALU.mult))
                    link(e.scalar_tensor_tensor(out=rstd[:, :], in0=nr_t[:, :], scalar=1.5, in1=rstd[:, :],
                                                op0=ALU.add, op1=ALU.mult))
                e.tensor_scalar(out=q_scale[i % 2][:, :], in0=rstd[:, 0:R2], scalar1=SCALE2, scalar2=None,
                                op0=ALU.mult).then_inc(ev("dv_q_scale"), 1)
                e.tensor_scalar(out=q_nscale[i % 2][:, :], in0=rstd[:, 0:R2], scalar1=-SCALE2, scalar2=None,
                                op0=ALU.mult).then_inc(ev("dv_q_scale"), 1)
                wait(e, "pe_tkn", i)
                e.scalar_tensor_tensor(out=k_cos[:, :, :], in0=k, scalar=rstd[:, R2:R2 + 1], in1=tk(2),
                                       op0=ALU.mult, op1=ALU.mult).then_inc(ev("dv_k_part"), 1)
                e.scalar_tensor_tensor(out=k_sin[:, :, :], in0=k[:, ::-1, :], scalar=rstd[:, R2:R2 + 1], in1=tk(3),
                                       op0=ALU.mult, op1=ALU.mult).then_inc(ev("dv_k_part"), 1)
                wait(e, "dv_k_part", 2 * (i + 1))
                e.tensor_tensor(k_cos[:, :, :], k_cos[:, :, :], k_sin[:, :, :], ALU.add).then_inc(ev("dv_k_rope"), 1)
            if who == "pool":
                wait(e, "dv_q_cos", i + 1)
                wait(e, "dv_q_rope", i + 1)
                e.tensor_tensor(q_cos[:, :, :, :], q_cos[:, :, :, :], q_sin[:, :, :, :], ALU.add).then_inc(ev("po_q_rope"), 1)

        def st_tk(who, e, i):
            if who == "pe":
                wait(e, f"ld_kv{i % 2}", 16 * PAGES_ROW * (i // 2 + 1))
                wait(e, "dv_s2", 4 * i)
                for c in range(CACHED // P):
                    last = e.transpose(b0[:, P * c:P * (c + 1)], kv[i % 2][:, c, 0:HD2], ident[:, :])
                last.then_inc(ev("pe_tk"), 1)
            if who == "act":
                wait(e, "pe_tk", i + 1)
                wait(e, "pe_s2", 4 * i)
                e.activation(KT_h[:, 0:CACHED], b0, ACT.Copy).then_inc(ev("ac_kt"), 1)
            if who == "dve":
                wait(e, "ac_kt", i + 1)
                e.tensor_tensor(KT_l[:, 0:CACHED], b0, f32(KT_h[:, 0:CACHED]), ALU.subtract).then_inc(ev("dv_kt"), 1)

        def st_tq2(who, e, i):
            if who == "pe":
                wait(e, "dv_s2", 4 * i)
                wait(e, "po_q_rope", i + 1)
                qf = q_cos[:, :, :, :].rearrange("p h a d -> p (h a d)")
                for h in range(R2):
                    last = e.transpose(b1[:, P * h:P * (h + 1)], qf[:, P * h:P * (h + 1)], ident[:, :])
                last.then_inc(ev("pe_tq"), 1)
                wait(e, "dv_k_rope", i + 1)
                e.transpose(b5[:, 2 * HD2:3 * HD2], k_cos[:, :, :].rearrange("p a d -> p (a d)"), ident[:, :])\
                    .then_inc(ev("pe_tkn"), 1)
            if who == "act":
                wait(e, "pe_s2", 4 * i)
                wait(e, "pe_tq", i + 1)
                e.activation(QT_h[:, :], b1, ACT.Copy).then_inc(ev("ac_qt"), 1)
                wait(e, "pe_tkn", i + 1)
                e.activation(KT_h[:, CACHED:], b5[:, 2 * HD2:3 * HD2], ACT.Copy).then_inc(ev("ac_ktn"), 1)
            if who == "dve":
                wait(e, "ac_qt", i + 1)
                e.tensor_tensor(QT_l[:, :], b1, f32(QT_h[:, :]), ALU.subtract).then_inc(ev("dv_qt"), 1)
                wait(e, "ac_ktn", i + 1)
                e.tensor_tensor(KT_l[:, CACHED:], b5[:, 2 * HD2:3 * HD2], f32(KT_h[:, CACHED:]), ALU.subtract)\
                    .then_inc(ev("dv_ktn"), 1)

        def st_v(who, e, i):
            nc_ = CACHED // P
            if who == "dve":
                wait(e, f"ld_kv{i % 2}", 16 * PAGES_ROW * (i // 2 + 1))
                wait(e, "pe_pv", KC * i)
                e.tensor_copy(V_h[:, 0:nc_, :], kv[i % 2][:, :, HD2:]).then_inc(ev("dv_vh"), 1)
                wait(e, "ac_vnew", i + 1)
                e.tensor_tensor(V_l[:, nc_, :], b5[:, HD2:2 * HD2], f32(V_h[:, nc_, :]), ALU.subtract)\
                    .then_inc(ev("dv_vnew"), 1)
            if who == "act":
                wait(e, "dv_ktn", i + 1)
                wait(e, "pe_pv", KC * i)
                e.activation(V_h[:, nc_, :], b5[:, HD2:2 * HD2], ACT.Copy).then_inc(ev("ac_vnew"), 1)
            if who == "pool":
                wait(e, "dv_vh", i + 1)
                e.tensor_tensor(V_l[:, 0:nc_, :], kv[i % 2][:, :, HD2:], f32(V_h[:, 0:nc_, :]), ALU.subtract)\
                    .then_inc(ev("po_vl"), 1)

        def st_scores2(who, e, i, h):
            b = i % B
            n = 4 * i + h
            p2 = pair[h % 2][:, :, 0:KEYS // 2]
            if who == "pe":
                if h == 0:
                    wait(e, "dv_qt", i + 1)
                    wait(e, "dv_kt", i + 1)
                    wait(e, "dv_ktn", i + 1)
                    wait(e, "dv_kt", i + 1)
                if h == 1:
                    wait(e, "dv_o", i)
                    wait(e, "dv_acc", i - 1)
                if h >= 2:
                    wait(e, "dv_s2", n - 1)
                hc = slice(P * h, P * (h + 1))
                for m, (q, kt) in enumerate(((QT_h, KT_h), (QT_h, KT_l), (QT_l, KT_h))):
                    for s in range(2):
                        last = e.matmul(pair[h % 2][:, s, 0:KEYS // 2], q[:, hc],
                                        kt[:, KEYS // 2 * s:KEYS // 2 * (s + 1)], start=(m == 0), stop=(m == 2))
                last.then_inc(ev("pe_s2"), 1)
            if who == "dve":
                wait(e, "pe_s2", n + 1)
                wait(e, "pe_pt", KC * i)
                if h == 0:
                    wait(e, "ac_exp2", 4 * i)
                    wait(e, "dv_q_scale", 2 * (i + 1))
                e.tensor_tensor_reduce(out=prob[:, h, :].rearrange("p (a k) -> p a k", a=2), in0=p2,
                                       in1=key_mask[:, b, :].rearrange("p (a k) -> p a k", a=2),
                                       scale=1.0, scalar=LOWEST, op0=ALU.add, op1=ALU.max,
                                       accum_out=mx2[:, h:h + 1]).then_inc(ev("dv_s2"), 1)
                wait(e, "dv_s2", n + 1)
                e.tensor_scalar(out=nm2[:, h:h + 1], in0=mx2[:, h:h + 1], scalar1=q_nscale[i % 2][:, h:h + 1],
                                scalar2=None, op0=ALU.mult).then_inc(ev("dv_nm2"), 1)
            if who == "act":
                wait(e, "dv_nm2", n + 1)
                if h == 0:
                    wait(e, "dv_inv2", 4 * i)
                e.activation(prob[:, h, :], prob[:, h, :], ACT.Exp, bias=nm2[:, h:h + 1],
                             scale=q_scale[i % 2][:, h:h + 1], accum_out=sum2[:, h:h + 1]).then_inc(ev("ac_exp2"), 1)

        def st_norm2(who, e, i, h):
            n = 4 * i + h
            if who == "dve":
                wait(e, "ac_exp2", n + 1)
                wait(e, "po_norm", n - 3)
                e.reciprocal(inv2[:, h:h + 1], sum2[:, h:h + 1]).then_inc(ev("dv_inv2"), 1)
            if who == "pool":
                wait(e, "dv_inv2", n + 1)
                e.tensor_tensor(prob[:, h, :], prob[:, h, :], inv2[:, h:h + 1].broadcast_to([P, KEYS]), ALU.mult)\
                    .then_inc(ev("po_norm"), 1)

        def st_pt(who, e, i, c):
            n = KC * i + c
            t = (b6, b7)[n % 2]
            if who == "pe":
                wait(e, "po_norm", 4 * (i + 1))
                wait(e, "dv_pt", n - 1)
                for h in range(R2):
                    last = e.transpose(t[:, P * h:P * (h + 1)], prob[:, h, P * c:P * (c + 1)], ident[:, :])
                last.then_inc(ev("pe_pt"), 1)

        def st_pt_evac(who, e, i, c):
            n = KC * i + c
            t = (b6, b7)[n % 2]
            if who == "act":
                wait(e, "pe_pt", n + 1)
                wait(e, "pe_pv", n - 1)
                e.activation(PT_h[n % 2][:, :], t, ACT.Copy).then_inc(ev("ac_pt"), 1)
            if who == "dve":
                wait(e, "ac_pt", n + 1)
                e.tensor_tensor(PT_l[n % 2][:, :], t, f32(PT_h[n % 2][:, :]), ALU.subtract).then_inc(ev("dv_pt"), 1)

        def st_pv(who, e, i, c):
            n = KC * i + c
            if who == "pe":
                if c == 0:
                    wait(e, "dv_s2", 4 * (i + 1))
                    wait(e, "po_vl", i + 1)
                    wait(e, "dv_vnew", i + 1)
                wait(e, "dv_pt", n + 1)
                k = n % 2
                e.matmul(b2, V_h[:, c, :], PT_h[k][:, :], start=(c == 0), stop=False)
                e.matmul(b2, V_h[:, c, :], PT_l[k][:, :], start=False, stop=False)
                e.matmul(b2, V_l[:, c, :], PT_h[k][:, :], start=False, stop=(c == KC - 1)).then_inc(ev("pe_pv"), 1)

        def st_o(who, e, i):
            if who == "act":
                wait(e, "pe_pv", KC * (i + 1))
                wait(e, "pe_wo2", i)
                e.activation(OT_h[:, :], b2, ACT.Copy).then_inc(ev("ac_o"), 1)
            if who == "dve":
                wait(e, "ac_o", i + 1)
                e.tensor_tensor(OT_l[:, :], b2, f32(OT_h[:, :]), ALU.subtract).then_inc(ev("dv_o"), 1)

        def st_wo2(who, e, i):
            g, b = divmod(i, B)
            if who == "pe":
                wait(e, "dv_o", i + 1)
                wait(e, "dv_s2", min(4 * (i + 2), 4 * GROUPS))
                split_mm(e, b3, [(OT_h[:, P * h:P * (h + 1)], OT_l[:, P * h:P * (h + 1)],
                                  wog_h[g % 2][:, h, :], wog_l[g % 2][:, h, :]) for h in range(R2)])\
                    .then_inc(ev("pe_wo2"), 1)
            if who == "dve":
                wait(e, "pe_wo2", i + 1)
                if g == 0:
                    e.tensor_copy(acc2[:, b, :], b3).then_inc(ev("dv_acc"), 1)
                else:
                    wait(e, "dv_acc", i - B + 1)
                    e.tensor_tensor(acc2[:, b, :], b3, acc2[:, b, :], ALU.add).then_inc(ev("dv_acc"), 1)

        def st_ffn_load(who, e):
            if who == "sp":
                wait(e, "dv_acc", GROUPS)
                e.dma_start(kern_raw[:, :, :], I["ffn_kernel"]).then_inc(ev("ld_f"), 16)
                for s in range(2):
                    for c in range(C):
                        e.dma_start(a_eff[64 * s:64 * (s + 1), :, c, 0:RANK],
                                    aeff_dram[2 * c + s, :, :].rearrange("b (p r) -> p b r", r=RANK)).then_inc(ev("ld_f"), 16)
                e.dma_start(a_sh[:, :, :], I["a_shared"]).then_inc(ev("ld_f"), 16)
                for j in range(GJ):
                    rj = RANK // GJ
                    e.dma_start(b_eff[rj * j:rj * (j + 1), :, :],
                                beff_dram[j, :, :].rearrange("b (r o) -> r b o", o=D)).then_inc(ev("ld_b"), 16)
                for b in range(B):
                    e.dma_start(b_eff[RANK:2 * RANK, b, :], I["b_shared"]).then_inc(ev("ld_b"), 16)
                    e.dma_start(b_eff[2 * RANK:2 * RANK + 1, b, :], I["bias"]).then_inc(ev("ld_b"), 16)
            if who == "dve":
                wait(e, "ld_f", 16 * (2 + 2 * C))
                e.tensor_copy(kern_h[:, :, :], kern_raw[:, :, :]).then_inc(ev("dv_kern"), 1)
                e.tensor_copy(a_eff[:, :, :, RANK:], a_sh[:, :, :].unsqueeze(1).broadcast_to([P, B, C, RANK]))\
                    .then_inc(ev("dv_aeff"), 1)
                wait(e, "dv_kern", 1)
                e.tensor_tensor(kern_l[:, :, :], kern_raw[:, :, :], f32(kern_h[:, :, :]), ALU.subtract).then_inc(ev("dv_kern"), 1)
                wait(e, "dv_aeff", 1)
                e.tensor_copy(a_h[:, :, :, :], a_eff[:, :, :, :]).then_inc(ev("dv_aeff"), 1)
                wait(e, "dv_aeff", 2)
                e.tensor_tensor(a_l[:, :, :, :], a_eff[:, :, :, :], f32(a_h[:, :, :, :]), ALU.subtract).then_inc(ev("dv_aeff"), 1)
            if who == "pool":
                wait(e, "dv_acc", GROUPS)
                for k in range(2):
                    e.memset(axT[k][2 * RANK:2 * RANK + 1, :], 1.0).then_inc(ev("po_ones"), 1)

        def st_ffn_T(who, e, b):
            k = b % 2
            t = (b0, b1)[k]
            if who == "sp":
                wait(e, "dv_y", b - 1)
                e.dma_start(x1_in[k][:, :], x1_dram[b, :, :]).then_inc(ev(f"ld_x1_{k}"), 16)
            if who == "pe":
                if b == 0:
                    wait(e, "dv_acc", GROUPS)
                wait(e, "dv_fT", b - 1)
                for c in range(C):
                    last = e.transpose(t[:, P * c:P * (c + 1)], acc2[:, b, P * c:P * (c + 1)], ident[:, :])
                last.then_inc(ev("pe_fT"), 1)
            if who == "act":
                wait(e, "pe_fT", b + 1)
                wait(e, "pe_ff", b - 1)
                e.activation(flat(oT3_h[k][:, :, :]), t, ACT.Copy).then_inc(ev("ac_fT"), 1)
            if who == "dve":
                wait(e, "ac_fT", b + 1)
                e.tensor_tensor(flat(oT3_l[k][:, :, :]), t, f32(flat(oT3_h[k][:, :, :])), ALU.subtract).then_inc(ev("dv_fT"), 1)

        def st_ffn_mm(who, e, b):
            k = b % 2
            if who == "pe":
                if b == 0:
                    wait(e, "dv_kern", 2)
                    wait(e, "dv_aeff", 3)
                wait(e, "dv_fT", b + 1)
                wait(e, "ac_ax", b - 1)
                split_mm(e, (b4, b5)[k][:, 0:2 * RANK],
                         [(oT3_h[k][:, c, :], oT3_l[k][:, c, :], a_h[:, b, c, :], a_l[:, b, c, :]) for c in range(C)])\
                    .then_inc(ev("pe_ax"), 1)
                wait(e, "dv_y", b - 1)
                o = (b2, b3)[k]
                for c in range(C):
                    e.matmul(o, oT3_h[k][:, c, :], kern_h[:, c, :], start=(c == 0), stop=False)
                    e.matmul(o, oT3_h[k][:, c, :], kern_l[:, c, :], start=False, stop=False)
                    last = e.matmul(o, oT3_l[k][:, c, :], kern_h[:, c, :], start=False, stop=False)
                last.then_inc(ev("pe_ff"), 1)
            if who == "act":
                wait(e, "pe_ax", b + 1)
                wait(e, "pe_axT", b)
                e.activation(ax[:, :], (b4, b5)[k][:, 0:2 * RANK], ACT.Copy).then_inc(ev("ac_ax"), 1)

        def st_ffn_out(who, e, b):
            k = b % 2
            t = (b6, b7)[k][0:2 * RANK, 0:P]
            if who == "pe":
                wait(e, "ac_ax", b + 1)
                wait(e, "ac_axT", b - 1)
                e.transpose(t, ax[:, :], ident[:, :]).then_inc(ev("pe_axT"), 1)
                if b == 0:
                    wait(e, "ld_b", 16 * (GJ + 2 * B))
                    wait(e, "po_ones", 2)
                wait(e, "ac_axT", b + 1)
                e.matmul((b2, b3)[k], axT[k][:, :], b_eff[:, b, :], start=False, stop=True).then_inc(ev("pe_out"), 1)
            if who == "act":
                wait(e, "pe_axT", b + 1)
                wait(e, "pe_out", b - 1)
                e.activation(axT[k][0:2 * RANK, :], t, ACT.Copy).then_inc(ev("ac_axT"), 1)
            if who == "dve":
                wait(e, "pe_out", b + 1)
                wait(e, f"ld_x1_{k}", 16 * (b // 2 + 1))
                wait(e, f"st_y{k}", 16 * (b // 2))
                e.tensor_tensor(y[k][:, :], (b2, b3)[k], x1_in[k][:, :], ALU.add).then_inc(ev("dv_y"), 1)
            if who == "sp":
                wait(e, "dv_y", b + 1)
                e.dma_start(out[b, :, :], y[k][:, :]).then_inc(ev(f"st_y{k}"), 16)

        def st_end(who, e):
            if who == "sp":
                for k in range(2):
                    wait(e, f"st_y{k}", 16 * (B // 2))

        plan = []
        add = lambda f, *a: plan.append((f, a))

        add(st_constants)
        add(st_load1, 0)
        add(st_lora_eff, 0)
        add(st_lora_eff, 1)
        add(st_tables)
        add(st_weights1)
        add(st_split1, 0)
        add(st_cond, 0)
        add(st_load1, 1)
        add(st_hT, 0)
        add(st_qkv1, 0)
        add(st_split1, 1)
        for k in range(5):
            add(st_tq, 0, k)
        for b in range(B + 1):
            core, nxt, prev = b < B, b + 1 < B, b > 0
            if core:
                add(st_loadx, b)
            for s in range(8):
                if core:
                    add(st_scores1, b, s)
                if s == 0:
                    if prev:
                        add(st_pv1, b - 1, 6)
                        add(st_pt1, b - 1, 7)
                elif s == 1:
                    if prev:
                        add(st_pv1, b - 1, 7)
                        add(st_osum, b - 1, 1)
                        add(st_onorm, b - 1)
                    if core:
                        add(st_pt1, b, 0)
                elif core:
                    add(st_pv1, b, s - 2)
                    if s == 5:
                        add(st_osum, b, 0)
                    add(st_pt1, b, s - 1)
                if s == 1 and nxt:
                    add(st_cond, b + 1)
                if s == 2:
                    if nxt:
                        add(st_hT, b + 1)
                    if prev:
                        add(st_oT, b - 1)
                if s == 3 and prev:
                    add(st_wo1, b - 1)
                if s == 4:
                    if prev:
                        add(st_x1T, b - 1)
                    if b + 2 < B:
                        add(st_load1, b + 2)
                if s == 5 and nxt:
                    add(st_qkv1, b + 1)
                if s == 6 and nxt:
                    for k in range(3):
                        add(st_tq, b + 1, k)
                if s == 7:
                    if nxt:
                        for k in range(3, 5):
                            add(st_tq, b + 1, k)
                    if b + 2 < B:
                        add(st_split1, b + 2)

        add(st_phase2)
        for c in range(C):
            add(st_wload, 0, c)
        add(st_load2, 0)
        add(st_load2, 1)
        add(st_proj, 0, 0)
        add(st_proj, 0, 1)
        add(st_rope, 0)
        add(st_tk, 0)
        add(st_tq2, 0)
        for i in range(GROUPS):
            g, b = divmod(i, B)
            nxt, prev = i + 1 < GROUPS, i > 0
            if prev:
                add(st_o, i - 1)
            add(st_v, i)
            for h in range(R2):
                add(st_scores2, i, h)
                if h >= 1:
                    add(st_norm2, i, h - 1)
            add(st_norm2, i, R2 - 1)
            if nxt:
                add(st_proj, i + 1, 0)
                add(st_proj, i + 1, 1)
            add(st_pt, i, 0)
            add(st_pt, i, 1)
            if nxt:
                add(st_tk, i + 1)
                add(st_rope, i + 1)
            if prev:
                add(st_wo2, i - 1)
            add(st_pt_evac, i, 0)
            add(st_pt_evac, i, 1)
            add(st_pv, i, 0)
            add(st_pt, i, 2)
            add(st_pt_evac, i, 2)
            add(st_pv, i, 1)
            add(st_pt, i, 3)
            add(st_pt_evac, i, 3)
            if i + 2 < GROUPS:
                add(st_load2, i + 2)
            if g + 1 < KV2 and 1 <= b <= C:
                add(st_wload, g + 1, b - 1)
            add(st_pv, i, 2)
            add(st_pt, i, 4)
            add(st_pt_evac, i, 4)
            if nxt:
                add(st_tq2, i + 1)
            add(st_pv, i, 3)
            add(st_pv, i, 4)
        add(st_o, GROUPS - 1)
        add(st_wo2, GROUPS - 1)

        add(st_ffn_load)
        add(st_ffn_T, 0)
        for b in range(B):
            add(st_ffn_mm, b)
            if b + 1 < B:
                add(st_ffn_T, b + 1)
            add(st_ffn_out, b)
        add(st_end)

        for f, a in plan:
            if f is st_hT:
                turn(("h", a[0]))
            elif f is st_tq:
                turn(("tq",) + a)
            elif f is st_pt1:
                turn(("pt", 8 * a[0] + a[1]))
            elif f is st_oT:
                turn(("o", a[0]))
            elif f is st_x1T:
                turn(("x1", a[0]))

        def run(who, e):
            for f, a in plan:
                f(who, e, *a)

        block = ctx.enter_context(nc.Block())

        @block.sync
        def _(e):
            run("sp", e)

        @block.gpsimd
        def _(e):
            run("pool", e)

        @block.vector
        def _(e):
            run("dve", e)

        @block.scalar
        def _(e):
            run("act", e)

        @block.tensor
        def _(e):
            run("pe", e)


def kernel(**inputs):
    import numpy as np
    import concourse.bacc as bacc
    from concourse import mybir
    from concourse.bass_utils import run_bass_kernel_spmd

    a = {k: np.asarray(v) for k, v in inputs.items()}
    con = np.ascontiguousarray

    def chunks(w):
        return con(w.reshape(-1, P, w.shape[-1]).transpose(1, 0, 2))

    wq1 = a["L0_attn_wq"].reshape(D, KV1 // 2, 2, R1, HD1).transpose(0, 1, 3, 2, 4).reshape(D, H1 * HD1)
    w_q = a["L0_cond2_Wq"].reshape(KV2, QC, D)
    w_k = a["L0_cond2_Wk"].reshape(KV2, HD2, D)
    w_v = a["L0_cond2_Wv"].reshape(KV2, HD2, D)
    w_qkv2 = np.concatenate([w_q, w_k, w_v], axis=1)
    w_qkv2 = w_qkv2.transpose(0, 2, 1).reshape(KV2, C, P, WC).transpose(0, 2, 1, 3)
    w_o2 = a["L0_cond2_Wo"].reshape(D, KV2, R2, HD2).transpose(1, 3, 2, 0)
    kv_cache = np.concatenate([a["L0_cond2_k_cache"], a["L0_cond2_v_cache"]], axis=-1)
    arrays = {
        "x": a["x"],
        "x_t": chunks(a["x"].reshape(B * P, D).T),
        "lora_ids": a["itok_B_3_7"].reshape(1, B),
        "page_ids": a["itok_Bx16_0_63"].reshape(1, B * PAGES_ROW),
        "lens": a["itok_B_207_1644"].reshape(B),
        "lora_w": a["L0_cond_weight"].transpose(0, 2, 1).reshape(8, C, P, D).transpose(0, 2, 1, 3),
        "w_qkv1": chunks(np.concatenate([wq1, a["L0_attn_wk"], a["L0_attn_wv"]], axis=1)),
        "w_o1": chunks(a["L0_attn_wo"]),
        "w_qkv2": w_qkv2,
        "w_o2": w_o2,
        "q_norm_w": a["L0_cond2_q_norm_w"],
        "k_norm_w": a["L0_cond2_k_norm_w"],
        "kv_cache": kv_cache.transpose(2, 0, 1, 3),
        "gate_t": a["L0_ffn_gate"].T,
        "lora_a": a["L0_ffn_lora_A"].transpose(0, 2, 1).reshape(N_LORA, GJ, LFLAT).transpose(1, 0, 2).reshape(P, LFLAT),
        "lora_b": a["L0_ffn_lora_B"].transpose(0, 2, 1).reshape(N_LORA, GJ, LFLAT).transpose(1, 0, 2).reshape(P, LFLAT),
        "a_shared": chunks(a["L0_ffn_lora_A_shared"].T),
        "b_shared": a["L0_ffn_lora_B_shared"].T,
        "bias": a["L0_ffn_bias"].reshape(1, D),
        "ffn_kernel": chunks(a["L0_ffn_kernel"]),
        "inv_freq": (np.float32(1.0) / np.power(np.float32(10000.0), np.arange(0, HD2, 2, dtype=np.float32) / np.float32(HD2))),
    }
    arrays = {k: con(v) for k, v in arrays.items()}
    nc = bacc.Bacc("TRN2", target_bir_lowering=False, num_devices=1)
    I = {k: nc.dram_tensor(f"in_{k}", v.shape, mybir.dt.from_np(v.dtype), kind="ExternalInput").ap()
         for k, v in arrays.items()}
    out = nc.dram_tensor("out_y", (B, P, D), mybir.dt.float32, kind="ExternalOutput").ap()
    build_program(nc, I, out)
    r = run_bass_kernel_spmd(nc, [{f"in_{k}": v for k, v in arrays.items()}], core_ids=[0])
    return r.results[0]["out_y"]
```

```python
from contextlib import ExitStack

import numpy as np
import concourse.bass as bass
from concourse import mybir

F32 = mybir.dt.float32
R32 = mybir.dt.float32r
BF16 = mybir.dt.bfloat16
I32 = mybir.dt.int32
ALU = mybir.AluOpType
ACT = mybir.ActivationFunctionType
AX = mybir.AxisListType

P = 128
B = 8
D = 512
C = D // P
H1, KV1, HD1 = 32, 8, 16
R1 = H1 // KV1
QKV1 = (H1 + 2 * KV1) * HD1
SCALE1 = HD1 ** -0.5
STEPS = B * KV1
H2, KV2, HD2 = 32, 8, 128
R2 = H2 // KV2
PAGES, PAGE, PAGES_ROW = 64, 32, 16
CACHED = PAGE * PAGES_ROW
KEYS = CACHED + P
KC = KEYS // P
SCALE2 = 1.0 / float(np.sqrt(HD2))
EPS = 1e-6
QC = R2 * HD2
WC = QC + 2 * HD2
GROUPS = KV2 * B
HALF = HD2 // 2
N_LORA, RANK = 16, 32
GJ = 8
LFLAT = D * RANK // GJ
MASKED = -1e30
LOWEST = -3e38
MAGIC_ROUND = 12582912.0
TWO_PI_PARTS = (6.28125, 0.0019350051879882812, 3.019916050561733e-07)
PI_SAFE = 3.1415925
RSQRT_MAGIC = 0x5F3759DF


def build_program(nc, I, out):
    ctx = ExitStack()
    with ctx:
        def sb(name, shape, dt=F32, scope=ctx):
            return scope.enter_context(nc.sbuf_tensor(name, shape, dt))

        def sem(name):
            return ctx.enter_context(nc.semaphore(name))

        x1_dram = nc.dram_tensor("x1_dram", [B, P, D], F32, kind="Internal").ap()
        tabs_dram = nc.dram_tensor("tabs_dram", [B, P, 4 * HD2], F32, kind="Internal").ap()
        aeff_dram = nc.dram_tensor("aeff_dram", [GJ, B, LFLAT], F32, kind="Internal").ap()
        beff_dram = nc.dram_tensor("beff_dram", [GJ, B, LFLAT], F32, kind="Internal").ap()

        bank = [ctx.enter_context(nc.psum_tensor(f"bank{i}", [P, 512], F32)) for i in range(4, 8)]
        pair = [ctx.enter_context(nc.psum_tensor(f"pair{i}", [P, 2, 512], F32)) for i in range(2)]
        b0, b1, b2, b3 = (pair[0][:, 0, :], pair[0][:, 1, :], pair[1][:, 0, :], pair[1][:, 1, :])
        b4, b5, b6, b7 = (t[:, :] for t in bank)

        xT_h = sb("xT_h", [P, C, B * P], R32)
        xT_l = sb("xT_l", [P, C, B * P], R32)
        ident = sb("ident", [P, P])
        ident_r = sb("ident_r", [P, P], R32)
        lens = sb("lens", [P, B])
        page_ids = sb("page_ids", [1, B * PAGES_ROW], I32)
        key_mask = sb("key_mask", [P, B, KEYS], BF16)
        acc2 = sb("acc2", [P, B, D])

        ph1 = ExitStack()
        s1 = lambda name, shape, dt=F32: sb(name, shape, dt, ph1)
        lw_raw = s1("lw_raw", [P, C, D])
        lw_h, lw_l = s1("lw_h", [P, C, D], R32), s1("lw_l", [P, C, D], R32)
        wa_h, wa_l = s1("wa_h", [P, C, QKV1], R32), s1("wa_l", [P, C, QKV1], R32)
        wo_h, wo_l = s1("wo_h", [P, C, D], R32), s1("wo_l", [P, C, D], R32)
        xr = [s1(f"xr{k}", [P, C, P]) for k in range(2)]
        x_in = [s1(f"x_in{k}", [P, D]) for k in range(2)]
        h_sb = s1("h_sb", [P, D])
        hT_h, hT_l = s1("hT_h", [P, C, P], R32), s1("hT_l", [P, C, P], R32)
        qs = s1("qs", [P, H1, 4, HD1], R32)
        ks = s1("ks", [P, KV1, 4, HD1], R32)
        vs = [s1(f"vs{k}", [P, KV1, 2, HD1], R32) for k in range(2)]
        causal = s1("causal", [P, P])
        ids = s1("ids", [1, B], I32)
        setup = ExitStack()
        s0 = lambda name, shape, dt=F32: sb(name, shape, dt, setup)
        w_raw, wo_raw = s0("w_raw", [P, C, QKV1]), s0("wo_raw", [P, C, D])
        lens_i = s0("lens_i", [P, B], I32)
        pos = s0("pos", [P, B])
        key_no = s0("key_no", [P, CACHED])
        tok_no = s0("tok_no", [P, 1])
        inv_freq = s0("inv_freq", [P, HALF])
        qw, kw = s0("qw", [P, HD2]), s0("kw", [P, HD2])
        ang = s0("ang", [P, B, HALF])
        turns = s0("turns", [P, B, HALF])
        cos = s0("cos", [P, B, HALF])
        sin = s0("sin", [P, B, HALF])
        tab = s0("tab", [P, B, HD2])
        gate_bd = s0("gate_bd", [P, GJ * B])
        la = acc2[:, 0:B // 2, :].rearrange("p b d -> p (b d)")
        leff = acc2[0:GJ * B, B // 2:B, :].rearrange("p b d -> p (b d)")
        setup.close()
        qT = [s1(f"qT{k}", [P, H1 // 2, P], R32) for k in range(2)]
        kT = [s1(f"kT{k}", [P, KV1 // 2, P], R32) for k in range(2)]
        p1 = [s1(f"p1_{k}", [P, R1, P]) for k in range(2)]
        nm1 = [s1(f"nm1_{k}", [P, R1]) for k in range(2)]
        sum1 = [s1(f"sum1_{k}", [P, H1]) for k in range(2)]
        inv1 = s1("inv1", [P, H1])
        pt_h = [s1(f"pt_h{k}", [P, R1, P], R32) for k in range(2)]
        pt_l = [s1(f"pt_l{k}", [P, R1, P], R32) for k in range(2)]
        osum = s1("osum", [P, H1, HD1])
        o_sb = s1("o_sb", [P, D])
        oT_h, oT_l = s1("oT_h", [P, C, P], R32), s1("oT_l", [P, C, P], R32)
        x1 = [s1(f"x1_{k}", [P, D]) for k in range(2)]
        ph1.close()

        ph2 = ExitStack()
        s2 = lambda name, shape, dt=F32: sb(name, shape, dt, ph2)
        wg_h = [s2(f"wg_h{k}", [P, C, WC], R32) for k in range(2)]
        wg_l = [s2(f"wg_l{k}", [P, C, WC], R32) for k in range(2)]
        wog_h = [s2(f"wog_h{k}", [P, R2, D], R32) for k in range(2)]
        wog_l = [s2(f"wog_l{k}", [P, R2, D], R32) for k in range(2)]
        wst = s2("wst", [P, WC])
        wost = s2("wost", [P, D])
        tabs = [s2(f"tabs{k}", [P, 4, HD2]) for k in range(2)]
        kv = [s2(f"kv{k}", [P, CACHED // P, 2 * HD2]) for k in range(2)]
        KT_h, KT_l = s2("KT_h", [P, KEYS], R32), s2("KT_l", [P, KEYS], R32)
        V_h, V_l = s2("V_h", [P, KC - 1, HD2], R32), s2("V_l", [P, KC - 1, HD2], R32)
        VN_h = [s2(f"VN_h{k}", [P, HD2], R32) for k in range(2)]
        VN_l = [s2(f"VN_l{k}", [P, HD2], R32) for k in range(2)]
        QT_h, QT_l = s2("QT_h", [P, QC], R32), s2("QT_l", [P, QC], R32)
        qk = s2("qk", [P, R2 + 1, 2, HALF])
        qk_sin = s2("qk_sin", [P, R2 + 1, 2, HALF])
        sq_junk = s2("sq_junk", [P, R2 + 1, HD2])
        ssq = s2("ssq", [P, R2 + 1])
        nr_x, nr_t = s2("nr_x", [P, R2 + 1]), s2("nr_t", [P, R2 + 1])
        nr_i = s2("nr_i", [P, R2 + 1], I32)
        rstd = s2("rstd", [P, R2 + 1])
        q_nscale = [s2(f"q_nscale{k}", [P, R2]) for k in range(2)]
        prob = s2("prob", [P, R2, KEYS])
        nm2 = s2("nm2", [P, R2])
        sum2, inv2 = s2("sum2", [P, R2]), s2("inv2", [P, R2])
        PT_h = [s2(f"PT_h{k}", [P, R2 * P], R32) for k in range(2)]
        PT_l = [s2(f"PT_l{k}", [P, R2 * P], R32) for k in range(2)]
        OT_h, OT_l = s2("OT_h", [P, R2 * P], R32), s2("OT_l", [P, R2 * P], R32)
        ph2.close()

        s3 = lambda name, shape, dt=F32: sb(name, shape, dt)
        kern_raw = s3("kern_raw", [P, C, D])
        kern_h, kern_l = s3("kern_h", [P, C, D], R32), s3("kern_l", [P, C, D], R32)
        a_sh = s3("a_sh", [P, C, RANK])
        a_eff = s3("a_eff", [P, B, C, 2 * RANK])
        a_h, a_l = s3("a_h", [P, B, C, 2 * RANK], R32), s3("a_l", [P, B, C, 2 * RANK], R32)
        b_eff = s3("b_eff", [2 * RANK + 1, B, D])
        x1_in = [s3(f"x1_in{k}", [P, D]) for k in range(2)]
        oT3_h = [s3(f"oT3_h{k}", [P, C, P], R32) for k in range(2)]
        oT3_l = [s3(f"oT3_l{k}", [P, C, P], R32) for k in range(2)]
        ax = s3("ax", [P, 2 * RANK])
        axT = [s3(f"axT{k}", [2 * RANK + 1, P]) for k in range(2)]
        y = [s3(f"y{k}", [P, D]) for k in range(2)]

        sems = {}

        def ev(name):
            if name not in sems:
                sems[name] = sem(name)
            return sems[name]

        counted = {}

        def after(eng, ins, name, n=1):
            counted[name] = counted.get(name, 0) + n
            ins.then_inc(ev(name), n)
            eng.wait_ge(ev(name), counted[name])

        def wait(eng, name, n):
            if n >= 1:
                eng.wait_ge(ev(name), n)

        def f32(ap):
            return ap.bitcast(F32)

        def split_mm(pe, o, pairs):
            for n, (ah, al, bh, bl) in enumerate(pairs):
                pe.matmul(o, ah, bh, start=(n == 0), stop=False)
                pe.matmul(o, ah, bl, start=False, stop=False)
                last = pe.matmul(o, al, bh, start=False, stop=(n == len(pairs) - 1))
            return last

        def st_constants(who, e):
            if who == "sp":
                e.dma_start(ids[:, :], I["lora_ids"]).then_inc(ev("ld_ids"), 16)
                e.dma_start(page_ids[:, :], I["page_ids"]).then_inc(ev("ld_pages"), 16)
                e.dma_start(lens_i[:, :], I["lens"].partition_broadcast(P)).then_inc(ev("ld_small"), 16)
                e.dma_start(inv_freq[:, :], I["inv_freq"].partition_broadcast(P)).then_inc(ev("ld_small"), 16)
                e.dma_start(qw[:, :], I["q_norm_w"].partition_broadcast(P)).then_inc(ev("ld_small"), 16)
                e.dma_start(kw[:, :], I["k_norm_w"].partition_broadcast(P)).then_inc(ev("ld_small"), 16)
            if who == "pool":
                after(e, e.memset(ident[:, :], 0.0), "po_setup")
                after(e, e.affine_select(out=ident[:, :], in_=ident[:, :], compare_op=ALU.not_equal,
                                         fill=1.0, base=0, pattern=[[-1, P]], channel_multiplier=1), "po_setup")
                e.tensor_copy(ident_r[:, :], ident[:, :]).then_inc(ev("po_ident"), 1)
                after(e, e.memset(causal[:, :], 0.0), "po_setup")
                e.affine_select(out=causal[:, :], in_=causal[:, :], compare_op=ALU.is_ge, fill=MASKED,
                                base=0, pattern=[[-1, P]], channel_multiplier=1).then_inc(ev("po_causal"), 1)
                e.iota(key_no[:, :], pattern=[[1, CACHED]], base=0, channel_multiplier=0,
                       allow_small_or_imprecise_dtypes=True).then_inc(ev("po_iota"), 1)
                e.iota(tok_no[:, :], pattern=[[0, 1]], base=0, channel_multiplier=1,
                       allow_small_or_imprecise_dtypes=True).then_inc(ev("po_iota"), 1)
                e.memset(gate_bd[:, :], 0.0).then_inc(ev("po_gate0"), 1)
                e.memset(key_mask[:, :, CACHED:], 0.0).then_inc(ev("po_mask0"), 1)

        def st_lora_eff(who, e, which):
            src, dst = ((I["lora_a"], aeff_dram), (I["lora_b"], beff_dram))[which]
            if who == "sp":
                if which == 0:
                    wait(e, "po_gate0", 1)
                    for j in range(GJ):
                        e.dma_start(gate_bd[N_LORA * j:N_LORA * (j + 1), B * j:B * (j + 1)],
                                    I["gate_t"]).then_inc(ev("ld_gate"), 16)
                else:
                    wait(e, "pe_leff", LFLAT // 512)
                e.dma_start(la, src).then_inc(ev("ld_la"), 16)
                wait(e, "dv_leff", (LFLAT // 512) * (which + 1))
                e.dma_start(dst.rearrange("j b n -> (j b) n"), leff).then_inc(ev("st_leff"), 16)
            if who == "pe":
                if which == 0:
                    wait(e, "ld_gate", 16 * GJ)
                wait(e, "ld_la", 16 * (which + 1))
                for k in range(LFLAT // 512):
                    n = which * (LFLAT // 512) + k
                    wait(e, "dv_leff", n - 1)
                    e.matmul((b4, b5)[n % 2][0:GJ * B, :], gate_bd[:, :], la[:, 512 * k:512 * (k + 1)],
                             start=True, stop=True).then_inc(ev("pe_leff"), 1)
            if who == "dve":
                if which == 1:
                    wait(e, "st_leff", 16)
                for k in range(LFLAT // 512):
                    n = which * (LFLAT // 512) + k
                    wait(e, "pe_leff", n + 1)
                    e.tensor_copy(leff[:, 512 * k:512 * (k + 1)], (b4, b5)[n % 2][0:GJ * B, :]).then_inc(ev("dv_leff"), 1)

        def st_tables(who, e):
            if who == "dve":
                link = lambda ins: after(e, ins, "dv_tab")
                wait(e, "ld_small", 64)
                wait(e, "po_iota", 2)
                link(e.tensor_copy(lens[:, :], lens_i[:, :]))
                link(e.tensor_scalar(out=pos[:, :], in0=lens[:, :], scalar1=tok_no[:, 0:1], scalar2=None, op0=ALU.add))
                wait(e, "po_mask0", 1)
                for b in range(B):
                    e.tensor_scalar(out=key_mask[:, b, 0:CACHED], in0=key_no[:, :], scalar1=lens[:, b:b + 1],
                                    scalar2=MASKED, op0=ALU.is_ge, op1=ALU.mult).then_inc(ev("dv_mask"), 1)
                link(e.tensor_tensor(ang[:, :, :], pos[:, :].unsqueeze(2).broadcast_to([P, B, HALF]),
                                     inv_freq[:, :].unsqueeze(1).broadcast_to([P, B, HALF]), ALU.mult))
                link(e.tensor_scalar(out=turns[:, :, :], in0=ang[:, :, :], scalar1=float(1 / (2 * np.pi)),
                                     scalar2=MAGIC_ROUND, op0=ALU.mult, op1=ALU.add))
                link(e.tensor_scalar(out=turns[:, :, :], in0=turns[:, :, :], scalar1=-MAGIC_ROUND, scalar2=None, op0=ALU.add))
                for part in TWO_PI_PARTS:
                    link(e.scalar_tensor_tensor(out=ang[:, :, :], in0=turns[:, :, :], scalar=-part,
                                                in1=ang[:, :, :], op0=ALU.mult, op1=ALU.add))
                e.tensor_scalar(out=ang[:, :, :], in0=ang[:, :, :], scalar1=PI_SAFE, scalar2=-PI_SAFE,
                                op0=ALU.min, op1=ALU.max).then_inc(ev("dv_ang"), 1)
                wait(e, "ac_sin", 2)
                link(e.tensor_tensor(cos[:, :, :], cos[:, :, :], cos[:, :, :], ALU.mult))
                link(e.tensor_scalar(out=cos[:, :, :], in0=cos[:, :, :], scalar1=-2.0, scalar2=1.0, op0=ALU.mult, op1=ALU.add))
                for n, (w, t) in enumerate(((qw, 0), (qw, 1), (kw, 0), (kw, 1))):
                    wait(e, "st_tab", 16 * n)
                    for half in range(2):
                        if t == 0:
                            f, ww = cos, w[:, HALF * half:HALF * (half + 1)]
                        else:
                            f, ww = sin, w[:, HALF * (1 - half):HALF * (2 - half)]
                        dst = tab[:, :, HALF * half:HALF * (half + 1)]
                        link(e.tensor_tensor(dst, f[:, :, :], ww.unsqueeze(1).broadcast_to([P, B, HALF]), ALU.mult))
                        if t == 1 and half == 0:
                            link(e.tensor_scalar(out=dst, in0=dst, scalar1=-1.0, scalar2=None, op0=ALU.mult))
                    e.engine_nop().then_inc(ev("dv_tabn"), 1)
            if who == "act":
                wait(e, "dv_ang", 1)
                e.activation(sin[:, :, :], ang[:, :, :], ACT.Sin).then_inc(ev("ac_sin"), 1)
                e.activation(cos[:, :, :], ang[:, :, :], ACT.Sin, scale=0.5).then_inc(ev("ac_sin"), 1)
            if who == "sp":
                for n in range(4):
                    wait(e, "dv_tabn", n + 1)
                    e.dma_start(tabs_dram[:, :, HD2 * n:HD2 * (n + 1)].rearrange("b p d -> p b d"),
                                tab[:, :, :]).then_inc(ev("st_tab"), 16)

        def st_weights1(who, e):
            if who == "sp":
                e.dma_start(w_raw[:, :, :], I["w_qkv1"]).then_inc(ev("ld_w1"), 16)
                e.dma_start(wo_raw[:, :, :], I["w_o1"]).then_inc(ev("ld_w1"), 16)
            if who == "dve":
                wait(e, "ld_w1", 32)
                after(e, e.tensor_copy(wa_h[:, :, :], w_raw[:, :, :]), "dv_w1h")
                e.tensor_tensor(wa_l[:, :, :], w_raw[:, :, :], f32(wa_h[:, :, :]), ALU.subtract).then_inc(ev("dv_w1"), 1)
                after(e, e.tensor_copy(wo_h[:, :, :], wo_raw[:, :, :]), "dv_w1h")
                e.tensor_tensor(wo_l[:, :, :], wo_raw[:, :, :], f32(wo_h[:, :, :]), ALU.subtract).then_inc(ev("dv_w1"), 1)

        turn_bank = (b6, b7)
        turn_no = {}

        def turn(key):
            return turn_no.setdefault(key, len(turn_no))

        def turn_claim(pe, key):
            n = turn(key)
            wait(pe, f"turn_free{n % 2}", n // 2)
            return turn_bank[n % 2]

        def filled(e, key):
            if key in turn_no:
                wait(e, f"turn_ready{turn_no[key] % 2}", turn_no[key] // 2 + 1)

        def emptied(e, key):
            if key in turn_no:
                wait(e, f"turn_free{turn_no[key] % 2}", turn_no[key] // 2 + 1)

        def turn_ready(ins, key):
            ins.then_inc(ev(f"turn_ready{turn(key) % 2}"), 1)

        def turn_read(e, key):
            n = turn(key)
            wait(e, f"turn_ready{n % 2}", n // 2 + 1)
            return turn_bank[n % 2]

        def turn_done(ins, key):
            ins.then_inc(ev(f"turn_free{turn(key) % 2}"), 1)

        def evac_split(who, e, key, dst_h, dst_l, name):
            if who == "act":
                t = turn_read(e, key)
                e.activation(dst_h, t, ACT.Copy).then_inc(ev(f"ac_{name}"), 1)
            if who == "dve":
                t = turn_read(e, key)
                counted[name] = counted.get(name, 0) + 1
                wait(e, f"ac_{name}", counted[name])
                ins = e.tensor_tensor(dst_l, t, f32(dst_h), ALU.subtract)
                turn_done(ins, key)

        def flat(ap):
            return ap.rearrange("p a b -> p (a b)")

        def st_load1(who, e, b):
            if who == "sp":
                if b == 0:
                    wait(e, "ld_ids", 16)
                    st_load1.regs = [e.alloc_register(f"lora_id{k}") for k in range(B)]
                    e.load(st_load1.regs, ids[0:1, :])
                wait(e, "po_lw", b)
                w = e.snap(st_load1.regs[b], min_val=0, max_val=7)
                e.dma_start(lw_raw[:, :, :], I["lora_w"][bass.ds(w, 1), :, :, :].rearrange("a p c n -> (a p) c n"))\
                    .then_inc(ev("ld_lw"), 16)
                wait(e, "po_x", b - 1)
                e.dma_start(xr[b % 2][:, :, :], I["x_t"][:, :, P * b:P * (b + 1)]).then_inc(ev(f"ld_xr{b % 2}"), 16)

        def st_loadx(who, e, b):
            if who == "sp":
                wait(e, "dv_x1", b - 1)
                e.dma_start(x_in[b % 2][:, :], I["x"][b, :, :]).then_inc(ev(f"ld_x{b % 2}"), 16)

        def st_split1(who, e, b):
            cols = slice(P * b, P * (b + 1))
            if who == "dve":
                wait(e, "ld_lw", 16 * (b + 1))
                wait(e, "pe_cond", b)
                e.tensor_copy(lw_h[:, :, :], lw_raw[:, :, :]).then_inc(ev("dv_lw"), 1)
                wait(e, f"ld_xr{b % 2}", 16 * (b // 2 + 1))
                e.tensor_copy(xT_h[:, :, cols], xr[b % 2][:, :, :]).then_inc(ev("dv_x"), 1)
            if who == "pool":
                wait(e, "dv_lw", b + 1)
                wait(e, "pe_cond", b)
                e.tensor_tensor(lw_l[:, :, :], lw_raw[:, :, :], f32(lw_h[:, :, :]), ALU.subtract).then_inc(ev("po_lw"), 1)
                wait(e, "dv_x", b + 1)
                e.tensor_tensor(xT_l[:, :, cols], xr[b % 2][:, :, :], f32(xT_h[:, :, cols]), ALU.subtract).then_inc(ev("po_x"), 1)

        def st_cond(who, e, b):
            cols = slice(P * b, P * (b + 1))
            if who == "pe":
                wait(e, "po_lw", b + 1)
                wait(e, "po_x", b + 1)
                wait(e, "dv_x1", b - 2)
                split_mm(e, b0, [(xT_h[:, c, cols], xT_l[:, c, cols], lw_h[:, c, :], lw_l[:, c, :])
                                 for c in range(C)]).then_inc(ev("pe_cond"), 1)
            if who == "act":
                wait(e, "pe_cond", b + 1)
                filled(e, ("h", b - 1))
                e.activation(h_sb[:, :], b0, ACT.Copy).then_inc(ev("ac_h"), 1)

        def st_hT(who, e, b):
            if who == "pe":
                wait(e, "ac_h", b + 1)
                t = turn_claim(e, ("h", b))
                for c in range(C):
                    last = e.transpose(t[:, P * c:P * (c + 1)], h_sb[:, P * c:P * (c + 1)], ident[:, :])
                turn_ready(last, ("h", b))
            else:
                if who in ("act", "dve"):
                    wait(e, "pe_qkv", 2 * b)
                evac_split(who, e, ("h", b), flat(hT_h[:, :, :]), flat(hT_l[:, :, :]), "hT")

        def st_qkv1(who, e, b):
            if who == "pe":
                emptied(e, ("h", b))
                if b == 0:
                    wait(e, "dv_w1", 2)
                wait(e, "dv_qs", b)
                split_mm(e, b1, [(hT_h[:, c, :], hT_l[:, c, :], wa_h[:, c, 0:H1 * HD1], wa_l[:, c, 0:H1 * HD1])
                                 for c in range(C)]).then_inc(ev("pe_qkv"), 1)
                wait(e, "dv_vs", b)
                split_mm(e, b2[:, 0:2 * KV1 * HD1],
                         [(hT_h[:, c, :], hT_l[:, c, :], wa_h[:, c, H1 * HD1:], wa_l[:, c, H1 * HD1:])
                          for c in range(C)]).then_inc(ev("pe_qkv"), 1)
            q = b1.rearrange("p (h o d) -> p h o d", h=H1, o=1)
            k = b2[:, 0:KV1 * HD1].rearrange("p (h o d) -> p h o d", h=KV1, o=1)
            v = b2[:, KV1 * HD1:2 * KV1 * HD1].rearrange("p (h d) -> p h d", h=KV1)
            if who == "act":
                wait(e, "pe_qkv", 2 * b + 1)
                filled(e, ("tq", b - 1, 4))
                e.activation(qs[:, :, 0:2, :], q.broadcast_to([P, H1, 2, HD1]), ACT.Copy).then_inc(ev("ac_qs"), 1)
                wait(e, "pe_qkv", 2 * b + 2)
                e.activation(ks[:, :, 0::2, :], k.broadcast_to([P, KV1, 2, HD1]), ACT.Copy).then_inc(ev("ac_ks"), 1)
                wait(e, "pe_pv1", 8 * (b - 1))
                e.activation(vs[b % 2][:, :, 0, :], v, ACT.Copy).then_inc(ev("ac_vs"), 1)
            if who == "dve":
                wait(e, "ac_qs", b + 1)
                e.tensor_tensor(qs[:, :, 2:4, :], q.broadcast_to([P, H1, 2, HD1]), f32(qs[:, :, 0:2, :]),
                                ALU.subtract).then_inc(ev("dv_qs"), 1)
                wait(e, "ac_vs", b + 1)
                wait(e, "ac_ks", b + 1)
                e.tensor_tensor(ks[:, :, 1::2, :], k.broadcast_to([P, KV1, 2, HD1]), f32(ks[:, :, 0::2, :]),
                                ALU.subtract).then_inc(ev("dv_ks"), 1)
                e.tensor_tensor(vs[b % 2][:, :, 1, :], v, f32(vs[b % 2][:, :, 0, :]), ALU.subtract).then_inc(ev("dv_vs"), 1)

        def st_tq(who, e, b, k):
            key = ("tq", b, k)
            src = flat(ks[:, :, :, :].rearrange("p h f d -> p h (f d)")) if k == 4 else \
                flat(qs[:, :, :, :].rearrange("p h f d -> p h (f d)"))[:, 512 * k:512 * (k + 1)]
            if who == "pe":
                if k == 0:
                    wait(e, "dv_qs", b + 1)
                if k == 4:
                    wait(e, "dv_ks", b + 1)
                t = turn_claim(e, key).bitcast(R32)
                for j in range(4):
                    last = e.transpose(t[:, P * j:P * (j + 1)], src[:, P * j:P * (j + 1)], ident_r[:, :])
                turn_ready(last, key)
            if who == ("act", "dve")[k % 2]:
                dst = kT[b % 2][:, :, :] if k == 4 else qT[b % 2][:, 4 * k:4 * (k + 1), :]
                t = turn_read(e, key)
                wait(e, "pe_s1", 8 * (b - 1))
                if b == 0:
                    wait(e, "dv_w1", 2)
                    wait(e, "st_tab", 64)
                    wait(e, "st_leff", 32)
                ins = e.activation(flat(dst), t, ACT.Copy) if who == "act" else e.tensor_copy(flat(dst), t)
                turn_done(ins, key)

        def st_scores1(who, e, b, s):
            n = 8 * b + s
            half, pr = s % 2, s // 2
            rows = slice(64 * half, 64 * (half + 1))
            sc = (b4, b5)[n % 2]
            if who == "pe":
                if s == 0:
                    for k in range(5):
                        emptied(e, ("tq", b, k))
                if n == 0:
                    wait(e, "dv_leff", 2 * LFLAT // 512)
                wait(e, "dv_s1", 4 * (n - 1))
                for r in range(R1):
                    last = e.matmul(sc[:, P * r:P * (r + 1)], qT[b % 2][rows, 4 * pr + r, :],
                                    kT[b % 2][rows, pr, :], start=True, stop=True)
                last.then_inc(ev("pe_s1"), 1)
            if who == "dve":
                wait(e, "pe_s1", n + 1)
                filled(e, ("pt", n - 2))
                if n == 0:
                    wait(e, "po_causal", 1)
                wait(e, "ac_exp1", 4 * (n - 1))
                for r in range(R1):
                    e.tensor_tensor_reduce(out=p1[n % 2][:, r, :], in0=sc[:, P * r:P * (r + 1)], in1=causal[:, :],
                                           scale=-SCALE1, scalar=-LOWEST, op0=ALU.add, op1=ALU.min,
                                           accum_out=nm1[n % 2][:, r:r + 1]).then_inc(ev("dv_s1"), 1)
            if who == "act":
                wait(e, "dv_s1", 4 * (n + 1))
                wait(e, "dv_inv1", b - 1)
                for r in range(R1):
                    e.activation(p1[n % 2][:, r, :], p1[n % 2][:, r, :], ACT.Exp, bias=nm1[n % 2][:, r:r + 1],
                                 scale=-1.0, accum_out=sum1[b % 2][:, R1 * s + r:R1 * s + r + 1])\
                        .then_inc(ev("ac_exp1"), 1)

        def st_pt1(who, e, b, s):
            n = 8 * b + s
            key = ("pt", n)
            if who == "pe":
                wait(e, "ac_exp1", 4 * (n + 1))
                t = turn_claim(e, key)
                for r in range(R1):
                    last = e.transpose(t[:, P * r:P * (r + 1)], p1[n % 2][:, r, :], ident[:, :])
                turn_ready(last, key)
            else:
                if who in ("act", "dve"):
                    wait(e, "pe_pv1", n - 1)
                evac_split(who, e, key, flat(pt_h[n % 2][:, :, :]), flat(pt_l[n % 2][:, :, :]), "pt1")

        def st_pv1(who, e, b, s):
            n = 8 * b + s
            if who == "pe":
                emptied(e, ("pt", n))
                if s == 0:
                    wait(e, "dv_vs", b + 1)
                if s % 4 == 0:
                    wait(e, "dv_osum", 2 * b + s // 4)
                for r in range(R1):
                    o = b3[:, 2 * HD1 * (R1 * (s % 4) + r):][:, 0:2 * HD1]
                    v = vs[b % 2][:, s, :, :].rearrange("p a d -> p (a d)")
                    e.matmul(o, pt_h[n % 2][:, r, :], v, start=True, stop=False)
                    last = e.matmul(o, pt_l[n % 2][:, r, :], v, start=False, stop=True)
                last.then_inc(ev("pe_pv1"), 1)

        def st_osum(who, e, b, half):
            if who == "dve":
                wait(e, "pe_pv1", 8 * b + 4 * (half + 1))
                if half == 0:
                    wait(e, "dv_onorm", b)
                e.tensor_reduce(osum[:, 16 * half:16 * (half + 1), :],
                                b3.rearrange("p (h a d) -> p h d a", h=16, a=2), AX.X, ALU.add)\
                    .then_inc(ev("dv_osum"), 1)

        def st_onorm(who, e, b):
            if who == "dve":
                wait(e, "ac_exp1", 32 * (b + 1))
                e.reciprocal(inv1[:, :], sum1[b % 2][:, :]).then_inc(ev("dv_inv1"), 1)
                wait(e, "dv_inv1", b + 1)
                wait(e, "dv_osum", 2 * (b + 1))
                filled(e, ("o", b - 1))
                e.tensor_tensor(o_sb[:, :].rearrange("p (h d) -> p h d", h=H1), osum[:, :, :],
                                inv1[:, :].unsqueeze(2).broadcast_to([P, H1, HD1]), ALU.mult)\
                    .then_inc(ev("dv_onorm"), 1)

        def st_oT(who, e, b):
            key = ("o", b)
            if who == "pe":
                wait(e, "dv_onorm", b + 1)
                t = turn_claim(e, key)
                for c in range(C):
                    last = e.transpose(t[:, P * c:P * (c + 1)], o_sb[:, P * c:P * (c + 1)], ident[:, :])
                turn_ready(last, key)
            else:
                if who in ("act", "dve"):
                    wait(e, "pe_wo1", b)
                evac_split(who, e, key, flat(oT_h[:, :, :]), flat(oT_l[:, :, :]), "oT")

        def st_wo1(who, e, b):
            if who == "pe":
                emptied(e, ("o", b))
                wait(e, "ac_h", min(b + 3, B))
                split_mm(e, b0, [(oT_h[:, c, :], oT_l[:, c, :], wo_h[:, c, :], wo_l[:, c, :]) for c in range(C)])\
                    .then_inc(ev("pe_wo1"), 1)
            if who == "dve":
                wait(e, "pe_wo1", b + 1)
                wait(e, f"ld_x{b % 2}", 16 * (b // 2 + 1))
                filled(e, ("x1", b - 2))
                wait(e, f"st_x1_{b % 2}", 16 * (b // 2))
                e.tensor_tensor(x1[b % 2][:, :], b0, x_in[b % 2][:, :], ALU.add).then_inc(ev("dv_x1"), 1)
            if who == "sp":
                wait(e, "dv_x1", b + 1)
                e.dma_start(x1_dram[b, :, :], x1[b % 2][:, :]).then_inc(ev(f"st_x1_{b % 2}"), 16)

        def st_x1T(who, e, b):
            key = ("x1", b)
            cols = slice(P * b, P * (b + 1))
            if who == "pe":
                wait(e, "dv_x1", b + 1)
                t = turn_claim(e, key)
                for c in range(C):
                    last = e.transpose(t[:, P * c:P * (c + 1)], x1[b % 2][:, P * c:P * (c + 1)], ident[:, :])
                turn_ready(last, key)
            elif who in ("act", "dve"):
                t = turn_read(e, key).rearrange("p (c t) -> p c t", c=C)
                if who == "act":
                    wait(e, "pe_cond", b + 1)
                    e.activation(xT_h[:, :, cols], t, ACT.Copy).then_inc(ev("ac_x1T"), 1)
                else:
                    wait(e, "ac_x1T", b + 1)
                    turn_done(e.tensor_tensor(xT_l[:, :, cols], t, f32(xT_h[:, :, cols]), ALU.subtract), key)

        def phase1_over(e):
            for key, n in turn_no.items():
                if n >= len(turn_no) - 2:
                    emptied(e, key)
            wait(e, "st_x1_0", 16 * (B // 2))
            wait(e, "st_x1_1", 16 * (B // 2))

        def st_phase2(who, e):
            phase1_over(e)

        def st_load2(who, e, i):
            if who == "sp":
                g, b = divmod(i, B)
                if i == 0:
                    wait(e, "ld_pages", 16)
                    st_load2.regs = [e.alloc_register(f"page{k}") for k in range(PAGES_ROW)]
                wait(e, "dv_k_rope", 2 * (i - 1))
                e.dma_start(tabs[i % 2][:, :, :], tabs_dram[b, :, :].rearrange("p (t d) -> p t d", t=4))\
                    .then_inc(ev(f"ld_tabs{i % 2}"), 16)
                e.load(st_load2.regs, page_ids[0:1, PAGES_ROW * b:PAGES_ROW * (b + 1)])
                wait(e, "pe_tk", i - 1)
                wait(e, "po_vl", i - 1)
                for k in range(PAGES_ROW):
                    page = e.snap(st_load2.regs[k], min_val=0, max_val=PAGES - 1)
                    j, c = k % (P // PAGE), k // (P // PAGE)
                    e.dma_start(kv[i % 2][PAGE * j:PAGE * (j + 1), c, :],
                                I["kv_cache"][g, bass.ds(page, 1), :, :].rearrange("a p n -> (a p) n"))\
                        .then_inc(ev(f"ld_kv{i % 2}"), 16)

        def st_wload(who, e, g, c, kind):
            if who == "sp":
                wait(e, f"po_wg{kind}", C * g + c)
                e.dma_start((wst, wost)[kind][:, :], (I["w_qkv2"], I["w_o2"])[kind][g, :, c, :])\
                    .then_inc(ev(f"ld_wg{kind}"), 16)

        def st_wsplit(who, e, g, c, kind):
            n = C * g + c
            w = g % 2
            raw, hi, lo = ((wst, wg_h[w], wg_l[w]), (wost, wog_h[w], wog_l[w]))[kind]
            if who == "dve":
                wait(e, f"ld_wg{kind}", 16 * (n + 1))
                wait(e, "pe_wo2" if kind else "pe_kv", B * (g - 1))
                e.tensor_copy(hi[:, c, :], raw[:, :]).then_inc(ev(f"dv_wg{kind}"), 1)
            if who == "pool":
                wait(e, f"dv_wg{kind}", n + 1)
                wait(e, "pe_wo2" if kind else "pe_kv", B * (g - 1))
                e.tensor_tensor(lo[:, c, :], raw[:, :], f32(hi[:, c, :]), ALU.subtract).then_inc(ev(f"po_wg{kind}"), 1)

        def st_proj(who, e, i, part):
            g, b = divmod(i, B)
            w = g % 2
            cols = slice(P * b, P * (b + 1))
            if who == "pe":
                if part == 0:
                    wait(e, "po_wg0", C * (g + 1))
                    wait(e, "dv_q_rope", 2 * i)
                    wait(e, "ac_sq", 5 * i)
                if part < 2:
                    for c in range(2 * part, 2 * part + 2):
                        e.matmul(b4, xT_h[:, c, cols], wg_h[w][:, c, 0:QC], start=(c == 0), stop=False)
                        e.matmul(b4, xT_h[:, c, cols], wg_l[w][:, c, 0:QC], start=False, stop=False)
                        last = e.matmul(b4, xT_l[:, c, cols], wg_h[w][:, c, 0:QC], start=False, stop=(c == C - 1))
                    if part == 1:
                        last.then_inc(ev("pe_q"), 1)
                else:
                    wait(e, "dv_o", i - 1)
                    split_mm(e, b5[:, 0:2 * HD2],
                             [(xT_h[:, c, cols], xT_l[:, c, cols], wg_h[w][:, c, QC:], wg_l[w][:, c, QC:])
                              for c in range(C)]).then_inc(ev("pe_kv"), 1)

        def st_rope(who, e, i, part):
            q = b4.rearrange("p (h a d) -> p h a d", h=R2, a=2)
            k = b5[:, 0:HD2].rearrange("p (a d) -> p a d", a=2)
            t = tabs[i % 2]
            if who == "dve":
                tq = t[:, part, :].rearrange("p (o a d) -> p o a d", o=1, a=2).broadcast_to([P, R2, 2, HALF])
                tk = t[:, 2 + part, :].rearrange("p (a d) -> p a d", a=2)
                if part == 0:
                    wait(e, "pe_q", i + 1)
                    wait(e, f"ld_tabs{i % 2}", 16 * (i // 2 + 1))
                    wait(e, "pe_tkn", i)
                    e.tensor_tensor(qk[:, 0:R2, :, :], q, tq, ALU.mult).then_inc(ev("dv_q_rope"), 1)
                    wait(e, "pe_kv", i + 1)
                    e.tensor_tensor(qk[:, R2, :, :], k, tk, ALU.mult).then_inc(ev("dv_k_rope"), 1)
                else:
                    wait(e, "po_rope", i)
                    e.tensor_tensor(qk_sin[:, 0:R2, :, :], q[:, :, ::-1, :], tq, ALU.mult).then_inc(ev("dv_q_rope"), 1)
                    e.tensor_tensor(qk_sin[:, R2, :, :], k[:, ::-1, :], tk, ALU.mult).then_inc(ev("dv_k_rope"), 1)
            if who == "pool" and part == 1:
                wait(e, "dv_q_rope", 2 * (i + 1))
                wait(e, "dv_k_rope", 2 * (i + 1))
                e.tensor_tensor(qk[:, :, :, :], qk[:, :, :, :], qk_sin[:, :, :, :], ALU.add).then_inc(ev("po_rope"), 1)

        def st_squares(who, e, i):
            if who == "act":
                wait(e, "dv_nr_x", i)
                wait(e, "dv_q_rope", 2 * (i + 1))
                for h in range(R2):
                    e.activation(sq_junk[:, h, :], b4[:, HD2 * h:HD2 * (h + 1)], ACT.Square,
                                 accum_out=ssq[:, h:h + 1]).then_inc(ev("ac_sq"), 1)
                wait(e, "dv_k_rope", 2 * (i + 1))
                e.activation(sq_junk[:, R2, :], b5[:, 0:HD2], ACT.Square,
                             accum_out=ssq[:, R2:R2 + 1]).then_inc(ev("ac_sq"), 1)
                wait(e, "pe_pv", KC * (i - 1))
                e.activation(VN_h[i % 2][:, :], b5[:, HD2:2 * HD2], ACT.Copy).then_inc(ev("ac_vn"), 1)
            if who == "dve":
                wait(e, "ac_vn", i + 1)
                e.tensor_tensor(VN_l[i % 2][:, :], b5[:, HD2:2 * HD2], f32(VN_h[i % 2][:, :]), ALU.subtract)\
                    .then_inc(ev("dv_vn"), 1)

        def st_rstd(who, e, i):
            if who == "dve":
                link = lambda ins: after(e, ins, "dv_nr")
                wait(e, "ac_sq", 5 * (i + 1))
                wait(e, "po_rstd", 2 * i)
                e.tensor_scalar(out=nr_x[:, :], in0=ssq[:, :], scalar1=1.0 / HD2, scalar2=EPS,
                                op0=ALU.mult, op1=ALU.add).then_inc(ev("dv_nr_x"), 1)
                wait(e, "dv_nr_x", i + 1)
                link(e.tensor_scalar(out=nr_i[:, :], in0=nr_x[:, :].bitcast(I32), scalar1=1, scalar2=None,
                                     op0=ALU.logical_shift_right))
                wait(e, "dv_k_scale", i)
                e.tensor_scalar(out=rstd[:, :].bitcast(I32), in0=nr_i[:, :], scalar1=-1.0,
                                scalar2=float(RSQRT_MAGIC), op0=ALU.mult, op1=ALU.add).then_inc(ev("dv_guess"), 1)
                e.tensor_scalar(out=nr_x[:, :], in0=nr_x[:, :], scalar1=-0.5, scalar2=None, op0=ALU.mult)\
                    .then_inc(ev("dv_guess"), 1)
            if who == "pool":
                link = lambda ins: after(e, ins, "po_nr")
                wait(e, "dv_guess", 2 * (i + 1))
                for n in range(3):
                    link(e.tensor_tensor(nr_t[:, :], rstd[:, :], rstd[:, :], ALU.mult))
                    link(e.tensor_tensor(nr_t[:, :], nr_t[:, :], nr_x[:, :], ALU.mult))
                    link(e.tensor_scalar(out=nr_t[:, :], in0=nr_t[:, :], scalar1=1.5, scalar2=None, op0=ALU.add))
                    step = e.tensor_tensor(rstd[:, :], nr_t[:, :], rstd[:, :], ALU.mult)
                    if n < 2:
                        link(step)
                step.then_inc(ev("po_rstd"), 1)
                wait(e, "po_rstd", 2 * i + 1)
                wait(e, "dv_s2", 4 * (i - 1))
                e.tensor_scalar(out=q_nscale[i % 2][:, :], in0=rstd[:, 0:R2], scalar1=-SCALE2, scalar2=None,
                                op0=ALU.mult).then_inc(ev("po_rstd"), 1)

        def st_k_scale(who, e, i):
            if who == "dve":
                wait(e, "po_rstd", 2 * i + 1)
                wait(e, "po_rope", i + 1)
                e.tensor_scalar(out=qk[:, R2, :, :], in0=qk[:, R2, :, :], scalar1=rstd[:, R2:R2 + 1], scalar2=None,
                                op0=ALU.mult).then_inc(ev("dv_k_scale"), 1)

        def st_tk(who, e, i):
            if who == "pe":
                wait(e, f"ld_kv{i % 2}", 16 * PAGES_ROW * (i // 2 + 1))
                wait(e, "dv_s2", 4 * i)
                for c in range(CACHED // P):
                    last = e.transpose(b0[:, P * c:P * (c + 1)], kv[i % 2][:, c, 0:HD2], ident[:, :])
                last.then_inc(ev("pe_tk"), 1)

        def st_tk_evac(who, e, i):
            if who == "act":
                wait(e, "pe_tk", i + 1)
                wait(e, "pe_s2", 4 * i)
                e.activation(KT_h[:, 0:CACHED], b0, ACT.Copy).then_inc(ev("ac_kt"), 1)
            if who == "dve":
                wait(e, "ac_kt", i + 1)
                e.tensor_tensor(KT_l[:, 0:CACHED], b0, f32(KT_h[:, 0:CACHED]), ALU.subtract).then_inc(ev("dv_kt"), 1)

        def st_tq2(who, e, i):
            if who == "pe":
                wait(e, "dv_s2", 4 * i)
                wait(e, "po_rope", i + 1)
                for h in range(R2):
                    last = e.transpose(b1[:, P * h:P * (h + 1)], qk[:, h, :, :].rearrange("p a d -> p (a d)"),
                                       ident[:, :])
                last.then_inc(ev("pe_tq"), 1)

        def st_tq2_evac(who, e, i):
            if who == "act":
                wait(e, "pe_s2", 4 * i)
                wait(e, "pe_tq", i + 1)
                e.activation(QT_h[:, :], b1, ACT.Copy).then_inc(ev("ac_qt"), 1)
            if who == "dve":
                wait(e, "ac_qt", i + 1)
                e.tensor_tensor(QT_l[:, :], b1, f32(QT_h[:, :]), ALU.subtract).then_inc(ev("dv_qt"), 1)

        def st_tkn(who, e, i):
            if who == "pe":
                wait(e, "dv_s2", 4 * i)
                wait(e, "dv_k_scale", i + 1)
                e.transpose(b2[:, 0:P], qk[:, R2, :, :].rearrange("p a d -> p (a d)"), ident[:, :])\
                    .then_inc(ev("pe_tkn"), 1)

        def st_tkn_evac(who, e, i):
            if who == "act":
                wait(e, "pe_tkn", i + 1)
                wait(e, "pe_s2", 4 * i)
                e.activation(KT_h[:, CACHED:], b2[:, 0:P], ACT.Copy).then_inc(ev("ac_ktn"), 1)
            if who == "dve":
                wait(e, "ac_ktn", i + 1)
                e.tensor_tensor(KT_l[:, CACHED:], b2[:, 0:P], f32(KT_h[:, CACHED:]), ALU.subtract)\
                    .then_inc(ev("dv_ktn"), 1)

        def st_v(who, e, i):
            if who == "dve":
                wait(e, f"ld_kv{i % 2}", 16 * PAGES_ROW * (i // 2 + 1))
                wait(e, "pe_pv", KC * i - 1)
                e.tensor_copy(V_h[:, :, :], kv[i % 2][:, :, HD2:]).then_inc(ev("dv_vh"), 1)
            if who == "pool":
                wait(e, "dv_vh", i + 1)
                e.tensor_tensor(V_l[:, :, :], kv[i % 2][:, :, HD2:], f32(V_h[:, :, :]), ALU.subtract)\
                    .then_inc(ev("po_vl"), 1)

        def st_scores2(who, e, i, h):
            b = i % B
            n = 4 * i + h
            if who == "pe":
                if h == 0:
                    wait(e, "dv_qt", i + 1)
                    wait(e, "dv_kt", i + 1)
                    wait(e, "dv_ktn", i + 1)
                if h == 1:
                    wait(e, "dv_acc", i - 1)
                if h >= 2:
                    wait(e, "dv_s2", n - 1)
                hc = slice(P * h, P * (h + 1))
                for m, (q, kt) in enumerate(((QT_h, KT_h), (QT_h, KT_l), (QT_l, KT_h))):
                    for s in range(2):
                        last = e.matmul(pair[h % 2][:, s, 0:KEYS // 2], q[:, hc],
                                        kt[:, KEYS // 2 * s:KEYS // 2 * (s + 1)], start=(m == 0), stop=(m == 2))
                last.then_inc(ev("pe_s2"), 1)
            if who == "dve":
                wait(e, "pe_s2", n + 1)
                if h == 0:
                    wait(e, "pe_pt", KC * i)
                    wait(e, "ac_exp2", 4 * i)
                    wait(e, "po_rstd", 2 * (i + 1))
                e.tensor_tensor_reduce(out=prob[:, h, :].rearrange("p (a k) -> p a k", a=2),
                                       in0=pair[h % 2][:, :, 0:KEYS // 2],
                                       in1=key_mask[:, b, :].rearrange("p (a k) -> p a k", a=2),
                                       scale=q_nscale[i % 2][:, h:h + 1], scalar=-LOWEST, op0=ALU.add, op1=ALU.min,
                                       accum_out=nm2[:, h:h + 1]).then_inc(ev("dv_s2"), 1)
            if who == "act":
                wait(e, "dv_s2", n + 1)
                if h == 0:
                    wait(e, "dv_inv2", 4 * i)
                e.activation(prob[:, h, :], prob[:, h, :], ACT.Exp, bias=nm2[:, h:h + 1],
                             scale=-1.0, accum_out=sum2[:, h:h + 1]).then_inc(ev("ac_exp2"), 1)

        def st_norm2(who, e, i, h):
            n = 4 * i + h
            if who == "dve":
                wait(e, "ac_exp2", n + 1)
                wait(e, "po_norm", n - 3)
                e.reciprocal(inv2[:, h:h + 1], sum2[:, h:h + 1]).then_inc(ev("dv_inv2"), 1)
            if who == "pool":
                wait(e, "dv_inv2", n + 1)
                e.tensor_tensor(prob[:, h, :], prob[:, h, :], inv2[:, h:h + 1].broadcast_to([P, KEYS]), ALU.mult)\
                    .then_inc(ev("po_norm"), 1)

        def st_pt(who, e, i, c):
            n = KC * i + c
            t = (b6, b7)[n % 2]
            if who == "pe":
                wait(e, "po_norm", 4 * (i + 1))
                wait(e, "dv_pt", n - 1)
                for h in range(R2):
                    last = e.transpose(t[:, P * h:P * (h + 1)], prob[:, h, P * c:P * (c + 1)], ident[:, :])
                last.then_inc(ev("pe_pt"), 1)

        def st_pt_evac(who, e, i, c):
            n = KC * i + c
            t = (b6, b7)[n % 2]
            if who == "act":
                wait(e, "pe_pt", n + 1)
                wait(e, "pe_pv", n - 1)
                e.activation(PT_h[n % 2][:, :], t, ACT.Copy).then_inc(ev("ac_pt"), 1)
            if who == "dve":
                wait(e, "ac_pt", n + 1)
                e.tensor_tensor(PT_l[n % 2][:, :], t, f32(PT_h[n % 2][:, :]), ALU.subtract).then_inc(ev("dv_pt"), 1)

        def st_pv(who, e, i, c):
            n = KC * i + c
            if who == "pe":
                if c == 0:
                    j = min(i + 2, GROUPS)
                    wait(e, "dv_k_rope", 2 * j)
                    wait(e, "dv_vn", j)
                    wait(e, "po_vl", i + 1)
                wait(e, "dv_pt", n + 1)
                k = n % 2
                vh, vl = (V_h[:, c, :], V_l[:, c, :]) if c < KC - 1 else (VN_h[i % 2][:, :], VN_l[i % 2][:, :])
                e.matmul(b5, vh, PT_h[k][:, :], start=(c == 0), stop=False)
                e.matmul(b5, vh, PT_l[k][:, :], start=False, stop=False)
                e.matmul(b5, vl, PT_h[k][:, :], start=False, stop=(c == KC - 1)).then_inc(ev("pe_pv"), 1)

        def st_o(who, e, i):
            if who == "act":
                wait(e, "pe_pv", KC * (i + 1))
                wait(e, "pe_wo2", i)
                e.activation(OT_h[:, :], b5, ACT.Copy).then_inc(ev("ac_o"), 1)
            if who == "dve":
                wait(e, "ac_o", i + 1)
                e.tensor_tensor(OT_l[:, :], b5, f32(OT_h[:, :]), ALU.subtract).then_inc(ev("dv_o"), 1)

        def st_wo2(who, e, i):
            g, b = divmod(i, B)
            if who == "pe":
                wait(e, "dv_o", i + 1)
                wait(e, "dv_s2", min(4 * (i + 2), 4 * GROUPS))
                if b == 0:
                    wait(e, "po_wg1", C * (g + 1))
                split_mm(e, b3, [(OT_h[:, P * h:P * (h + 1)], OT_l[:, P * h:P * (h + 1)],
                                  wog_h[g % 2][:, h, :], wog_l[g % 2][:, h, :]) for h in range(R2)])\
                    .then_inc(ev("pe_wo2"), 1)

        def st_acc(who, e, i):
            g, b = divmod(i, B)
            if who == "dve":
                wait(e, "pe_wo2", i + 1)
                if g == 0:
                    e.tensor_copy(acc2[:, b, :], b3).then_inc(ev("dv_acc"), 1)
                else:
                    wait(e, "dv_acc", i - B + 1)
                    e.tensor_tensor(acc2[:, b, :], b3, acc2[:, b, :], ALU.add).then_inc(ev("dv_acc"), 1)

        def st_ffn_load(who, e):
            if who == "sp":
                wait(e, "dv_acc", GROUPS)
                e.dma_start(kern_raw[:, :, :], I["ffn_kernel"]).then_inc(ev("ld_f"), 16)
                for s in range(2):
                    for c in range(C):
                        e.dma_start(a_eff[64 * s:64 * (s + 1), :, c, 0:RANK],
                                    aeff_dram[2 * c + s, :, :].rearrange("b (p r) -> p b r", r=RANK)).then_inc(ev("ld_f"), 16)
                e.dma_start(a_sh[:, :, :], I["a_shared"]).then_inc(ev("ld_f"), 16)
                for j in range(GJ):
                    rj = RANK // GJ
                    e.dma_start(b_eff[rj * j:rj * (j + 1), :, :],
                                beff_dram[j, :, :].rearrange("b (r o) -> r b o", o=D)).then_inc(ev("ld_b"), 16)
                for b in range(B):
                    e.dma_start(b_eff[RANK:2 * RANK, b, :], I["b_shared"]).then_inc(ev("ld_b"), 16)
                    e.dma_start(b_eff[2 * RANK:2 * RANK + 1, b, :], I["bias"]).then_inc(ev("ld_b"), 16)
            if who == "dve":
                wait(e, "ld_f", 16 * (2 + 2 * C))
                e.tensor_copy(kern_h[:, :, :], kern_raw[:, :, :]).then_inc(ev("dv_kern"), 1)
                e.tensor_copy(a_eff[:, :, :, RANK:], a_sh[:, :, :].unsqueeze(1).broadcast_to([P, B, C, RANK]))\
                    .then_inc(ev("dv_aeff"), 1)
                wait(e, "dv_kern", 1)
                e.tensor_tensor(kern_l[:, :, :], kern_raw[:, :, :], f32(kern_h[:, :, :]), ALU.subtract).then_inc(ev("dv_kern"), 1)
                wait(e, "dv_aeff", 1)
                e.tensor_copy(a_h[:, :, :, :], a_eff[:, :, :, :]).then_inc(ev("dv_aeff"), 1)
                wait(e, "dv_aeff", 2)
                e.tensor_tensor(a_l[:, :, :, :], a_eff[:, :, :, :], f32(a_h[:, :, :, :]), ALU.subtract).then_inc(ev("dv_aeff"), 1)
            if who == "pool":
                wait(e, "dv_acc", GROUPS)
                for k in range(2):
                    e.memset(axT[k][2 * RANK:2 * RANK + 1, :], 1.0).then_inc(ev("po_ones"), 1)

        def st_ffn_T(who, e, b):
            k = b % 2
            t = (b0, b1)[k]
            if who == "sp":
                wait(e, "dv_y", b - 1)
                e.dma_start(x1_in[k][:, :], x1_dram[b, :, :]).then_inc(ev(f"ld_x1_{k}"), 16)
            if who == "pe":
                if b == 0:
                    wait(e, "dv_acc", GROUPS)
                wait(e, "dv_fT", b - 1)
                for c in range(C):
                    last = e.transpose(t[:, P * c:P * (c + 1)], acc2[:, b, P * c:P * (c + 1)], ident[:, :])
                last.then_inc(ev("pe_fT"), 1)
            if who == "act":
                wait(e, "pe_fT", b + 1)
                wait(e, "pe_ff", b - 1)
                e.activation(flat(oT3_h[k][:, :, :]), t, ACT.Copy).then_inc(ev("ac_fT"), 1)
            if who == "dve":
                wait(e, "ac_fT", b + 1)
                e.tensor_tensor(flat(oT3_l[k][:, :, :]), t, f32(flat(oT3_h[k][:, :, :])), ALU.subtract).then_inc(ev("dv_fT"), 1)

        def st_ffn_mm(who, e, b):
            k = b % 2
            if who == "pe":
                if b == 0:
                    wait(e, "dv_kern", 2)
                    wait(e, "dv_aeff", 3)
                wait(e, "dv_fT", b + 1)
                wait(e, "ac_ax", b - 1)
                split_mm(e, (b4, b5)[k][:, 0:2 * RANK],
                         [(oT3_h[k][:, c, :], oT3_l[k][:, c, :], a_h[:, b, c, :], a_l[:, b, c, :]) for c in range(C)])\
                    .then_inc(ev("pe_ax"), 1)
                wait(e, "dv_y", b - 1)
                o = (b2, b3)[k]
                for c in range(C):
                    e.matmul(o, oT3_h[k][:, c, :], kern_h[:, c, :], start=(c == 0), stop=False)
                    e.matmul(o, oT3_h[k][:, c, :], kern_l[:, c, :], start=False, stop=False)
                    last = e.matmul(o, oT3_l[k][:, c, :], kern_h[:, c, :], start=False, stop=False)
                last.then_inc(ev("pe_ff"), 1)
            if who == "act":
                wait(e, "pe_ax", b + 1)
                wait(e, "pe_axT", b)
                e.activation(ax[:, :], (b4, b5)[k][:, 0:2 * RANK], ACT.Copy).then_inc(ev("ac_ax"), 1)

        def st_ffn_out(who, e, b):
            k = b % 2
            t = (b6, b7)[k][0:2 * RANK, 0:P]
            if who == "pe":
                wait(e, "ac_ax", b + 1)
                wait(e, "ac_axT", b - 1)
                e.transpose(t, ax[:, :], ident[:, :]).then_inc(ev("pe_axT"), 1)
                if b == 0:
                    wait(e, "ld_b", 16 * (GJ + 2 * B))
                    wait(e, "po_ones", 2)
                wait(e, "ac_axT", b + 1)
                e.matmul((b2, b3)[k], axT[k][:, :], b_eff[:, b, :], start=False, stop=True).then_inc(ev("pe_out"), 1)
            if who == "act":
                wait(e, "pe_axT", b + 1)
                wait(e, "pe_out", b - 1)
                e.activation(axT[k][0:2 * RANK, :], t, ACT.Copy).then_inc(ev("ac_axT"), 1)
            if who == "dve":
                wait(e, "pe_out", b + 1)
                wait(e, f"ld_x1_{k}", 16 * (b // 2 + 1))
                wait(e, f"st_y{k}", 16 * (b // 2))
                e.tensor_tensor(y[k][:, :], (b2, b3)[k], x1_in[k][:, :], ALU.add).then_inc(ev("dv_y"), 1)
            if who == "sp":
                wait(e, "dv_y", b + 1)
                e.dma_start(out[b, :, :], y[k][:, :]).then_inc(ev(f"st_y{k}"), 16)

        def st_end(who, e):
            if who == "sp":
                for k in range(2):
                    wait(e, f"st_y{k}", 16 * (B // 2))

        plan = []
        add = lambda f, *a: plan.append((f, a))

        add(st_constants)
        add(st_load1, 0)
        add(st_lora_eff, 0)
        add(st_lora_eff, 1)
        add(st_tables)
        add(st_weights1)
        add(st_split1, 0)
        add(st_cond, 0)
        add(st_load1, 1)
        add(st_hT, 0)
        add(st_qkv1, 0)
        add(st_split1, 1)
        for k in range(5):
            add(st_tq, 0, k)
        for b in range(B + 1):
            core, nxt, prev = b < B, b + 1 < B, b > 0
            if core:
                add(st_loadx, b)
            for s in range(8):
                if core:
                    add(st_scores1, b, s)
                if s == 0:
                    if prev:
                        add(st_pv1, b - 1, 6)
                        add(st_pt1, b - 1, 7)
                elif s == 1:
                    if prev:
                        add(st_pv1, b - 1, 7)
                        add(st_osum, b - 1, 1)
                        add(st_onorm, b - 1)
                    if core:
                        add(st_pt1, b, 0)
                elif core:
                    add(st_pv1, b, s - 2)
                    if s == 5:
                        add(st_osum, b, 0)
                    add(st_pt1, b, s - 1)
                if s == 1 and nxt:
                    add(st_cond, b + 1)
                if s == 2:
                    if nxt:
                        add(st_hT, b + 1)
                    if prev:
                        add(st_oT, b - 1)
                if s == 3 and prev:
                    add(st_wo1, b - 1)
                if s == 4:
                    if prev:
                        add(st_x1T, b - 1)
                    if b + 2 < B:
                        add(st_load1, b + 2)
                if s == 5 and nxt:
                    add(st_qkv1, b + 1)
                if s == 6 and nxt:
                    for k in range(3):
                        add(st_tq, b + 1, k)
                if s == 7:
                    if nxt:
                        for k in range(3, 5):
                            add(st_tq, b + 1, k)
                    if b + 2 < B:
                        add(st_split1, b + 2)

        add(st_phase2)
        split_in = {i: [] for i in range(GROUPS)}
        split_in[0] = [(0, c, 1) for c in range(C)]
        for g in range(1, KV2):
            for c in range(C):
                split_in[B * (g - 1) + 1 + c].append((g, c, 0))
                split_in[B * (g - 1) + C + 1 + c].append((g, c, 1))
        add(st_load2, 0)
        for c in range(C):
            add(st_wload, 0, c, 0)
            add(st_wsplit, 0, c, 0)
        add(st_wload, 0, 0, 1)
        add(st_load2, 1)
        for part in range(3):
            add(st_proj, 0, part)
        add(st_rope, 0, 0)
        add(st_rope, 0, 1)
        add(st_squares, 0)
        add(st_rstd, 0)
        add(st_tk, 0)
        add(st_tk_evac, 0)
        add(st_tq2, 0)
        add(st_tq2_evac, 0)
        add(st_k_scale, 0)
        add(st_tkn, 0)
        add(st_tkn_evac, 0)
        add(st_v, 0)
        for i in range(GROUPS):
            g, b = divmod(i, B)
            nxt, prev = i + 1 < GROUPS, i > 0

            def if_next(f, *a):
                if nxt:
                    add(f, i + 1, *a)

            if i + 2 < GROUPS:
                add(st_load2, i + 2)
            if prev:
                add(st_o, i - 1)
            add(st_scores2, i, 0)
            add(st_scores2, i, 1)
            if_next(st_proj, 0)
            add(st_norm2, i, 0)
            add(st_scores2, i, 2)
            if_next(st_proj, 1)
            add(st_norm2, i, 1)
            add(st_scores2, i, 3)
            if_next(st_proj, 2)
            add(st_norm2, i, 2)
            if_next(st_rope, 0)
            add(st_norm2, i, 3)
            if_next(st_rope, 1)
            if_next(st_tk)
            if_next(st_squares)
            add(st_pt, i, 0)
            add(st_pt, i, 1)
            if_next(st_rstd)
            if prev:
                add(st_wo2, i - 1)
            add(st_pt_evac, i, 0)
            add(st_pt_evac, i, 1)
            if_next(st_tk_evac)
            add(st_pv, i, 0)
            add(st_pt, i, 2)
            add(st_pt_evac, i, 2)
            if prev:
                add(st_acc, i - 1)
            add(st_pv, i, 1)
            add(st_pt, i, 3)
            if_next(st_k_scale)
            add(st_pt_evac, i, 3)
            if_next(st_tq2)
            add(st_pv, i, 2)
            add(st_pt, i, 4)
            if_next(st_tq2_evac)
            if_next(st_tkn)
            add(st_pt_evac, i, 4)
            if_next(st_tkn_evac)
            add(st_pv, i, 3)
            add(st_pv, i, 4)
            if_next(st_v)
            for n, piece in enumerate(split_in[i]):
                add(st_wsplit, *piece)
                if n + 1 < len(split_in[i]):
                    add(st_wload, *split_in[i][n + 1])
            if nxt:
                for piece in split_in[i + 1][:1]:
                    add(st_wload, *piece)
        add(st_o, GROUPS - 1)
        add(st_wo2, GROUPS - 1)
        add(st_acc, GROUPS - 1)

        add(st_ffn_load)
        add(st_ffn_T, 0)
        for b in range(B):
            add(st_ffn_mm, b)
            if b + 1 < B:
                add(st_ffn_T, b + 1)
            add(st_ffn_out, b)
        add(st_end)

        for f, a in plan:
            if f is st_hT:
                turn(("h", a[0]))
            elif f is st_tq:
                turn(("tq",) + a)
            elif f is st_pt1:
                turn(("pt", 8 * a[0] + a[1]))
            elif f is st_oT:
                turn(("o", a[0]))
            elif f is st_x1T:
                turn(("x1", a[0]))

        def run(who, e):
            for f, a in plan:
                f(who, e, *a)

        block = ctx.enter_context(nc.Block())

        @block.sync
        def _(e):
            run("sp", e)

        @block.gpsimd
        def _(e):
            run("pool", e)

        @block.vector
        def _(e):
            run("dve", e)

        @block.scalar
        def _(e):
            run("act", e)

        @block.tensor
        def _(e):
            run("pe", e)


def kernel(**inputs):
    import numpy as np
    import concourse.bacc as bacc
    from concourse import mybir
    from concourse.bass_utils import run_bass_kernel_spmd

    a = {k: np.asarray(v) for k, v in inputs.items()}
    con = np.ascontiguousarray

    def chunks(w):
        return con(w.reshape(-1, P, w.shape[-1]).transpose(1, 0, 2))

    wq1 = a["L0_attn_wq"].reshape(D, KV1 // 2, 2, R1, HD1).transpose(0, 1, 3, 2, 4).reshape(D, H1 * HD1)
    w_q = a["L0_cond2_Wq"].reshape(KV2, QC, D)
    w_k = a["L0_cond2_Wk"].reshape(KV2, HD2, D)
    w_v = a["L0_cond2_Wv"].reshape(KV2, HD2, D)
    w_qkv2 = np.concatenate([w_q, w_k, w_v], axis=1)
    w_qkv2 = w_qkv2.transpose(0, 2, 1).reshape(KV2, C, P, WC).transpose(0, 2, 1, 3)
    w_o2 = a["L0_cond2_Wo"].reshape(D, KV2, R2, HD2).transpose(1, 3, 2, 0)
    kv_cache = np.concatenate([a["L0_cond2_k_cache"], a["L0_cond2_v_cache"]], axis=-1)
    arrays = {
        "x": a["x"],
        "x_t": chunks(a["x"].reshape(B * P, D).T),
        "lora_ids": a["itok_B_3_7"].reshape(1, B),
        "page_ids": a["itok_Bx16_0_63"].reshape(1, B * PAGES_ROW),
        "lens": a["itok_B_207_1644"].reshape(B),
        "lora_w": a["L0_cond_weight"].transpose(0, 2, 1).reshape(8, C, P, D).transpose(0, 2, 1, 3),
        "w_qkv1": chunks(np.concatenate([wq1, a["L0_attn_wk"], a["L0_attn_wv"]], axis=1)),
        "w_o1": chunks(a["L0_attn_wo"]),
        "w_qkv2": w_qkv2,
        "w_o2": w_o2,
        "q_norm_w": a["L0_cond2_q_norm_w"],
        "k_norm_w": a["L0_cond2_k_norm_w"],
        "kv_cache": kv_cache.transpose(2, 0, 1, 3),
        "gate_t": a["L0_ffn_gate"].T,
        "lora_a": a["L0_ffn_lora_A"].transpose(0, 2, 1).reshape(N_LORA, GJ, LFLAT).transpose(1, 0, 2).reshape(P, LFLAT),
        "lora_b": a["L0_ffn_lora_B"].transpose(0, 2, 1).reshape(N_LORA, GJ, LFLAT).transpose(1, 0, 2).reshape(P, LFLAT),
        "a_shared": chunks(a["L0_ffn_lora_A_shared"].T),
        "b_shared": a["L0_ffn_lora_B_shared"].T,
        "bias": a["L0_ffn_bias"].reshape(1, D),
        "ffn_kernel": chunks(a["L0_ffn_kernel"]),
        "inv_freq": (np.float32(1.0) / np.power(np.float32(10000.0), np.arange(0, HD2, 2, dtype=np.float32) / np.float32(HD2))),
    }
    arrays = {k: con(v) for k, v in arrays.items()}
    nc = bacc.Bacc("TRN2", target_bir_lowering=False, num_devices=1)
    I = {k: nc.dram_tensor(f"in_{k}", v.shape, mybir.dt.from_np(v.dtype), kind="ExternalInput").ap()
         for k, v in arrays.items()}
    out = nc.dram_tensor("out_y", (B, P, D), mybir.dt.float32, kind="ExternalOutput").ap()
    build_program(nc, I, out)
    r = run_bass_kernel_spmd(nc, [{f"in_{k}": v for k, v in arrays.items()}], core_ids=[0])
    return r.results[0]["out_y"]
```

```python
from contextlib import ExitStack

import numpy as np
import concourse.bass as bass
from concourse import mybir

F32 = mybir.dt.float32
R32 = mybir.dt.float32r
BF16 = mybir.dt.bfloat16
I32 = mybir.dt.int32
ALU = mybir.AluOpType
ACT = mybir.ActivationFunctionType
AX = mybir.AxisListType

P = 128
B = 8
D = 512
C = D // P
H1, KV1, HD1 = 32, 8, 16
R1 = H1 // KV1
QKV1 = (H1 + 2 * KV1) * HD1
SCALE1 = HD1 ** -0.5
STEPS = B * KV1
H2, KV2, HD2 = 32, 8, 128
R2 = H2 // KV2
PAGES, PAGE, PAGES_ROW = 64, 32, 16
CACHED = PAGE * PAGES_ROW
KEYS = CACHED + P
KC = KEYS // P
SCALE2 = 1.0 / float(np.sqrt(HD2))
EPS = 1e-6
QC = R2 * HD2
WC = QC + 2 * HD2
GROUPS = KV2 * B
HALF = HD2 // 2
N_LORA, RANK = 16, 32
GJ = 8
LFLAT = D * RANK // GJ
MASKED = -1e30
LOWEST = -3e38
MAGIC_ROUND = 12582912.0
TWO_PI_PARTS = (6.28125, 0.0019350051879882812, 3.019916050561733e-07)
PI_SAFE = 3.1415925
RSQRT_MAGIC = 0x5F3759DF


def build_program(nc, I, out):
    ctx = ExitStack()
    with ctx:
        def sb(name, shape, dt=F32, scope=ctx):
            return scope.enter_context(nc.sbuf_tensor(name, shape, dt))

        def sem(name):
            return ctx.enter_context(nc.semaphore(name))

        x1_dram = nc.dram_tensor("x1_dram", [B, P, D], F32, kind="Internal").ap()
        tabs_dram = nc.dram_tensor("tabs_dram", [B, P, 4 * HD2], F32, kind="Internal").ap()
        aeff_dram = nc.dram_tensor("aeff_dram", [GJ, B, LFLAT], F32, kind="Internal").ap()
        beff_dram = nc.dram_tensor("beff_dram", [GJ, B, LFLAT], F32, kind="Internal").ap()

        bank = [ctx.enter_context(nc.psum_tensor(f"bank{i}", [P, 512], F32)) for i in range(4, 8)]
        pair = [ctx.enter_context(nc.psum_tensor(f"pair{i}", [P, 2, 512], F32)) for i in range(2)]
        b0, b1, b2, b3 = (pair[0][:, 0, :], pair[0][:, 1, :], pair[1][:, 0, :], pair[1][:, 1, :])
        b4, b5, b6, b7 = (t[:, :] for t in bank)

        xT_h = sb("xT_h", [P, C, B * P], R32)
        xT_l = sb("xT_l", [P, C, B * P], R32)
        ident = sb("ident", [P, P])
        ident_r = sb("ident_r", [P, P], R32)
        lens = sb("lens", [P, B])
        page_ids = sb("page_ids", [1, B * PAGES_ROW], I32)
        key_mask = sb("key_mask", [P, B, KEYS], BF16)
        acc2 = sb("acc2", [P, B, D])

        kv = [sb(f"kv{k}", [P, CACHED // P, 2 * HD2]) for k in range(2)]

        ph1 = ExitStack()
        s1 = lambda name, shape, dt=F32: sb(name, shape, dt, ph1)
        lw_raw = s1("lw_raw", [P, C, D])
        lw_h, lw_l = s1("lw_h", [P, C, D], R32), s1("lw_l", [P, C, D], R32)
        wa_h, wa_l = s1("wa_h", [P, C, QKV1], R32), s1("wa_l", [P, C, QKV1], R32)
        wo_h, wo_l = s1("wo_h", [P, C, D], R32), s1("wo_l", [P, C, D], R32)
        x_in = [s1(f"x_in{k}", [P, D]) for k in range(2)]
        osum = s1("osum", [P, H1, HD1])
        o_sb = s1("o_sb", [P, D])
        oT_h, oT_l = s1("oT_h", [P, C, P], R32), s1("oT_l", [P, C, P], R32)
        x1 = [s1(f"x1_{k}", [P, D]) for k in range(2)]
        xr = [s1(f"xr{k}", [P, C, P]) for k in range(2)]
        h_sb = s1("h_sb", [P, D])
        hT_h, hT_l = s1("hT_h", [P, C, P], R32), s1("hT_l", [P, C, P], R32)
        qs = s1("qs", [P, H1, 4, HD1], R32)
        ks = s1("ks", [P, KV1, 4, HD1], R32)
        vs = [s1(f"vs{k}", [P, KV1, 2, HD1], R32) for k in range(2)]
        causal = s1("causal", [P, P])
        ids = s1("ids", [1, B], I32)
        lens_i = s1("lens_i", [P, B], I32)
        pos = s1("pos", [P, B])
        tok_no = s1("tok_no", [P, 1])
        inv_freq = s1("inv_freq", [P, HALF])
        qw, kw = s1("qw", [P, HD2]), s1("kw", [P, HD2])
        gate_bd = s1("gate_bd", [P, GJ * B])
        acc_flat = acc2[:, :, :].rearrange("p b d -> p (b d)")
        AN = B * HALF
        ang, turns, cos, sin = (acc_flat[:, AN * k:AN * (k + 1)].rearrange("p (b d) -> p b d", b=B) for k in range(4))
        tab = acc_flat[:, 4 * AN:6 * AN].rearrange("p (b d) -> p b d", b=B)
        key_no = acc_flat[:, 6 * AN:6 * AN + CACHED]
        LH = LFLAT // 2
        la = kv[0][:, :, :].rearrange("p c n -> p (c n)")
        leff = kv[1][0:GJ * B, :, :].rearrange("p c n -> p (c n)")
        raw = ExitStack()
        w_raw, wo_raw = sb("w_raw", [P, C, QKV1], F32, raw), sb("wo_raw", [P, C, D], F32, raw)
        raw.close()
        qT = [s1(f"qT{k}", [P, H1 // 2, P], R32) for k in range(2)]
        kT = [s1(f"kT{k}", [P, KV1 // 2, P], R32) for k in range(2)]
        p1 = [s1(f"p1_{k}", [P, R1, P]) for k in range(2)]
        nm1 = [s1(f"nm1_{k}", [P, R1]) for k in range(2)]
        sum1 = [s1(f"sum1_{k}", [P, H1]) for k in range(2)]
        inv1 = s1("inv1", [P, H1])
        pt_h = [s1(f"pt_h{k}", [P, R1, P], R32) for k in range(2)]
        pt_l = [s1(f"pt_l{k}", [P, R1, P], R32) for k in range(2)]
        ph1.close()

        ph2 = ExitStack()
        s2 = lambda name, shape, dt=F32: sb(name, shape, dt, ph2)
        wg_h, wg_l, wog_h, wog_l, tabs = [], [], [], [], []
        for k in range(2):
            wg_h.append(s2(f"wg_h{k}", [P, C, WC], R32))
            wg_l.append(s2(f"wg_l{k}", [P, C, WC], R32))
            if k == 0:
                wst = s2("wst", [P, WC])
                wost = s2("wost", [P, D])
            wog_h.append(s2(f"wog_h{k}", [P, R2, D], R32))
            wog_l.append(s2(f"wog_l{k}", [P, R2, D], R32))
            tabs.append(s2(f"tabs{k}", [P, 4, HD2]))
        KT_h, KT_l = s2("KT_h", [P, KEYS], R32), s2("KT_l", [P, KEYS], R32)
        V_h, V_l = s2("V_h", [P, KC - 1, HD2], R32), s2("V_l", [P, KC - 1, HD2], R32)
        VN_h = [s2(f"VN_h{k}", [P, HD2], R32) for k in range(2)]
        VN_l = [s2(f"VN_l{k}", [P, HD2], R32) for k in range(2)]
        QT_h, QT_l = s2("QT_h", [P, QC], R32), s2("QT_l", [P, QC], R32)
        qk = s2("qk", [P, R2 + 1, 2, HALF])
        qk_sin = s2("qk_sin", [P, R2 + 1, 2, HALF])
        sq_junk = s2("sq_junk", [P, R2 + 1, HD2])
        ssq = s2("ssq", [P, R2 + 1])
        nr_x, nr_t = s2("nr_x", [P, R2 + 1]), s2("nr_t", [P, R2 + 1])
        nr_i = s2("nr_i", [P, R2 + 1], I32)
        rstd = s2("rstd", [P, R2 + 1])
        q_nscale = [s2(f"q_nscale{k}", [P, R2]) for k in range(2)]
        prob = s2("prob", [P, R2, KEYS])
        nm2 = s2("nm2", [P, R2])
        sum2, inv2 = s2("sum2", [P, R2]), s2("inv2", [P, R2])
        PT_h = [s2(f"PT_h{k}", [P, R2 * P], R32) for k in range(3)]
        PT_l = [s2(f"PT_l{k}", [P, R2 * P], R32) for k in range(3)]
        OT_h, OT_l = s2("OT_h", [P, R2 * P], R32), s2("OT_l", [P, R2 * P], R32)
        ph2.close()

        s3 = lambda name, shape, dt=F32: sb(name, shape, dt)
        kern_h, kern_l = s3("kern_h", [P, C, D], R32), s3("kern_l", [P, C, D], R32)
        kst = s3("kst", [P, D])
        a_eff = s3("a_eff", [P, B, C, 2 * RANK])
        a_h, a_l = s3("a_h", [P, B, C, 2 * RANK], R32), s3("a_l", [P, B, C, 2 * RANK], R32)
        a_sh = s3("a_sh", [P, C, RANK])
        x1_in = [s3(f"x1_in{k}", [P, D]) for k in range(2)]
        oT3_h = [s3(f"oT3_h{k}", [P, C, P], R32) for k in range(2)]
        oT3_l = [s3(f"oT3_l{k}", [P, C, P], R32) for k in range(2)]
        b_eff = s3("b_eff", [2 * RANK + 1, B, D])
        ax = s3("ax", [P, 2 * RANK])
        axT = [s3(f"axT{k}", [2 * RANK + 1, P]) for k in range(2)]
        y = [s3(f"y{k}", [P, D]) for k in range(2)]

        sems = {}

        def ev(name):
            if name not in sems:
                sems[name] = sem(name)
            return sems[name]

        counted = {}

        def after(eng, ins, name, n=1):
            counted[name] = counted.get(name, 0) + n
            ins.then_inc(ev(name), n)
            eng.wait_ge(ev(name), counted[name])

        def wait(eng, name, n):
            if n >= 1:
                eng.wait_ge(ev(name), n)

        def f32(ap):
            return ap.bitcast(F32)

        def split_mm(pe, o, pairs, part=0, parts=1):
            size = len(pairs) // parts
            for n in range(size * part, size * (part + 1)):
                ah, al, bh, bl = pairs[n]
                pe.matmul(o, ah, bh, start=(n == 0), stop=False)
                pe.matmul(o, ah, bl, start=False, stop=False)
                last = pe.matmul(o, al, bh, start=False, stop=(n == len(pairs) - 1))
            return last

        def st_constants(who, e):
            if who == "sp":
                e.dma_start(page_ids[:, :], I["page_ids"]).then_inc(ev("ld_pages"), 16)
                e.dma_start(lens_i[:, :], I["lens"].partition_broadcast(P)).then_inc(ev("ld_small"), 16)
                e.dma_start(inv_freq[:, :], I["inv_freq"].partition_broadcast(P)).then_inc(ev("ld_small"), 16)
                e.dma_start(qw[:, :], I["q_norm_w"].partition_broadcast(P)).then_inc(ev("ld_small"), 16)
                e.dma_start(kw[:, :], I["k_norm_w"].partition_broadcast(P)).then_inc(ev("ld_small"), 16)
            if who == "pool":
                after(e, e.memset(ident[:, :], 0.0), "po_setup")
                after(e, e.affine_select(out=ident[:, :], in_=ident[:, :], compare_op=ALU.not_equal,
                                         fill=1.0, base=0, pattern=[[-1, P]], channel_multiplier=1), "po_setup")
                e.tensor_copy(ident_r[:, :], ident[:, :]).then_inc(ev("po_ident"), 1)
                after(e, e.memset(causal[:, :], 0.0), "po_setup")
                e.affine_select(out=causal[:, :], in_=causal[:, :], compare_op=ALU.is_ge, fill=MASKED,
                                base=0, pattern=[[-1, P]], channel_multiplier=1).then_inc(ev("po_causal"), 1)
                e.iota(key_no, pattern=[[1, CACHED]], base=0, channel_multiplier=0,
                       allow_small_or_imprecise_dtypes=True).then_inc(ev("po_iota"), 1)
                e.iota(tok_no[:, :], pattern=[[0, 1]], base=0, channel_multiplier=1,
                       allow_small_or_imprecise_dtypes=True).then_inc(ev("po_iota"), 1)
                e.memset(gate_bd[:, :], 0.0).then_inc(ev("po_gate0"), 1)
                e.memset(key_mask[:, :, CACHED:], 0.0).then_inc(ev("po_mask0"), 1)

        def st_lora_load(who, e, which):
            if who == "sp":
                if which == 0:
                    wait(e, "po_gate0", 1)
                    for j in range(GJ):
                        e.dma_start(gate_bd[N_LORA * j:N_LORA * (j + 1), B * j:B * (j + 1)],
                                    I["gate_t"]).then_inc(ev("ld_gate"), 16)
                wait(e, "pe_leff", 2 * which)
                src, half = I[("lora_a", "lora_b")[which // 2]], which % 2
                e.dma_start(la, src[:, LH * half:LH * (half + 1)]).then_inc(ev("ld_la"), 16)

        def st_lora_eff(who, e, m, rows_h):
            which, k = divmod(m, 2)
            if who == "pe":
                wait(e, "ac_h", rows_h)
                if m == 0:
                    wait(e, "ld_gate", 16 * GJ)
                wait(e, "ld_la", 16 * (which + 1))
                wait(e, "dv_leff", m)
                e.matmul(b0[0:GJ * B, :], gate_bd[:, :], la[:, 512 * k:512 * (k + 1)],
                         start=True, stop=True).then_inc(ev("pe_leff"), 1)
            if who == "dve":
                wait(e, "st_leff", 16 * which)
                wait(e, "pe_leff", m + 1)
                e.tensor_copy(leff[:, 512 * k:512 * (k + 1)], b0[0:GJ * B, :]).then_inc(ev("dv_leff"), 1)

        def st_lora_store(who, e, which):
            if who == "sp":
                dst, half = (aeff_dram, beff_dram)[which // 2], which % 2
                wait(e, "dv_leff", 2 * (which + 1))
                e.dma_start(dst.rearrange("j b n -> (j b) n")[:, LH * half:LH * (half + 1)], leff)\
                    .then_inc(ev("st_leff"), 16)

        def st_masks(who, e):
            if who == "dve":
                link = lambda ins: after(e, ins, "dv_tab")
                wait(e, "ld_small", 64)
                wait(e, "po_iota", 2)
                link(e.tensor_copy(lens[:, :], lens_i[:, :]))
                link(e.tensor_scalar(out=pos[:, :], in0=lens[:, :], scalar1=tok_no[:, 0:1], scalar2=None, op0=ALU.add))
                wait(e, "po_mask0", 1)
                for b in range(B):
                    e.tensor_scalar(out=key_mask[:, b, 0:CACHED], in0=key_no, scalar1=lens[:, b:b + 1],
                                    scalar2=MASKED, op0=ALU.is_ge, op1=ALU.mult).then_inc(ev("dv_mask"), 1)

        def st_angles(who, e):
            if who == "dve":
                link = lambda ins: after(e, ins, "dv_tab")
                link(e.tensor_tensor(ang, pos[:, :].unsqueeze(2).broadcast_to([P, B, HALF]),
                                     inv_freq[:, :].unsqueeze(1).broadcast_to([P, B, HALF]), ALU.mult))
                link(e.tensor_scalar(out=turns, in0=ang, scalar1=float(1 / (2 * np.pi)),
                                     scalar2=MAGIC_ROUND, op0=ALU.mult, op1=ALU.add))
                link(e.tensor_scalar(out=turns, in0=turns, scalar1=-MAGIC_ROUND, scalar2=None, op0=ALU.add))
                for part in TWO_PI_PARTS:
                    link(e.scalar_tensor_tensor(out=ang, in0=turns, scalar=-part,
                                                in1=ang, op0=ALU.mult, op1=ALU.add))
                e.tensor_scalar(out=ang, in0=ang, scalar1=PI_SAFE, scalar2=-PI_SAFE,
                                op0=ALU.min, op1=ALU.max).then_inc(ev("dv_ang"), 1)
            if who == "act":
                wait(e, "dv_ang", 1)
                e.activation(sin, ang, ACT.Sin).then_inc(ev("ac_sin"), 1)
                e.activation(cos, ang, ACT.Sin, scale=0.5).then_inc(ev("ac_sin"), 1)

        def st_table(who, e, n):
            w, t = ((qw, 0), (qw, 1), (kw, 0), (kw, 1))[n]
            if who == "dve":
                link = lambda ins: after(e, ins, "dv_tab")
                if n == 0:
                    wait(e, "ac_sin", 2)
                    link(e.tensor_tensor(cos, cos, cos, ALU.mult))
                    link(e.tensor_scalar(out=cos, in0=cos, scalar1=-2.0, scalar2=1.0, op0=ALU.mult, op1=ALU.add))
                if n == 1:
                    e.tensor_scalar(out=ang, in0=sin, scalar1=-1.0, scalar2=None, op0=ALU.mult)\
                        .then_inc(ev("dv_nsin"), 1)
                    wait(e, "dv_nsin", 1)
                wait(e, "st_tab", 16 * n)
                for half in range(2):
                    f = cos if t == 0 else (ang, sin)[half]
                    part = half if t == 0 else 1 - half
                    e.tensor_tensor(tab[:, :, HALF * half:HALF * (half + 1)], f,
                                    w[:, HALF * part:HALF * (part + 1)].unsqueeze(1).broadcast_to([P, B, HALF]),
                                    ALU.mult).then_inc(ev("dv_tabn"), 1)
            if who == "sp":
                wait(e, "dv_tabn", 2 * (n + 1))
                e.dma_start(tabs_dram[:, :, HD2 * n:HD2 * (n + 1)].rearrange("b p d -> p b d"),
                            tab).then_inc(ev("st_tab"), 16)

        def st_weights1(who, e, kind):
            raw, hi, lo = ((w_raw, wa_h, wa_l), (wo_raw, wo_h, wo_l))[kind]
            if who == "sp":
                e.dma_start(raw[:, :, :], I[("w_qkv1", "w_o1")[kind]]).then_inc(ev(f"ld_w1_{kind}"), 16)
            if who == "dve":
                wait(e, f"ld_w1_{kind}", 16)
                after(e, e.tensor_copy(hi[:, :, :], raw[:, :, :]), "dv_w1h")
                e.tensor_tensor(lo[:, :, :], raw[:, :, :], f32(hi[:, :, :]), ALU.subtract).then_inc(ev("dv_w1"), 1)

        turn_bank = {"p0": b6, "p1": b7, "0": b0, "1": b1, "2": b2}
        bank_uses = {}

        def turn_place(key):
            if key[0] == "pt":
                return f"p{key[1] % 2}"
            if key == ("x1", B - 1):
                return "p0"
            return "0" if key[0] == "o" else "2" if key[0] == "tq" and key[2] in (1, 3) else "1"

        def turn(key):
            where = turn_place(key)
            order = bank_uses.setdefault(where, [])
            if key not in order:
                order.append(key)
            return where, order.index(key)

        def turn_claim(pe, key):
            where, n = turn(key)
            wait(pe, f"turn_free_{where}", n)
            return turn_bank[where]

        def filled(e, key):
            if key in bank_uses.get(turn_place(key), ()):
                where, n = turn(key)
                wait(e, f"turn_ready_{where}", n + 1)

        def emptied(e, key):
            if key in bank_uses.get(turn_place(key), ()):
                where, n = turn(key)
                wait(e, f"turn_free_{where}", n + 1)

        def turn_ready(ins, key):
            ins.then_inc(ev(f"turn_ready_{turn(key)[0]}"), 1)

        def turn_read(e, key):
            filled(e, key)
            return turn_bank[turn(key)[0]]

        def turn_done(ins, key):
            ins.then_inc(ev(f"turn_free_{turn(key)[0]}"), 1)

        def evac_split(who, e, key, dst_h, dst_l, name):
            if who == "act":
                t = turn_read(e, key)
                e.activation(dst_h, t, ACT.Copy).then_inc(ev(f"ac_{name}"), 1)
            if who == "dve":
                t = turn_read(e, key)
                counted[name] = counted.get(name, 0) + 1
                wait(e, f"ac_{name}", counted[name])
                ins = e.tensor_tensor(dst_l, t, f32(dst_h), ALU.subtract)
                turn_done(ins, key)

        def flat(ap):
            return ap.rearrange("p a b -> p (a b)")

        def st_load1(who, e, b):
            if who == "sp":
                if b == 0:
                    e.dma_start(ids[:, :], I["lora_ids"]).then_inc(ev("ld_ids"), 16)
                    wait(e, "ld_ids", 16)
                    st_load1.regs = [e.alloc_register(f"lora_id{k}") for k in range(B)]
                    e.load(st_load1.regs, ids[0:1, :])
                wait(e, "lw_split", b)
                w = e.snap(st_load1.regs[b], min_val=0, max_val=7)
                e.dma_start(lw_raw[:, :, :], I["lora_w"][bass.ds(w, 1), :, :, :].rearrange("a p c n -> (a p) c n"))\
                    .then_inc(ev("ld_lw"), 16)
                wait(e, "x_split", b - 1)
                e.dma_start(xr[b % 2][:, :, :], I["x_t"][:, :, P * b:P * (b + 1)]).then_inc(ev(f"ld_xr{b % 2}"), 16)

        def st_loadx(who, e, b):
            if who == "sp":
                wait(e, "dv_x1", b - 1)
                e.dma_start(x_in[b % 2][:, :], I["x"][b, :, :]).then_inc(ev(f"ld_x{b % 2}"), 16)

        def st_split1(who, e, b):
            cols = slice(P * b, P * (b + 1))
            if who == "dve":
                wait(e, "ld_lw", 16 * (b + 1))
                wait(e, "pe_cond", b)
                e.tensor_copy(lw_h[:, :, :], lw_raw[:, :, :]).then_inc(ev("dv_lw"), 1)
                wait(e, f"ld_xr{b % 2}", 16 * (b // 2 + 1))
                e.tensor_copy(xT_h[:, :, cols], xr[b % 2][:, :, :]).then_inc(ev("dv_x"), 1)
            if who == ("pool" if b else "dve"):
                wait(e, "dv_lw", b + 1)
                wait(e, "pe_cond", b)
                e.tensor_tensor(lw_l[:, :, :], lw_raw[:, :, :], f32(lw_h[:, :, :]), ALU.subtract).then_inc(ev("lw_split"), 1)
                wait(e, "dv_x", b + 1)
                e.tensor_tensor(xT_l[:, :, cols], xr[b % 2][:, :, :], f32(xT_h[:, :, cols]), ALU.subtract).then_inc(ev("x_split"), 1)

        def st_cond(who, e, b, part):
            cols = slice(P * b, P * (b + 1))
            if who == "pe":
                wait(e, "lw_split", b + 1)
                wait(e, "x_split", b + 1)
                wait(e, "dv_x1", b - 2)
                if b == 2:
                    wait(e, "dv_leff", 4)
                last = split_mm(e, b0, [(xT_h[:, c, cols], xT_l[:, c, cols], lw_h[:, c, :], lw_l[:, c, :])
                                        for c in range(C)], part, 2)
                if part == 1:
                    last.then_inc(ev("pe_cond"), 1)
            if who == "act" and part == 1:
                wait(e, "pe_cond", b + 1)
                filled(e, ("h", b - 1))
                e.activation(h_sb[:, :], b0, ACT.Copy).then_inc(ev("ac_h"), 1)

        def st_hT(who, e, b):
            if who == "pe":
                wait(e, "ac_h", b + 1)
                if b == 0:
                    wait(e, "po_ident", 1)
                t = turn_claim(e, ("h", b))
                for c in range(C):
                    last = e.transpose(t[:, P * c:P * (c + 1)], h_sb[:, P * c:P * (c + 1)], ident[:, :])
                turn_ready(last, ("h", b))
            else:
                if who in ("act", "dve"):
                    wait(e, "pe_qkv", 2 * b)
                evac_split(who, e, ("h", b), flat(hT_h[:, :, :]), flat(hT_l[:, :, :]), "hT")

        def st_q1(who, e, b, part):
            q = b1.rearrange("p (h o d) -> p h o d", h=H1, o=1)
            if who == "pe":
                emptied(e, ("h", b))
                if b == 0:
                    wait(e, "dv_w1", 1)
                wait(e, "dv_qs", b)
                last = split_mm(e, b1, [(hT_h[:, c, :], hT_l[:, c, :], wa_h[:, c, 0:H1 * HD1],
                                         wa_l[:, c, 0:H1 * HD1]) for c in range(C)], part, 2)
                if part == 1:
                    last.then_inc(ev("pe_qkv"), 1)
            if who == "act" and part == 1:
                wait(e, "pe_qkv", 2 * b + 1)
                filled(e, ("tq", b - 1, 4))
                e.activation(qs[:, :, 0:2, :], q.broadcast_to([P, H1, 2, HD1]), ACT.Copy).then_inc(ev("ac_qs"), 1)
            if who == "dve" and part == 1:
                wait(e, "ac_qs", b + 1)
                e.tensor_tensor(qs[:, :, 2:4, :], q.broadcast_to([P, H1, 2, HD1]), f32(qs[:, :, 0:2, :]),
                                ALU.subtract).then_inc(ev("dv_qs"), 1)

        def st_kv1(who, e, b):
            k = b2[:, 0:KV1 * HD1].rearrange("p (h o d) -> p h o d", h=KV1, o=1)
            v = b2[:, KV1 * HD1:2 * KV1 * HD1].rearrange("p (h d) -> p h d", h=KV1)
            if who == "pe":
                wait(e, "dv_osum", 2 * (b - 1))
                split_mm(e, b2[:, 0:2 * KV1 * HD1],
                         [(hT_h[:, c, :], hT_l[:, c, :], wa_h[:, c, H1 * HD1:], wa_l[:, c, H1 * HD1:])
                          for c in range(C)]).then_inc(ev("pe_qkv"), 1)
            if who == "act":
                wait(e, "pe_qkv", 2 * b + 2)
                e.activation(ks[:, :, 0::2, :], k.broadcast_to([P, KV1, 2, HD1]), ACT.Copy).then_inc(ev("ac_ks"), 1)
                wait(e, "pe_pv1", 8 * (b - 1))
                e.activation(vs[b % 2][:, :, 0, :], v, ACT.Copy).then_inc(ev("ac_vs"), 1)
            if who == "dve":
                wait(e, "ac_vs", b + 1)
                wait(e, "ac_ks", b + 1)
                e.tensor_tensor(ks[:, :, 1::2, :], k.broadcast_to([P, KV1, 2, HD1]), f32(ks[:, :, 0::2, :]),
                                ALU.subtract).then_inc(ev("dv_ks"), 1)
                e.tensor_tensor(vs[b % 2][:, :, 1, :], v, f32(vs[b % 2][:, :, 0, :]), ALU.subtract).then_inc(ev("dv_vs"), 1)

        def st_tq(who, e, b, k):
            key = ("tq", b, k)
            src = flat(ks[:, :, :, :].rearrange("p h f d -> p h (f d)")) if k == 4 else \
                flat(qs[:, :, :, :].rearrange("p h f d -> p h (f d)"))[:, 512 * k:512 * (k + 1)]
            if who == "pe":
                if k == 0:
                    wait(e, "dv_qs", b + 1)
                if k == 4:
                    wait(e, "dv_ks", b + 1)
                if k == 1:
                    wait(e, "dv_vs", b + 1)
                t = turn_claim(e, key).bitcast(R32)
                for j in range(4):
                    last = e.transpose(t[:, P * j:P * (j + 1)], src[:, P * j:P * (j + 1)], ident_r[:, :])
                turn_ready(last, key)
            if who == ("act", "dve")[k % 2]:
                dst = kT[b % 2][:, :, :] if k == 4 else qT[b % 2][:, 4 * k:4 * (k + 1), :]
                t = turn_read(e, key)
                wait(e, "pe_s1", 8 * (b - 1))
                if b == 0:
                    wait(e, "dv_w1", 2)
                ins = e.activation(flat(dst), t, ACT.Copy) if who == "act" else e.tensor_copy(flat(dst), t)
                turn_done(ins, key)

        def st_scores1(who, e, b, s):
            n = 8 * b + s
            half, pr = s % 2, s // 2
            rows = slice(64 * half, 64 * (half + 1))
            sc = (b4, b5)[n % 2]
            if who == "pe":
                if s == 0:
                    for k in range(5):
                        emptied(e, ("tq", b, k))
                wait(e, "dv_s1", 4 * (n - 1))
                for r in range(R1):
                    last = e.matmul(sc[:, P * r:P * (r + 1)], qT[b % 2][rows, 4 * pr + r, :],
                                    kT[b % 2][rows, pr, :], start=True, stop=True)
                last.then_inc(ev("pe_s1"), 1)

        def st_max1(who, e, b, s):
            n = 8 * b + s
            sc = (b4, b5)[n % 2]
            if who == "dve":
                wait(e, "pe_s1", n + 1)
                filled(e, ("pt", n - 2))
                if n == 0:
                    wait(e, "po_causal", 1)
                wait(e, "ac_exp1", 4 * (n - 1))
                for r in range(R1):
                    e.tensor_tensor_reduce(out=p1[n % 2][:, r, :], in0=sc[:, P * r:P * (r + 1)], in1=causal[:, :],
                                           scale=-SCALE1, scalar=-LOWEST, op0=ALU.add, op1=ALU.min,
                                           accum_out=nm1[n % 2][:, r:r + 1]).then_inc(ev("dv_s1"), 1)

        def st_exp1(who, e, b, s):
            n = 8 * b + s
            if who == "act":
                wait(e, "dv_s1", 4 * (n + 1))
                wait(e, "dv_inv1", b - 1)
                for r in range(R1):
                    e.activation(p1[n % 2][:, r, :], p1[n % 2][:, r, :], ACT.Exp, bias=nm1[n % 2][:, r:r + 1],
                                 scale=-1.0, accum_out=sum1[b % 2][:, R1 * s + r:R1 * s + r + 1])\
                        .then_inc(ev("ac_exp1"), 1)

        def st_pt1(who, e, b, s):
            n = 8 * b + s
            key = ("pt", n)
            if who == "pe":
                wait(e, "ac_exp1", 4 * (n + 1))
                t = turn_claim(e, key)
                for r in range(R1):
                    last = e.transpose(t[:, P * r:P * (r + 1)], p1[n % 2][:, r, :], ident[:, :])
                turn_ready(last, key)

        def st_pt1_evac(who, e, b, s):
            n = 8 * b + s
            key = ("pt", n)
            if who in ("act", "dve"):
                wait(e, "pe_pv1", n - 1)
                evac_split(who, e, key, flat(pt_h[n % 2][:, :, :]), flat(pt_l[n % 2][:, :, :]), "pt1")

        def st_pv1(who, e, b, s):
            n = 8 * b + s
            if who == "pe":
                emptied(e, ("pt", n))
                if s == 0:
                    wait(e, "dv_vs", b + 1)
                if s == 0:
                    wait(e, "dv_osum", 2 * b - 1)
                if s == 4:
                    emptied(e, ("tq", b + 1, 3))
                for r in range(R1):
                    o = (b3, b2)[s // 4][:, 2 * HD1 * (R1 * (s % 4) + r):][:, 0:2 * HD1]
                    v = vs[b % 2][:, s, :, :].rearrange("p a d -> p (a d)")
                    e.matmul(o, pt_h[n % 2][:, r, :], v, start=True, stop=False)
                    last = e.matmul(o, pt_l[n % 2][:, r, :], v, start=False, stop=True)
                last.then_inc(ev("pe_pv1"), 1)

        def st_osum(who, e, b, half):
            if who == "dve":
                wait(e, "pe_pv1", 8 * b + 4 * (half + 1))
                if half == 0:
                    wait(e, "dv_onorm", b)
                e.tensor_reduce(osum[:, 16 * half:16 * (half + 1), :],
                                (b3, b2)[half].rearrange("p (h a d) -> p h d a", h=16, a=2), AX.X, ALU.add)\
                    .then_inc(ev("dv_osum"), 1)

        def st_onorm(who, e, b):
            if who == "dve":
                wait(e, "ac_exp1", 32 * (b + 1))
                e.reciprocal(inv1[:, :], sum1[b % 2][:, :]).then_inc(ev("dv_inv1"), 1)
                wait(e, "dv_inv1", b + 1)
                wait(e, "dv_osum", 2 * (b + 1))
                filled(e, ("o", b - 1))
                e.tensor_tensor(o_sb[:, :].rearrange("p (h d) -> p h d", h=H1), osum[:, :, :],
                                inv1[:, :].unsqueeze(2).broadcast_to([P, H1, HD1]), ALU.mult)\
                    .then_inc(ev("dv_onorm"), 1)

        def st_oT(who, e, b):
            key = ("o", b)
            if who == "pe":
                wait(e, "dv_onorm", b + 1)
                wait(e, "ac_h", min(b + 3, B))
                if b < 2:
                    wait(e, "dv_leff", 6 + 2 * b)
                t = turn_claim(e, key)
                for c in range(C):
                    last = e.transpose(t[:, P * c:P * (c + 1)], o_sb[:, P * c:P * (c + 1)], ident[:, :])
                turn_ready(last, key)
            else:
                if who in ("act", "dve"):
                    wait(e, "pe_wo1", b)
                evac_split(who, e, key, flat(oT_h[:, :, :]), flat(oT_l[:, :, :]), "oT")

        def st_wo1(who, e, b, part):
            if who == "pe":
                emptied(e, ("o", b))
                last = split_mm(e, b0, [(oT_h[:, c, :], oT_l[:, c, :], wo_h[:, c, :], wo_l[:, c, :])
                                        for c in range(C)], part, 2)
                if part == 1:
                    last.then_inc(ev("pe_wo1"), 1)
            if who == "dve" and part == 1:
                wait(e, "pe_wo1", b + 1)
                wait(e, f"ld_x{b % 2}", 16 * (b // 2 + 1))
                filled(e, ("x1", b - 2))
                wait(e, f"st_x1_{b % 2}", 16 * (b // 2))
                e.tensor_tensor(x1[b % 2][:, :], b0, x_in[b % 2][:, :], ALU.add).then_inc(ev("dv_x1"), 1)
            if who == "sp" and part == 1:
                wait(e, "dv_x1", b + 1)
                e.dma_start(x1_dram[b, :, :], x1[b % 2][:, :]).then_inc(ev(f"st_x1_{b % 2}"), 16)

        def st_x1T(who, e, b):
            key = ("x1", b)
            cols = slice(P * b, P * (b + 1))
            if who == "pe":
                wait(e, "dv_x1", b + 1)
                t = turn_claim(e, key)
                for c in range(C):
                    last = e.transpose(t[:, P * c:P * (c + 1)], x1[b % 2][:, P * c:P * (c + 1)], ident[:, :])
                turn_ready(last, key)
            elif who in ("act", "dve"):
                t = turn_read(e, key).rearrange("p (c t) -> p c t", c=C)
                if who == "act":
                    wait(e, "pe_cond", b + 1)
                    e.activation(xT_h[:, :, cols], t, ACT.Copy).then_inc(ev("ac_x1T"), 1)
                else:
                    wait(e, "ac_x1T", b + 1)
                    turn_done(e.tensor_tensor(xT_l[:, :, cols], t, f32(xT_h[:, :, cols]), ALU.subtract), key)

        def st_attention_done(who, e):
            if who in ("act", "dve", "pool"):
                wait(e, "pe_pv1", STEPS)
                wait(e, "ac_exp1", 4 * STEPS)
                wait(e, "dv_onorm", B)

        def st_phase2(who, e):
            for order in bank_uses.values():
                emptied(e, order[-1])
            wait(e, "st_x1_0", 16 * (B // 2))
            wait(e, "st_x1_1", 16 * (B // 2))

        def st_load2(who, e, i):
            if who == "sp":
                g, b = divmod(i, B)
                if i == 0:
                    wait(e, "ld_pages", 16)
                    wait(e, "st_tab", 64)
                    wait(e, "st_leff", 64)
                    wait(e, "pe_qkv", 2 * B)
                    st_load2.regs = [e.alloc_register(f"page{k}") for k in range(PAGES_ROW)]
                if i == 1:
                    st_phase2(who, e)
                wait(e, "dv_k_rope", 2 * (i - 1))
                e.dma_start(tabs[i % 2][:, :, :], tabs_dram[b, :, :].rearrange("p (t d) -> p t d", t=4))\
                    .then_inc(ev(f"ld_tabs{i % 2}"), 16)
                e.load(st_load2.regs, page_ids[0:1, PAGES_ROW * b:PAGES_ROW * (b + 1)])
                wait(e, "pe_tk", i - 1)
                wait(e, "po_vl", i - 1)
                for k in range(PAGES_ROW):
                    page = e.snap(st_load2.regs[k], min_val=0, max_val=PAGES - 1)
                    j, c = k % (P // PAGE), k // (P // PAGE)
                    e.dma_start(kv[i % 2][PAGE * j:PAGE * (j + 1), c, :],
                                I["kv_cache"][g, bass.ds(page, 1), :, :].rearrange("a p n -> (a p) n"))\
                        .then_inc(ev(f"ld_kv{i % 2}"), 16)

        def st_wload(who, e, g, c, kind):
            if who == "sp":
                if g == 0 and c == 0:
                    wait(e, "pe_qkv", 2 * B)
                wait(e, f"po_wg{kind}", C * g + c)
                e.dma_start((wst, wost)[kind][:, :], (I["w_qkv2"], I["w_o2"])[kind][g, :, c, :])\
                    .then_inc(ev(f"ld_wg{kind}"), 16)

        def st_wsplit(who, e, g, c, kind):
            n = C * g + c
            w = g % 2
            raw, hi, lo = ((wst, wg_h[w], wg_l[w]), (wost, wog_h[w], wog_l[w]))[kind]
            if who == "dve":
                wait(e, f"ld_wg{kind}", 16 * (n + 1))
                wait(e, "pe_wo2" if kind else "pe_kv", B * (g - 1))
                e.tensor_copy(hi[:, c, :], raw[:, :]).then_inc(ev(f"dv_wg{kind}"), 1)
            if who == "pool":
                wait(e, f"dv_wg{kind}", n + 1)
                wait(e, "pe_wo2" if kind else "pe_kv", B * (g - 1))
                e.tensor_tensor(lo[:, c, :], raw[:, :], f32(hi[:, c, :]), ALU.subtract).then_inc(ev(f"po_wg{kind}"), 1)

        def st_proj(who, e, i, part):
            g, b = divmod(i, B)
            w = g % 2
            cols = slice(P * b, P * (b + 1))
            if who == "pe":
                if i == 0:
                    wait(e, "dv_s1", 4 * STEPS)
                if part == 0:
                    wait(e, "po_wg0", C * (g + 1))
                    wait(e, "dv_q_rope", 2 * i)
                    wait(e, "ac_sq", 5 * i)
                    wait(e, "dv_ktn", i)
                if part < 2:
                    for c in range(2 * part, 2 * part + 2):
                        e.matmul(b4, xT_h[:, c, cols], wg_h[w][:, c, 0:QC], start=(c == 0), stop=False)
                        e.matmul(b4, xT_h[:, c, cols], wg_l[w][:, c, 0:QC], start=False, stop=False)
                        last = e.matmul(b4, xT_l[:, c, cols], wg_h[w][:, c, 0:QC], start=False, stop=(c == C - 1))
                    if part == 1:
                        last.then_inc(ev("pe_q"), 1)
                else:
                    wait(e, "dv_o", i - 1)
                    split_mm(e, b5[:, 0:2 * HD2],
                             [(xT_h[:, c, cols], xT_l[:, c, cols], wg_h[w][:, c, QC:], wg_l[w][:, c, QC:])
                              for c in range(C)]).then_inc(ev("pe_kv"), 1)

        def st_rope(who, e, i, part):
            q = b4.rearrange("p (h a d) -> p h a d", h=R2, a=2)
            k = b5[:, 0:HD2].rearrange("p (a d) -> p a d", a=2)
            t = tabs[i % 2]
            if who == "dve":
                tq = t[:, part, :].rearrange("p (o a d) -> p o a d", o=1, a=2).broadcast_to([P, R2, 2, HALF])
                tk = t[:, 2 + part, :].rearrange("p (a d) -> p a d", a=2)
                if part == 0:
                    wait(e, "ac_sq", 5 * i + 4)
                    wait(e, f"ld_tabs{i % 2}", 16 * (i // 2 + 1))
                    wait(e, "pe_tkn", i)
                    e.tensor_tensor(qk[:, 0:R2, :, :], q, tq, ALU.mult).then_inc(ev("dv_q_rope"), 1)
                    wait(e, "dv_vn", i + 1)
                    e.tensor_tensor(qk[:, R2, :, :], k, tk, ALU.mult).then_inc(ev("dv_k_rope"), 1)
                else:
                    wait(e, "po_rope", i)
                    e.tensor_tensor(qk_sin[:, 0:R2, :, :], q[:, :, ::-1, :], tq, ALU.mult).then_inc(ev("dv_q_rope"), 1)
                    e.tensor_tensor(qk_sin[:, R2, :, :], k[:, ::-1, :], tk, ALU.mult).then_inc(ev("dv_k_rope"), 1)
            if who == "pool" and part == 1:
                wait(e, "dv_q_rope", 2 * (i + 1))
                wait(e, "dv_k_rope", 2 * (i + 1))
                e.tensor_tensor(qk[:, :, :, :], qk[:, :, :, :], qk_sin[:, :, :, :], ALU.add).then_inc(ev("po_rope"), 1)

        def st_squares(who, e, i):
            if who == "act":
                wait(e, "dv_nr_x", i)
                wait(e, "pe_q", i + 1)
                for h in range(R2):
                    e.activation(sq_junk[:, h, :], b4[:, HD2 * h:HD2 * (h + 1)], ACT.Square,
                                 accum_out=ssq[:, h:h + 1]).then_inc(ev("ac_sq"), 1)
                wait(e, "pe_kv", i + 1)
                e.activation(sq_junk[:, R2, :], b5[:, 0:HD2], ACT.Square,
                             accum_out=ssq[:, R2:R2 + 1]).then_inc(ev("ac_sq"), 1)
                wait(e, "pe_pv", KC * (i - 1))
                e.activation(VN_h[i % 2][:, :], b5[:, HD2:2 * HD2], ACT.Copy).then_inc(ev("ac_vn"), 1)
            if who == "dve":
                wait(e, "ac_vn", i + 1)
                e.tensor_tensor(VN_l[i % 2][:, :], b5[:, HD2:2 * HD2], f32(VN_h[i % 2][:, :]), ALU.subtract)\
                    .then_inc(ev("dv_vn"), 1)

        def st_rstd(who, e, i):
            if who == "dve":
                link = lambda ins: after(e, ins, "dv_nr")
                wait(e, "ac_sq", 5 * (i + 1))
                wait(e, "po_rstd", 2 * i)
                e.tensor_scalar(out=nr_x[:, :], in0=ssq[:, :], scalar1=1.0 / HD2, scalar2=EPS,
                                op0=ALU.mult, op1=ALU.add).then_inc(ev("dv_nr_x"), 1)
                wait(e, "dv_nr_x", i + 1)
                link(e.tensor_scalar(out=nr_i[:, :], in0=nr_x[:, :].bitcast(I32), scalar1=1, scalar2=None,
                                     op0=ALU.logical_shift_right))
                wait(e, "dv_k_scale", i)
                e.tensor_scalar(out=rstd[:, :].bitcast(I32), in0=nr_i[:, :], scalar1=-1.0,
                                scalar2=float(RSQRT_MAGIC), op0=ALU.mult, op1=ALU.add).then_inc(ev("dv_guess"), 1)
                e.tensor_scalar(out=nr_x[:, :], in0=nr_x[:, :], scalar1=-0.5, scalar2=None, op0=ALU.mult)\
                    .then_inc(ev("dv_guess"), 1)
        def st_newton(who, e, i, steps):
            if who == "pool":
                link = lambda ins: after(e, ins, "po_nr")
                if 0 in steps:
                    wait(e, "dv_guess", 2 * (i + 1))
                for n in steps:
                    link(e.tensor_tensor(nr_t[:, :], rstd[:, :], rstd[:, :], ALU.mult))
                    link(e.tensor_tensor(nr_t[:, :], nr_t[:, :], nr_x[:, :], ALU.mult))
                    link(e.tensor_scalar(out=nr_t[:, :], in0=nr_t[:, :], scalar1=1.5, scalar2=None, op0=ALU.add))
                    step = e.tensor_tensor(rstd[:, :], nr_t[:, :], rstd[:, :], ALU.mult)
                    if n < 2:
                        link(step)
                if 2 in steps:
                    step.then_inc(ev("po_rstd"), 1)
                    wait(e, "po_rstd", 2 * i + 1)
                    wait(e, "dv_s2", 4 * (i - 1))
                    e.tensor_scalar(out=q_nscale[i % 2][:, :], in0=rstd[:, 0:R2], scalar1=-SCALE2, scalar2=None,
                                    op0=ALU.mult).then_inc(ev("po_rstd"), 1)

        def st_k_scale(who, e, i):
            if who == "dve":
                wait(e, "po_rstd", 2 * i + 1)
                wait(e, "po_rope", i + 1)
                e.tensor_scalar(out=qk[:, R2, :, :], in0=qk[:, R2, :, :], scalar1=rstd[:, R2:R2 + 1], scalar2=None,
                                op0=ALU.mult).then_inc(ev("dv_k_scale"), 1)

        def st_tk(who, e, i):
            if who == "pe":
                if i == 0:
                    wait(e, "dv_x1", B)
                wait(e, f"ld_kv{i % 2}", 16 * PAGES_ROW * (i // 2 + 1))
                wait(e, "dv_s2", 4 * i)
                for c in range(CACHED // P):
                    last = e.transpose(b0[:, P * c:P * (c + 1)], kv[i % 2][:, c, 0:HD2], ident[:, :])
                last.then_inc(ev("pe_tk"), 1)

        def st_tk_evac(who, e, i):
            if who == "act":
                wait(e, "pe_tk", i + 1)
                wait(e, "pe_s2", 4 * i)
                e.activation(KT_h[:, 0:CACHED], b0, ACT.Copy).then_inc(ev("ac_kt"), 1)
            if who == "dve":
                wait(e, "ac_kt", i + 1)
                e.tensor_tensor(KT_l[:, 0:CACHED], b0, f32(KT_h[:, 0:CACHED]), ALU.subtract).then_inc(ev("dv_kt"), 1)

        def st_tq2(who, e, i):
            if who == "pe":
                if i == 0:
                    emptied(e, ("x1", B - 2))
                wait(e, "dv_s2", 4 * i)
                wait(e, "po_rope", i + 1)
                for h in range(R2):
                    last = e.transpose(b1[:, P * h:P * (h + 1)], qk[:, h, :, :].rearrange("p a d -> p (a d)"),
                                       ident[:, :])
                last.then_inc(ev("pe_tq"), 1)

        def st_tq2_evac(who, e, i):
            if who == "act":
                wait(e, "pe_s2", 4 * i)
                wait(e, "pe_tq", i + 1)
                e.activation(QT_h[:, :], b1, ACT.Copy).then_inc(ev("ac_qt"), 1)
            if who == "dve":
                wait(e, "ac_qt", i + 1)
                e.tensor_tensor(QT_l[:, :], b1, f32(QT_h[:, :]), ALU.subtract).then_inc(ev("dv_qt"), 1)

        def st_tkn(who, e, i):
            if who == "pe":
                wait(e, "dv_q_rope", 2 * (i + 1))
                wait(e, "ac_sq", 5 * (i + 1))
                wait(e, "dv_k_scale", i + 1)
                e.transpose(b4[:, 0:P], qk[:, R2, :, :].rearrange("p a d -> p (a d)"), ident[:, :])\
                    .then_inc(ev("pe_tkn"), 1)

        def st_tkn_evac(who, e, i):
            if who == "act":
                wait(e, "pe_tkn", i + 1)
                wait(e, "pe_s2", 4 * i)
                e.activation(KT_h[:, CACHED:], b4[:, 0:P], ACT.Copy).then_inc(ev("ac_ktn"), 1)
            if who == "dve":
                wait(e, "ac_ktn", i + 1)
                e.tensor_tensor(KT_l[:, CACHED:], b4[:, 0:P], f32(KT_h[:, CACHED:]), ALU.subtract)\
                    .then_inc(ev("dv_ktn"), 1)

        def st_v(who, e, i):
            if who == "dve":
                wait(e, f"ld_kv{i % 2}", 16 * PAGES_ROW * (i // 2 + 1))
                wait(e, "pe_pv", KC * i - 1)
                e.tensor_copy(V_h[:, :, :], kv[i % 2][:, :, HD2:]).then_inc(ev("dv_vh"), 1)
            if who == "pool":
                wait(e, "dv_vh", i + 1)
                e.tensor_tensor(V_l[:, :, :], kv[i % 2][:, :, HD2:], f32(V_h[:, :, :]), ALU.subtract)\
                    .then_inc(ev("po_vl"), 1)

        def st_scores2(who, e, i, h):
            b = i % B
            n = 4 * i + h
            if who == "pe":
                if h == 0:
                    wait(e, "dv_qt", i + 1)
                    wait(e, "dv_kt", i + 1)
                if h == 1:
                    wait(e, "dv_acc", i - 1)
                    wait(e, "dv_pt", KC * i)
                if h >= 2:
                    wait(e, "dv_s2", n - 1)
                hc = slice(P * h, P * (h + 1))
                for s in range(2):
                    if h == 0 and s == 1:
                        wait(e, "dv_ktn", i + 1)
                    for m, (q, kt) in enumerate(((QT_h, KT_h), (QT_h, KT_l), (QT_l, KT_h))):
                        last = e.matmul(pair[h % 2][:, s, 0:KEYS // 2], q[:, hc],
                                        kt[:, KEYS // 2 * s:KEYS // 2 * (s + 1)], start=(m == 0), stop=(m == 2))
                last.then_inc(ev("pe_s2"), 1)
            if who == "dve":
                wait(e, "pe_s2", n + 1)
                if h == 0:
                    wait(e, "pe_pt", KC * i)
                    wait(e, "ac_exp2", 4 * i)
                    wait(e, "po_rstd", 2 * (i + 1))
                e.tensor_tensor_reduce(out=prob[:, h, :].rearrange("p (a k) -> p a k", a=2),
                                       in0=pair[h % 2][:, :, 0:KEYS // 2],
                                       in1=key_mask[:, b, :].rearrange("p (a k) -> p a k", a=2),
                                       scale=q_nscale[i % 2][:, h:h + 1], scalar=-LOWEST, op0=ALU.add, op1=ALU.min,
                                       accum_out=nm2[:, h:h + 1]).then_inc(ev("dv_s2"), 1)
            if who == "act":
                wait(e, "dv_s2", n + 1)
                if h == 0:
                    wait(e, "dv_inv2", 4 * i)
                e.activation(prob[:, h, :], prob[:, h, :], ACT.Exp, bias=nm2[:, h:h + 1],
                             scale=-1.0, accum_out=sum2[:, h:h + 1]).then_inc(ev("ac_exp2"), 1)

        def st_norm2(who, e, i, h):
            n = 4 * i + h
            if who == "dve":
                wait(e, "ac_exp2", n + 1)
                wait(e, "po_norm", n - 3)
                e.reciprocal(inv2[:, h:h + 1], sum2[:, h:h + 1]).then_inc(ev("dv_inv2"), 1)
            if who == "pool":
                wait(e, "dv_inv2", n + 1)
                e.tensor_tensor(prob[:, h, :], prob[:, h, :], inv2[:, h:h + 1].broadcast_to([P, KEYS]), ALU.mult)\
                    .then_inc(ev("po_norm"), 1)

        def st_pt(who, e, i, c):
            n = KC * i + c
            t = (b6, b7, b2)[n % 3]
            if who == "pe":
                wait(e, "po_norm", 4 * (i + 1))
                wait(e, "dv_s2", 4 * (i + 1))
                wait(e, "dv_pt", n - 2)
                for h in range(R2):
                    last = e.transpose(t[:, P * h:P * (h + 1)], prob[:, h, P * c:P * (c + 1)], ident[:, :])
                last.then_inc(ev("pe_pt"), 1)

        def st_pt_evac(who, e, i, c):
            n = KC * i + c
            t = (b6, b7, b2)[n % 3]
            if who == "act":
                wait(e, "pe_pt", n + 1)
                wait(e, "pe_pv", n - 2)
                e.activation(PT_h[n % 3][:, :], t, ACT.Copy).then_inc(ev("ac_pt"), 1)
            if who == "dve":
                wait(e, "ac_pt", n + 1)
                e.tensor_tensor(PT_l[n % 3][:, :], t, f32(PT_h[n % 3][:, :]), ALU.subtract).then_inc(ev("dv_pt"), 1)

        def st_pv(who, e, i, c):
            n = KC * i + c
            if who == "pe":
                if c == 0:
                    j = min(i + 2, GROUPS)
                    wait(e, "dv_k_rope", 2 * j)
                    wait(e, "dv_vn", j)
                    wait(e, "po_vl", i + 1)
                wait(e, "dv_pt", n + 1)
                k = n % 3
                vh, vl = (V_h[:, c, :], V_l[:, c, :]) if c < KC - 1 else (VN_h[i % 2][:, :], VN_l[i % 2][:, :])
                e.matmul(b5, vh, PT_h[k][:, :], start=(c == 0), stop=False)
                e.matmul(b5, vh, PT_l[k][:, :], start=False, stop=False)
                e.matmul(b5, vl, PT_h[k][:, :], start=False, stop=(c == KC - 1)).then_inc(ev("pe_pv"), 1)

        def st_o(who, e, i, part):
            if who == part == "act":
                wait(e, "pe_pv", KC * (i + 1))
                wait(e, "pe_wo2", i)
                e.activation(OT_h[:, :], b5, ACT.Copy).then_inc(ev("ac_o"), 1)
            if who == part == "dve":
                wait(e, "ac_o", i + 1)
                e.tensor_tensor(OT_l[:, :], b5, f32(OT_h[:, :]), ALU.subtract).then_inc(ev("dv_o"), 1)

        def st_wo2(who, e, i):
            g, b = divmod(i, B)
            if who == "pe":
                wait(e, "dv_o", i + 1)
                wait(e, "dv_s2", min(4 * (i + 2), 4 * GROUPS))
                if b == 0:
                    wait(e, "po_wg1", C * (g + 1))
                split_mm(e, b3, [(OT_h[:, P * h:P * (h + 1)], OT_l[:, P * h:P * (h + 1)],
                                  wog_h[g % 2][:, h, :], wog_l[g % 2][:, h, :]) for h in range(R2)])\
                    .then_inc(ev("pe_wo2"), 1)

        def st_acc(who, e, i):
            g, b = divmod(i, B)
            if who == "dve":
                wait(e, "pe_wo2", i + 1)
                if g == 0:
                    e.tensor_copy(acc2[:, b, :], b3).then_inc(ev("dv_acc"), 1)
                else:
                    wait(e, "dv_acc", i - B + 1)
                    e.tensor_tensor(acc2[:, b, :], b3, acc2[:, b, :], ALU.add).then_inc(ev("dv_acc"), 1)

        def st_ffn_load(who, e):
            if who == "sp":
                wait(e, "pe_kv", B * (KV2 - 1))
                wait(e, "pe_wo2", B * (KV2 - 1))
                wait(e, "po_wg0", C * KV2)
                wait(e, "po_wg1", C * KV2)
                wait(e, "st_leff", 64)
                for c in range(C):
                    for s in range(2):
                        e.dma_start(a_eff[64 * s:64 * (s + 1), :, c, 0:RANK],
                                    aeff_dram[2 * c + s, :, :].rearrange("b (p r) -> p b r", r=RANK)).then_inc(ev("ld_f"), 16)
                e.dma_start(a_sh[:, :, :], I["a_shared"]).then_inc(ev("ld_f"), 16)
            if who == "dve":
                wait(e, "ld_f", 16 * (1 + 2 * C))
                e.tensor_copy(a_eff[:, :, :, RANK:], a_sh[:, :, :].unsqueeze(1).broadcast_to([P, B, C, RANK]))\
                    .then_inc(ev("dv_ash"), 1)

        def st_ffn_kern(who, e, c):
            if who == "sp":
                wait(e, "po_kern", c)
                e.dma_start(kst[:, :], I["ffn_kernel"][:, c, :]).then_inc(ev("ld_kern"), 16)
            if who == "dve":
                wait(e, "ld_kern", 16 * (c + 1))
                e.tensor_copy(kern_h[:, c, :], kst[:, :]).then_inc(ev("dv_kern"), 1)
            if who == "pool":
                wait(e, "dv_kern", c + 1)
                e.tensor_tensor(kern_l[:, c, :], kst[:, :], f32(kern_h[:, c, :]), ALU.subtract).then_inc(ev("po_kern"), 1)

        def st_ffn_a(who, e, n):
            r = slice(2 * n, 2 * n + 2)
            if who == "dve":
                wait(e, "dv_ash", 1)
                e.tensor_copy(a_h[:, r, :, :], a_eff[:, r, :, :]).then_inc(ev("dv_ah"), 1)
            if who == "pool":
                wait(e, "dv_ah", n + 1)
                e.tensor_tensor(a_l[:, r, :, :], a_eff[:, r, :, :], f32(a_h[:, r, :, :]), ALU.subtract).then_inc(ev("po_al"), 1)

        def st_ffn_b(who, e):
            if who == "sp":
                wait(e, "pe_kv", GROUPS)
                wait(e, "st_leff", 64)
                for j in range(GJ):
                    rj = RANK // GJ
                    e.dma_start(b_eff[rj * j:rj * (j + 1), :, :],
                                beff_dram[j, :, :].rearrange("b (r o) -> r b o", o=D)).then_inc(ev("ld_b"), 16)
                for b in range(B):
                    e.dma_start(b_eff[RANK:2 * RANK, b, :], I["b_shared"]).then_inc(ev("ld_b"), 16)
                    e.dma_start(b_eff[2 * RANK:2 * RANK + 1, b, :], I["bias"]).then_inc(ev("ld_b"), 16)

        def st_ones(who, e):
            if who == "pool":
                wait(e, "pe_wo2", GROUPS)
                for k in range(2):
                    e.memset(axT[k][2 * RANK:2 * RANK + 1, :], 1.0).then_inc(ev("po_ones"), 1)

        def st_ffn_T(who, e, b):
            k = b % 2
            t = (b0, b1)[k]
            if who == "sp":
                if b == 0:
                    wait(e, "dv_k_rope", 2 * GROUPS)
                wait(e, "dv_y", b - 1)
                e.dma_start(x1_in[k][:, :], x1_dram[b, :, :]).then_inc(ev(f"ld_x1_{k}"), 16)
            if who == "pe":
                if b == 0:
                    wait(e, "dv_s2", 4 * GROUPS - 1)
                wait(e, "dv_acc", B * (KV2 - 1) + b + 1)
                wait(e, "dv_fT", b - 1)
                for c in range(C):
                    last = e.transpose(t[:, P * c:P * (c + 1)], acc2[:, b, P * c:P * (c + 1)], ident[:, :])
                last.then_inc(ev("pe_fT"), 1)
            if who == "act":
                wait(e, "pe_fT", b + 1)
                if b == 0:
                    wait(e, "pe_kv", GROUPS)
                    wait(e, "dv_k_rope", 2 * GROUPS)
                wait(e, "pe_ff", b - 1)
                e.activation(flat(oT3_h[k][:, :, :]), t, ACT.Copy).then_inc(ev("ac_fT"), 1)
            if who == "dve":
                wait(e, "ac_fT", b + 1)
                e.tensor_tensor(flat(oT3_l[k][:, :, :]), t, f32(flat(oT3_h[k][:, :, :])), ALU.subtract).then_inc(ev("dv_fT"), 1)

        def st_ffn_ax(who, e, b):
            k = b % 2
            if who == "pe":
                if b == 0:
                    wait(e, "po_al", B // 2)
                    wait(e, "dv_ah", B // 2)
                if b == 1:
                    wait(e, "dv_o", GROUPS)
                wait(e, "dv_fT", b + 1)
                wait(e, "ac_ax", b - 1)
                split_mm(e, (b4, b5)[k][:, 0:2 * RANK],
                         [(oT3_h[k][:, c, :], oT3_l[k][:, c, :], a_h[:, b, c, :], a_l[:, b, c, :]) for c in range(C)])\
                    .then_inc(ev("pe_ax"), 1)
            if who == "act":
                wait(e, "pe_ax", b + 1)
                wait(e, "pe_axT", b)
                e.activation(ax[:, :], (b4, b5)[k][:, 0:2 * RANK], ACT.Copy).then_inc(ev("ac_ax"), 1)

        def st_ffn_mm(who, e, b):
            k = b % 2
            if who == "pe":
                if b == 0:
                    wait(e, "po_kern", C)
                    wait(e, "dv_pt", KC * GROUPS)
                if b == 1:
                    wait(e, "dv_acc", GROUPS)
                wait(e, "dv_y", b - 1)
                o = (b2, b3)[k]
                for c in range(C):
                    e.matmul(o, oT3_h[k][:, c, :], kern_h[:, c, :], start=(c == 0), stop=False)
                    e.matmul(o, oT3_h[k][:, c, :], kern_l[:, c, :], start=False, stop=False)
                    last = e.matmul(o, oT3_l[k][:, c, :], kern_h[:, c, :], start=False, stop=False)
                last.then_inc(ev("pe_ff"), 1)

        def st_ffn_axT(who, e, b):
            k = b % 2
            t = (b6, b7)[k][0:2 * RANK, 0:P]
            if who == "pe":
                wait(e, "ac_ax", b + 1)
                wait(e, "ac_axT", b - 1)
                e.transpose(t, ax[:, :], ident[:, :]).then_inc(ev("pe_axT"), 1)
            if who == "act":
                wait(e, "pe_axT", b + 1)
                wait(e, "pe_out", b - 1)
                if b == 0:
                    wait(e, "pe_wo2", GROUPS)
                e.activation(axT[k][0:2 * RANK, :], t, ACT.Copy).then_inc(ev("ac_axT"), 1)

        def st_ffn_out(who, e, b):
            k = b % 2
            if who == "pe":
                if b == 0:
                    wait(e, "ld_b", 16 * (GJ + 2 * B))
                    wait(e, "po_ones", 2)
                wait(e, "ac_axT", b + 1)
                e.matmul((b2, b3)[k], axT[k][:, :], b_eff[:, b, :], start=False, stop=True).then_inc(ev("pe_out"), 1)
            if who == "dve":
                wait(e, "pe_out", b + 1)
                wait(e, f"ld_x1_{k}", 16 * (b // 2 + 1))
                wait(e, f"st_y{k}", 16 * (b // 2))
                e.tensor_tensor(y[k][:, :], (b2, b3)[k], x1_in[k][:, :], ALU.add).then_inc(ev("dv_y"), 1)
            if who == "sp":
                wait(e, "dv_y", b + 1)
                e.dma_start(out[b, :, :], y[k][:, :]).then_inc(ev(f"st_y{k}"), 16)

        def st_end(who, e):
            if who == "sp":
                for k in range(2):
                    wait(e, f"st_y{k}", 16 * (B // 2))

        plan = []
        ALL = ("sp", "pool", "dve", "act", "pe")

        def add(f, *a, on=ALL):
            plan.append((f, a, on))

        add(st_load1, 0)
        add(st_constants)
        add(st_weights1, 0, on=("sp",))
        add(st_weights1, 1, on=("sp",))
        add(st_split1, 0)
        add(st_load1, 1)
        add(st_weights1, 0, on=("dve",))
        add(st_cond, 0, 0)
        add(st_cond, 0, 1)
        add(st_hT, 0)
        add(st_weights1, 1, on=("dve",))
        add(st_q1, 0, 0)
        add(st_q1, 0, 1)
        add(st_kv1, 0)
        add(st_split1, 1)
        for k in range(5):
            add(st_tq, 0, k)
        add(st_load1, 2)
        add(st_lora_load, 0)
        add(st_scores1, 0, 0)
        add(st_max1, 0, 0)
        add(st_cond, 1, 0, on=("pe",))
        add(st_cond, 1, 1, on=("pe",))

        PE, EVAC = ("pe",), ("act", "dve", "sp")
        parts = {
            0: [(st_hT, 1)],
            1: [(st_q1, 1, 0)],
            2: [(st_q1, 1, 1)],
            3: [(st_oT, -1), (st_kv1, 1)],
            4: [(st_wo1, -1, 0), (st_tq, 1, 0), (st_tq, 1, 1)],
            5: [(st_wo1, -1, 1), (st_tq, 1, 2), (st_tq, 1, 3)],
            6: [(st_cond, 2, 0), (st_x1T, -1)],
            7: [(st_cond, 2, 1)],
        }
        lora_ticks = (1, 2, 4, 5, 9, 10, 17, 18)
        for n in range(STEPS + 9):
            b, s = divmod(n, 8)

            def step(f, k):
                if 0 <= k < STEPS:
                    add(f, *divmod(k, 8))

            def row(f, k, *a, on=ALL):
                if 0 <= k < B:
                    add(f, k, *a, on=on)

            step(st_pt1, n - 1)
            step(st_scores1, n + 1)
            for f, r, *a in parts[(n - 1) % 8]:
                row(f, (n - 1) // 8 + r, *a, on=EVAC)
            if n - 1 in lora_ticks:
                add(st_lora_eff, lora_ticks.index(n - 1), 0, on=("dve",))
            step(st_exp1, n)
            step(st_max1, n + 1)
            if s == 2:
                row(st_osum, b - 1, 1)
                row(st_onorm, b - 1)
            if s == 6:
                row(st_osum, b, 0)
                row(st_tq, b + 1, 4, on=PE)
            step(st_pt1_evac, n - 1)
            step(st_pv1, n - 2)
            if s == 6:
                row(st_tq, b + 1, 4, on=EVAC)
            for f, r, *a in parts[s]:
                row(f, b + r, *a, on=PE)
            if s == 1:
                row(st_split1, b + 2)
                row(st_loadx, b)
            if s == 2:
                row(st_load1, b + 3)
            k = n - (8 * (B - 2) + 4)
            if 0 <= k - 2 < 2 * C:
                add(st_wsplit, 0, (k - 2) // 2, k % 2)
            if 0 <= k < 2 * C:
                add(st_wload, 0, k // 2, k % 2)
            if b == B - 1:
                if s == 7:
                    add(st_load2, 0)
            if n in lora_ticks:
                add(st_lora_eff, lora_ticks.index(n), b + 2, on=PE)
            if n in (3, 6, 11, 19):
                which = (3, 6, 11, 19).index(n)
                add(st_lora_store, which)
                if which < 3:
                    add(st_lora_load, which + 1)
            if n == STEPS + 1:
                add(st_proj, 0, 0)
                add(st_proj, 0, 1)
            if n == STEPS + 3:
                add(st_proj, 0, 2)
            if n == STEPS + 4:
                add(st_attention_done)
                add(st_squares, 0)
                add(st_rstd, 0)
                add(st_newton, 0, (0,))
                add(st_rope, 0, 0)
                add(st_rope, 0, 1)
                add(st_newton, 0, (1, 2))
            if n == STEPS + 5:
                add(st_tq2, 0)
                add(st_tq2_evac, 0)
            if n == STEPS + 6:
                add(st_tk, 0)
                add(st_tk_evac, 0)
                add(st_k_scale, 0)
                add(st_tkn, 0)
                add(st_tkn_evac, 0)
            if n == 1:
                add(st_masks)
            if n == 3:
                add(st_angles)
            if n in (6, 9, 12, 15):
                add(st_table, n // 3 - 2)
        add(st_phase2)
        split_in = {i: [] for i in range(GROUPS)}
        for g in range(1, KV2):
            for c in range(C):
                split_in[B * (g - 1) + 1 + c].append((g, c, 0))
                split_in[B * (g - 1) + C + 1 + c].append((g, c, 1))
        add(st_load2, 1)
        add(st_v, 0)
        for i in range(GROUPS):
            g, b = divmod(i, B)
            nxt, prev = i + 1 < GROUPS, i > 0

            def if_next(f, *a):
                if nxt:
                    add(f, i + 1, *a)

            if i + 2 < GROUPS:
                add(st_load2, i + 2)
            add(st_scores2, i, 0)
            add(st_scores2, i, 1)
            if prev:
                add(st_pv, i - 1, KC - 1)
                add(st_o, i - 1, "act")
            add(st_norm2, i, 0)
            add(st_scores2, i, 2)
            add(st_norm2, i, 1)
            add(st_scores2, i, 3)
            add(st_norm2, i, 2)
            if prev:
                add(st_o, i - 1, "dve")
            add(st_norm2, i, 3)
            if not nxt:
                add(st_wo2, i - 1)
                add(st_ffn_T, 0)
            for part in range(3):
                if_next(st_proj, part)
            if_next(st_squares)
            if_next(st_rstd)
            if_next(st_newton, (0,))
            if_next(st_rope, 0)
            if_next(st_rope, 1)
            if_next(st_newton, (1, 2))
            if_next(st_tk)
            add(st_pt, i, 0)
            add(st_pt, i, 1)
            add(st_pt_evac, i, 0)
            add(st_pt_evac, i, 1)
            if_next(st_tk_evac)
            if prev and nxt:
                add(st_wo2, i - 1)
            add(st_pt, i, 2)
            for n, piece in enumerate(split_in[i]):
                add(st_wsplit, *piece)
            if nxt:
                for piece in split_in[i + 1]:
                    add(st_wload, *piece)
            n = i - (GROUPS - 6)
            if n == -1:
                add(st_ffn_load, on=("sp",))
            if n == 0:
                add(st_ffn_load, on=("dve",))
            if 0 <= n + 1 < C:
                add(st_ffn_kern, n + 1, on=("sp",))
            if 0 <= n < C:
                add(st_ffn_kern, n, on=("dve", "pool"))
                add(st_ffn_a, n)
            if n == C:
                add(st_ffn_b)
            add(st_pv, i, 0)
            if_next(st_tq2)
            add(st_pt_evac, i, 2)
            if_next(st_tq2_evac)
            if_next(st_k_scale)
            add(st_pt, i, 3)
            add(st_pt_evac, i, 3)
            add(st_pv, i, 1)
            add(st_pt, i, 4)
            add(st_pt_evac, i, 4)
            add(st_pv, i, 2)
            if_next(st_tkn)
            if_next(st_tkn_evac)
            if prev:
                add(st_acc, i - 1)
            add(st_pv, i, 3)
            if_next(st_v)
        add(st_pv, GROUPS - 1, KC - 1)
        add(st_o, GROUPS - 1, "act")
        add(st_o, GROUPS - 1, "dve")
        add(st_ones)
        add(st_ffn_T, 1)
        add(st_ffn_ax, 0)
        add(st_ffn_mm, 0)
        add(st_wo2, GROUPS - 1)
        add(st_acc, GROUPS - 1)
        for b in range(1, B):
            if b + 1 < B:
                add(st_ffn_T, b + 1)
            add(st_ffn_ax, b)
            add(st_ffn_axT, b - 1)
            add(st_ffn_mm, b)
            add(st_ffn_out, b - 1)
        add(st_ffn_axT, B - 1)
        add(st_ffn_out, B - 1)
        add(st_end)

        for f, a, on in plan:
            if f is st_hT:
                turn(("h", a[0]))
            elif f is st_tq:
                turn(("tq",) + a)
            elif f is st_pt1:
                turn(("pt", 8 * a[0] + a[1]))
            elif f is st_oT:
                turn(("o", a[0]))
            elif f is st_x1T:
                turn(("x1", a[0]))

        def run(who, e):
            for f, a, on in plan:
                if who in on:
                    f(who, e, *a)

        block = ctx.enter_context(nc.Block())

        @block.sync
        def _(e):
            run("sp", e)

        @block.gpsimd
        def _(e):
            run("pool", e)

        @block.vector
        def _(e):
            run("dve", e)

        @block.scalar
        def _(e):
            run("act", e)

        @block.tensor
        def _(e):
            run("pe", e)


def kernel(**inputs):
    import numpy as np
    import concourse.bacc as bacc
    from concourse import mybir
    from concourse.bass_utils import run_bass_kernel_spmd

    a = {k: np.asarray(v) for k, v in inputs.items()}
    con = np.ascontiguousarray

    def chunks(w):
        return con(w.reshape(-1, P, w.shape[-1]).transpose(1, 0, 2))

    wq1 = a["L0_attn_wq"].reshape(D, KV1 // 2, 2, R1, HD1).transpose(0, 1, 3, 2, 4).reshape(D, H1 * HD1)
    w_q = a["L0_cond2_Wq"].reshape(KV2, QC, D)
    w_k = a["L0_cond2_Wk"].reshape(KV2, HD2, D)
    w_v = a["L0_cond2_Wv"].reshape(KV2, HD2, D)
    w_qkv2 = np.concatenate([w_q, w_k, w_v], axis=1)
    w_qkv2 = w_qkv2.transpose(0, 2, 1).reshape(KV2, C, P, WC).transpose(0, 2, 1, 3)
    w_o2 = a["L0_cond2_Wo"].reshape(D, KV2, R2, HD2).transpose(1, 3, 2, 0)
    kv_cache = np.concatenate([a["L0_cond2_k_cache"], a["L0_cond2_v_cache"]], axis=-1)
    arrays = {
        "x": a["x"],
        "x_t": chunks(a["x"].reshape(B * P, D).T),
        "lora_ids": a["itok_B_3_7"].reshape(1, B),
        "page_ids": a["itok_Bx16_0_63"].reshape(1, B * PAGES_ROW),
        "lens": a["itok_B_207_1644"].reshape(B),
        "lora_w": a["L0_cond_weight"].transpose(0, 2, 1).reshape(8, C, P, D).transpose(0, 2, 1, 3),
        "w_qkv1": chunks(np.concatenate([wq1, a["L0_attn_wk"], a["L0_attn_wv"]], axis=1)),
        "w_o1": chunks(a["L0_attn_wo"]),
        "w_qkv2": w_qkv2,
        "w_o2": w_o2,
        "q_norm_w": a["L0_cond2_q_norm_w"],
        "k_norm_w": a["L0_cond2_k_norm_w"],
        "kv_cache": kv_cache.transpose(2, 0, 1, 3),
        "gate_t": a["L0_ffn_gate"].T,
        "lora_a": a["L0_ffn_lora_A"].transpose(0, 2, 1).reshape(N_LORA, GJ, LFLAT).transpose(1, 0, 2).reshape(P, LFLAT),
        "lora_b": a["L0_ffn_lora_B"].transpose(0, 2, 1).reshape(N_LORA, GJ, LFLAT).transpose(1, 0, 2).reshape(P, LFLAT),
        "a_shared": chunks(a["L0_ffn_lora_A_shared"].T),
        "b_shared": a["L0_ffn_lora_B_shared"].T,
        "bias": a["L0_ffn_bias"].reshape(1, D),
        "ffn_kernel": chunks(a["L0_ffn_kernel"]),
        "inv_freq": (np.float32(1.0) / np.power(np.float32(10000.0), np.arange(0, HD2, 2, dtype=np.float32) / np.float32(HD2))),
    }
    arrays = {k: con(v) for k, v in arrays.items()}
    nc = bacc.Bacc("TRN2", target_bir_lowering=False, num_devices=1)
    I = {k: nc.dram_tensor(f"in_{k}", v.shape, mybir.dt.from_np(v.dtype), kind="ExternalInput").ap()
         for k, v in arrays.items()}
    out = nc.dram_tensor("out_y", (B, P, D), mybir.dt.float32, kind="ExternalOutput").ap()
    build_program(nc, I, out)
    r = run_bass_kernel_spmd(nc, [{f"in_{k}": v for k, v in arrays.items()}], core_ids=[0])
    return r.results[0]["out_y"]
```
